# Optimizing a Trainium2 kernel written in Bass

```python
import numpy as np
import jax
import jax.numpy as jnp

def _softmax(x, axis=-1):
    return jax.nn.softmax(x, axis=axis)

def _gelu(x):
    return jax.nn.gelu(x, approximate=True)

def _silu(x):
    return jax.nn.silu(x)

def _sigmoid(x):
    return jax.nn.sigmoid(x)

def _layernorm(x, axis=-1, eps=1e-05):
    m = jnp.mean(x, axis=axis, keepdims=True)
    v = jnp.var(x, axis=axis, keepdims=True)
    return (x - m) / jnp.sqrt(v + eps)

def _scatter_add(tgt, idx, src, axis=0):
    return tgt.at[idx].add(src)

def _segment_sum(src, seg, n):
    return jax.ops.segment_sum(src, seg, n)
kernel_name = 'mk_hybrid_d1_jaxref_r8_93badb'

def setup_inputs(seed: int=0):
    np.random.seed(seed)
    _w = jnp.asarray

    def _L0_attn_a_setup():
        import jax, jax.numpy as jnp
        import numpy as np
        B, T, D = (2, 256, 128)
        H, W = (16, 32)
        HD = D // H
        key = jax.random.key(seed)
        ks = jax.random.split(key, 5)
        s = 0.02
        return {'x': jax.random.normal(ks[0], (B, T, D), dtype=jnp.float32), 'Wqkv': jax.random.normal(ks[1], (3 * D, D), dtype=jnp.float32) * s, 'bqkv': jax.random.normal(ks[2], (3 * D,), dtype=jnp.float32) * s, 'Wo': jax.random.normal(ks[3], (D, D), dtype=jnp.float32) * s, 'bo': jax.random.normal(ks[4], (D,), dtype=jnp.float32) * s}
    _L0_attn_a_in = _L0_attn_a_setup()

    def _L0_attn_b_setup():
        import jax, jax.numpy as jnp
        import numpy as np
        B, L, D_MODEL = (2, 128, 128)
        N_LAYERS = 2
        D_INNER = 2 * D_MODEL
        D_STATE = 16
        D_CONV = 4
        DT_RANK = (D_MODEL + 15) // 16
        INIT_SCALE = 0.02

        def _silu(x):
            return x * jax.nn.sigmoid(x)

        def _causal_conv1d(u, w, b):
            ut = jnp.pad(jnp.transpose(u, (0, 2, 1)), ((0, 0), (0, 0), (D_CONV - 1, 0)))
            y = jax.lax.conv_general_dilated(ut, w[:, None, :], window_strides=(1,), padding='VALID', feature_group_count=D_INNER, dimension_numbers=('NCH', 'OIH', 'NCH'))
            return jnp.transpose(y + b[None, :, None], (0, 2, 1))

        def _selective_scan(u, dt, A, Bm, Cm, Dvec):
            dA = jnp.exp(dt[..., None] * A)
            dBu = dt[..., None] * Bm[:, :, None, :] * u[..., None]

            def step(h, xs):
                dA_t, dBu_t, C_t = xs
                h = dA_t * h + dBu_t
                y = jnp.einsum('bdn,bn->bd', h, C_t)
                return (h, y)
            h0 = jnp.zeros((u.shape[0], D_INNER, D_STATE), u.dtype)
            _, ys = jax.lax.scan(step, h0, (jnp.swapaxes(dA, 0, 1), jnp.swapaxes(dBu, 0, 1), jnp.swapaxes(Cm, 0, 1)))
            return jnp.swapaxes(ys, 0, 1) + u * Dvec

        def _mamba_layer(x, W_in, conv_w, conv_b, W_x, W_dt, b_dt, A_log, Dvec, W_out):
            xz = jnp.einsum('bld,ed->ble', x, W_in)
            u, z = jnp.split(xz, 2, axis=-1)
            u = _silu(_causal_conv1d(u, conv_w, conv_b))
            x_dbl = jnp.einsum('bld,rd->blr', u, W_x)
            dt, Bm, Cm = jnp.split(x_dbl, [DT_RANK, DT_RANK + D_STATE], axis=-1)
            dt = jax.nn.softplus(jnp.einsum('blr,dr->bld', dt, W_dt) + b_dt)
            A = -jnp.exp(A_log)
            y = _selective_scan(u, dt, A, Bm, Cm, Dvec)
            y = y * _silu(z)
            return jnp.einsum('bld,od->blo', y, W_out)
        key = jax.random.key(seed)
        ks = jax.random.split(key, 8)
        f32 = jnp.float32
        dt_init = float(np.log(np.expm1(0.01)))
        return {'x': jax.random.normal(ks[0], (B, L, D_MODEL), f32), 'W_in': jax.random.normal(ks[1], (N_LAYERS, 2 * D_INNER, D_MODEL), f32) * INIT_SCALE, 'conv_w': jax.random.normal(ks[2], (N_LAYERS, D_INNER, D_CONV), f32) * INIT_SCALE, 'conv_b': jnp.zeros((N_LAYERS, D_INNER), f32), 'W_x': jax.random.normal(ks[3], (N_LAYERS, DT_RANK + 2 * D_STATE, D_INNER), f32) * INIT_SCALE, 'W_dt': jax.random.normal(ks[4], (N_LAYERS, D_INNER, DT_RANK), f32) * INIT_SCALE, 'b_dt': jnp.full((N_LAYERS, D_INNER), dt_init, f32), 'A_log': jnp.tile(jnp.log(jnp.arange(1, D_STATE + 1, dtype=f32)), (N_LAYERS, D_INNER, 1)), 'D': jnp.ones((N_LAYERS, D_INNER), f32), 'W_out': jax.random.normal(ks[5], (N_LAYERS, D_MODEL, D_INNER), f32) * INIT_SCALE}
    _L0_attn_b_in = _L0_attn_b_setup()

    def _L0_ffn_setup():
        import jax, jax.numpy as jnp
        import numpy as np
        B, S, D = (4, 256, 128)
        E = 8
        TOPK = 2
        I = 938

        def _swiglu(x, gate_up, down):
            h = jnp.einsum('bsd,fd->bsf', x, gate_up)
            g, u = jnp.split(h, 2, axis=-1)
            return jnp.einsum('bsi,di->bsd', jax.nn.silu(g) * u, down)
        key = jax.random.key(seed)
        ks = jax.random.split(key, 6)
        scale = 1.0 / np.sqrt(D)
        return {'hidden_states': jax.random.normal(ks[0], (B, S, D), dtype=jnp.float32), 'gate_weight': jax.random.normal(ks[1], (E, D), dtype=jnp.float32) * scale, 'shared_gate_up': jax.random.normal(ks[2], (2 * I, D), dtype=jnp.float32) * scale, 'shared_down': jax.random.normal(ks[3], (D, I), dtype=jnp.float32) * (1.0 / np.sqrt(I)), 'experts_gate_up': jax.random.normal(ks[4], (E, 2 * I, D), dtype=jnp.float32) * scale, 'experts_down': jax.random.normal(ks[5], (E, D, I), dtype=jnp.float32) * (1.0 / np.sqrt(I))}
    _L0_ffn_in = _L0_ffn_setup()
    _d = {'L0_attn_a_x': _L0_attn_a_in['x'], 'L0_attn_a_Wqkv': _L0_attn_a_in['Wqkv'], 'L0_attn_a_bqkv': _L0_attn_a_in['bqkv'], 'L0_attn_a_Wo': _L0_attn_a_in['Wo'], 'L0_attn_a_bo': _L0_attn_a_in['bo'], 'L0_attn_b_W_in': _L0_attn_b_in['W_in'], 'L0_attn_b_conv_w': _L0_attn_b_in['conv_w'], 'L0_attn_b_conv_b': _L0_attn_b_in['conv_b'], 'L0_attn_b_W_x': _L0_attn_b_in['W_x'], 'L0_attn_b_W_dt': _L0_attn_b_in['W_dt'], 'L0_attn_b_b_dt': _L0_attn_b_in['b_dt'], 'L0_attn_b_A_log': _L0_attn_b_in['A_log'], 'L0_attn_b_D': _L0_attn_b_in['D'], 'L0_attn_b_W_out': _L0_attn_b_in['W_out'], 'L0_ffn_gate_weight': _L0_ffn_in['gate_weight'], 'L0_ffn_shared_gate_up': _L0_ffn_in['shared_gate_up'], 'L0_ffn_shared_down': _L0_ffn_in['shared_down'], 'L0_ffn_experts_gate_up': _L0_ffn_in['experts_gate_up'], 'L0_ffn_experts_down': _L0_ffn_in['experts_down']}
    _x0 = _d['L0_attn_a_x']
    _d['L0_attn_a_x'] = jax.random.normal(jax.random.fold_in(jax.random.key(seed), 1), (4, 1024, 128), dtype=_x0.dtype)
    del _x0
    return _d

def reference(L0_attn_a_x, L0_attn_a_Wqkv, L0_attn_a_bqkv, L0_attn_a_Wo, L0_attn_a_bo, L0_attn_b_W_in, L0_attn_b_conv_w, L0_attn_b_conv_b, L0_attn_b_W_x, L0_attn_b_W_dt, L0_attn_b_b_dt, L0_attn_b_A_log, L0_attn_b_D, L0_attn_b_W_out, L0_ffn_gate_weight, L0_ffn_shared_gate_up, L0_ffn_shared_down, L0_ffn_experts_gate_up, L0_ffn_experts_down):

    def _L0_attn_a_ref(x, Wqkv, bqkv, Wo, bo):
        import jax, jax.numpy as jnp
        import numpy as np
        B, T, D = (2, 256, 128)
        H, W = (16, 32)
        HD = D // H
        b, t, d = x.shape
        qkv = x @ Wqkv.T + bqkv
        qkv = qkv.reshape(b, t, 3, H, HD)
        q = jnp.transpose(qkv[:, :, 0], (0, 2, 1, 3))
        k = jnp.transpose(qkv[:, :, 1], (0, 2, 1, 3))
        v = jnp.transpose(qkv[:, :, 2], (0, 2, 1, 3))
        scores = jnp.einsum('bhid,bhjd->bhij', q, k) / jnp.sqrt(jnp.float32(HD))
        i = jnp.arange(t)[:, None]
        j = jnp.arange(t)[None, :]
        mask = (j <= i) & (j >= i - (W - 1))
        scores = jnp.where(mask, scores, -jnp.inf)
        probs = jax.nn.softmax(scores, axis=-1)
        y = jnp.einsum('bhij,bhjd->bhid', probs, v)
        y = jnp.transpose(y, (0, 2, 1, 3)).reshape(b, t, d)
        return y @ Wo.T + bo

    def _L0_attn_b_ref(x, W_in, conv_w, conv_b, W_x, W_dt, b_dt, A_log, D, W_out):
        import jax, jax.numpy as jnp
        import numpy as np
        B, L, D_MODEL = (2, 128, 128)
        N_LAYERS = 2
        D_INNER = 2 * D_MODEL
        D_STATE = 16
        D_CONV = 4
        DT_RANK = (D_MODEL + 15) // 16
        INIT_SCALE = 0.02

        def _silu(x):
            return x * jax.nn.sigmoid(x)

        def _causal_conv1d(u, w, b):
            ut = jnp.pad(jnp.transpose(u, (0, 2, 1)), ((0, 0), (0, 0), (D_CONV - 1, 0)))
            y = jax.lax.conv_general_dilated(ut, w[:, None, :], window_strides=(1,), padding='VALID', feature_group_count=D_INNER, dimension_numbers=('NCH', 'OIH', 'NCH'))
            return jnp.transpose(y + b[None, :, None], (0, 2, 1))

        def _selective_scan(u, dt, A, Bm, Cm, Dvec):
            dA = jnp.exp(dt[..., None] * A)
            dBu = dt[..., None] * Bm[:, :, None, :] * u[..., None]

            def step(h, xs):
                dA_t, dBu_t, C_t = xs
                h = dA_t * h + dBu_t
                y = jnp.einsum('bdn,bn->bd', h, C_t)
                return (h, y)
            h0 = jnp.zeros((u.shape[0], D_INNER, D_STATE), u.dtype)
            _, ys = jax.lax.scan(step, h0, (jnp.swapaxes(dA, 0, 1), jnp.swapaxes(dBu, 0, 1), jnp.swapaxes(Cm, 0, 1)))
            return jnp.swapaxes(ys, 0, 1) + u * Dvec

        def _mamba_layer(x, W_in, conv_w, conv_b, W_x, W_dt, b_dt, A_log, Dvec, W_out):
            xz = jnp.einsum('bld,ed->ble', x, W_in)
            u, z = jnp.split(xz, 2, axis=-1)
            u = _silu(_causal_conv1d(u, conv_w, conv_b))
            x_dbl = jnp.einsum('bld,rd->blr', u, W_x)
            dt, Bm, Cm = jnp.split(x_dbl, [DT_RANK, DT_RANK + D_STATE], axis=-1)
            dt = jax.nn.softplus(jnp.einsum('blr,dr->bld', dt, W_dt) + b_dt)
            A = -jnp.exp(A_log)
            y = _selective_scan(u, dt, A, Bm, Cm, Dvec)
            y = y * _silu(z)
            return jnp.einsum('bld,od->blo', y, W_out)
        residual = x
        h = x
        for i in range(N_LAYERS):
            h = _mamba_layer(h, W_in[i], conv_w[i], conv_b[i], W_x[i], W_dt[i], b_dt[i], A_log[i], D[i], W_out[i])
        return h + residual

    def _L0_ffn_ref(hidden_states, gate_weight, shared_gate_up, shared_down, experts_gate_up, experts_down):
        import jax, jax.numpy as jnp
        import numpy as np
        B, S, D = (4, 256, 128)
        E = 8
        TOPK = 2
        I = 938

        def _swiglu(x, gate_up, down):
            h = jnp.einsum('bsd,fd->bsf', x, gate_up)
            g, u = jnp.split(h, 2, axis=-1)
            return jnp.einsum('bsi,di->bsd', jax.nn.silu(g) * u, down)
        x = hidden_states
        out = _swiglu(x, shared_gate_up, shared_down)
        logits = jnp.einsum('bsd,ed->bse', x, gate_weight)
        probs = jax.nn.softmax(logits.astype(jnp.float32), axis=-1)
        top_p, sel = jax.lax.top_k(probs, TOPK)
        top_p = top_p / (jnp.sum(top_p, axis=-1, keepdims=True) + 1e-08)
        cw = jnp.sum(top_p[..., None] * jax.nn.one_hot(sel, E, dtype=top_p.dtype), axis=2)
        for e in range(E):
            y = _swiglu(x, experts_gate_up[e], experts_down[e])
            out = out + cw[..., e:e + 1] * y
        return out
    x = L0_attn_a_x
    x = x + _L0_attn_a_ref(_layernorm(x, axis=-1), L0_attn_a_Wqkv, L0_attn_a_bqkv, L0_attn_a_Wo, L0_attn_a_bo)
    x = x + _L0_ffn_ref(_layernorm(x, axis=-1), L0_ffn_gate_weight, L0_ffn_shared_gate_up, L0_ffn_shared_down, L0_ffn_experts_gate_up, L0_ffn_experts_down)
    x = x + _L0_attn_b_ref(_layernorm(x, axis=-1), L0_attn_b_W_in, L0_attn_b_conv_w, L0_attn_b_conv_b, L0_attn_b_W_x, L0_attn_b_W_dt, L0_attn_b_b_dt, L0_attn_b_A_log, L0_attn_b_D, L0_attn_b_W_out)
    x = x + _L0_ffn_ref(_layernorm(x, axis=-1), L0_ffn_gate_weight, L0_ffn_shared_gate_up, L0_ffn_shared_down, L0_ffn_experts_gate_up, L0_ffn_experts_down)
    return x

_drawn_inputs = setup_inputs


def setup_inputs(seed=0):
    import zlib

    import numpy as np

    out = dict(_drawn_inputs(seed))
    spreads = {'L0_attn_b_conv_b': (0.0, 0.1),
     'L0_attn_b_b_dt': (-4.600165843963623, 0.2),
     'L0_attn_b_D': (1.0, 0.2)}
    factors = {}
    for name, (base, spread) in spreads.items():
        noise = np.random.default_rng([zlib.crc32(name.encode()), seed]).standard_normal(out[name].shape)
        drawn = base * np.exp(spread * noise) if base else spread * noise
        out[name] = jnp.asarray(drawn.astype(out[name].dtype))
    for name, factor in factors.items():
        out[name] = (out[name] * factor).astype(out[name].dtype)
    return out
```

```python
from contextlib import ExitStack

import concourse.bass as bass
from concourse import mybir
import numpy as np

F32 = mybir.dt.float32
BF16 = mybir.dt.bfloat16
I32 = mybir.dt.int32
U32 = mybir.dt.uint32
ALU = mybir.AluOpType
ACT = mybir.ActivationFunctionType
AX = mybir.AxisListType
ds = bass.ds

P = 128
B, T, D = 4, 1024, 128
NT = B * T // P
TPB = T // P
EPS = 1e-5

H, HD, WIN = 16, 8, 32
HG = P // 32
NG = H // HG
NW = P // 32
KW = 64
MASKED = -1e30

E, I = 8, 938
GU = 2 * I
IA = 512
IB = I - IA
CA, CB = IA // P, -(-IB // P)
ITAIL = IB - (CB - 1) * P
NC = CA + CB
LODGERS = 2
SLOTS = 2 * NT + E
ROW = D + 1

NL, DI, NS, TAPS, RANK = 2, 256, 16, 4, 8
HALF = DI // P
XR = 2 * NS + RANK
SEG = 512


def wait(eng, sem, value):
    if isinstance(value, int) and value <= 0:
        return
    eng.wait_ge(sem, value)


def hybrid_block_kernel(nc, a, out, phases):
    ctx = ExitStack()
    with ctx:
        def sb(name, shape, dt=F32, scope=ctx):
            return scope.enter_context(nc.sbuf_tensor(name, shape, dt))

        def sem(name, scope=ctx):
            return scope.enter_context(nc.semaphore(name))

        X = sb("X", [P, NT * D])
        ident = sb("ident", [P, P])
        gate_up = sb("gate_up", [P, (E + 1) * GU])
        down = sb("down", [P, (E + 1) * NC * D])
        gateT = sb("gateT", [P, E])
        mean = sb("mean", [P, NT])
        rstd = sb("rstd", [P, NT])
        row_stats = sb("row_stats", [P, NT, 6])
        apart = sb("apart", [P, NT])

        ones_tile = sb("ones_tile", [P, NT])
        all_ones = sb("all_ones", [P, P])
        before = sb("before", [P, P])
        earlier = sb("earlier", [P, E * E])
        tile_number = sb("tile_number", [P, SLOTS])
        tile_start = sb("tile_start", [P, SLOTS])
        token_row = sb("token_row", [P, 2 * NT], I32)
        nobody = sb("nobody", [P, ROW], I32)

        routed = [nc.dram_tensor(f"routed_{n}", (SLOTS * P, ROW), F32, kind="Internal").ap() for n in range(2)]
        expert_out = [nc.dram_tensor(f"expert_out_{n}", (2 * B * T + P, D), F32, kind="Internal").ap() for n in range(2)]

        x_in = sem("x_in")
        small_in = sem("small_in")
        experts_in = sem("experts_in")
        prefilled = sem("prefilled")

        def load_x(sp):
            x_d = a["x"].rearrange("(t p) d -> p t d", p=P)
            x_s = X[:].rearrange("p (t d) -> p t d", d=D)
            for n in range(4):
                sp.dma_start(x_s[:, n * 8:(n + 1) * 8, :], x_d[:, n * 8:(n + 1) * 8, :]).then_inc(x_in, 16)

        def load_expert(sp, n, done):
            sp.dma_start(gate_up[:, n * GU:(n + 1) * GU], a["gate_up"][:, n * GU:(n + 1) * GU]).then_inc(done, 16)
            body = down[:, n * NC * D:(n + 1) * NC * D]
            sp.dma_start(body[:, 0:(NC - 1) * D], a["down"][:, n * (NC - 1) * D:(n + 1) * (NC - 1) * D]).then_inc(done, 16)
            sp.dma_start(body[0:ITAIL, (NC - 1) * D:NC * D], a["down_tail"][:, n * D:(n + 1) * D]).then_inc(done, 16)

        def load_experts(sp):
            sp.dma_start(gateT[:], a["gateT"]).then_inc(experts_in, 16)
            for dst, name in shapes:
                sp.dma_start(dst[:], a[name]).then_inc(experts_in, 16)
            for n in range(E, -1, -1):
                load_expert(sp, n, experts_in)

        lodgers_in = sem("lodgers_in")
        shapes = [(ones_tile, "ones_tile"), (all_ones, "all_ones"), (before, "before"), (earlier, "earlier"),
                  (tile_number, "tile_number"), (tile_start, "tile_start"), (token_row, "token_row")]
        EXPERTS_IN = 16 * (1 + len(shapes) + 3 * (E + 1))
        s_nobody = sem("s_nobody")

        def prefill(sp):
            sp.dma_start(nobody[:], a["nobody"]).then_inc(s_nobody, 16)
            sp.wait_ge(s_nobody, 16)
            for dst in routed:
                sp.dma_start(dst.rearrange("(t p) r -> p t r", p=P), nobody[:].bitcast(F32).unsqueeze(1).to_broadcast([P, SLOTS, ROW])).then_inc(prefilled, 16)

        def stats_dve(dve, s_stats, s_var, s_std, s_rstd):
            with dve.Fori(0, NT) as t:
                dve.bn_stats(row_stats[:, ds(t, 1), :], X[:, ds(t * D, D)]).then_inc(s_stats, 1)
            dve.wait_ge(s_stats, NT)
            dve.tensor_tensor(mean[:], row_stats[:, :, 1], row_stats[:, :, 4], ALU.add)
            dve.tensor_tensor(apart[:], row_stats[:, :, 1], row_stats[:, :, 4], ALU.subtract)
            dve.tensor_tensor(rstd[:], row_stats[:, :, 2], row_stats[:, :, 5], ALU.add).then_inc(s_stats, 1)
            dve.wait_ge(s_stats, NT + 1)
            dve.tensor_scalar(mean[:], mean[:], 0.5, None, ALU.mult)
            dve.tensor_scalar(rstd[:], rstd[:], 1.0 / D, EPS, ALU.mult, ALU.add)
            dve.scalar_tensor_tensor(apart[:], apart[:], 0.25, apart[:], ALU.mult, ALU.mult).then_inc(s_stats, 1)
            dve.wait_ge(s_stats, NT + 2)
            dve.tensor_tensor(rstd[:], rstd[:], apart[:], ALU.add).then_inc(s_var, 1)
            dve.wait_ge(s_std, 1)
            dve.reciprocal(rstd[:], rstd[:]).then_inc(s_rstd, 1)
            dve.wait_ge(s_rstd, 1)

        def stats_act(act, s_var, s_std):
            act.wait_ge(s_var, 1)
            act.activation(rstd[:], rstd[:], ACT.Sqrt).then_inc(s_std, 1)

        def layernorm(dve, dst, t):
            return dve.tensor_scalar(dst, X[:, ds(t * D, D)], mean[:, ds(t, 1)], rstd[:, ds(t, 1)], ALU.subtract, ALU.mult)

        def attention():
            scope = ExitStack()
            with scope:
                def tb(name, shape, dt=F32):
                    return sb(name, shape, dt, scope)

                def ts(name):
                    return sem("at_" + name, scope)

                wqkvT = tb("wqkvT", [P, 3 * D])
                woT = tb("woT", [P, D])
                bqkv = tb("bqkv", [P, 3])
                bq = tb("bq", [P, 1])
                bo = tb("bo", [1, D])
                ones = tb("ones", [1, P])
                own_head = tb("own_head", [P, HG, 32])
                mask = tb("mask", [P, 2, NW * KW])
                xn = tb("xn", [P, 2, D])
                xnT = tb("xnT", [P, B, 32 + P])
                qT = tb("qT", [P, 2, P])
                kT = tb("kT", [P, B, 32 + P])
                q_spread = tb("q_spread", [P, 2, NW, HG, 32])
                v = tb("v", [P, B, 2, D])
                sc = tb("sc", [P, NG, NW, KW])
                probs = tb("probs", [P, 2, NG, NW, KW])
                top = tb("top", [P, 16])
                total = tb("total", [P, 16])
                inv = tb("inv", [P, 16])
                probsT = tb("probsT", [P, 2, NG * P])
                own = tb("own", [P, 2, 2, HG, 32])
                ysum = tb("ysum", [P, P])
                yT = tb("yT", [P, P])

                score_ps = scope.enter_context(nc.psum_tensor("score_ps", [P, NG, SEG], F32))
                turn_ps = scope.enter_context(nc.psum_tensor("turn_ps", [P, NG, P], F32))
                pv_ps = scope.enter_context(nc.psum_tensor("pv_ps", [P, 2, SEG], F32))
                qkv_ps = scope.enter_context(nc.psum_tensor("qkv_ps", [P, SEG], F32))

                s_stats, s_var, s_std, s_rstd = ts("stats"), ts("var"), ts("std"), ts("rstd")
                s_zero, s_bq = ts("zeroed"), ts("bq")
                s_ln, s_x_turned, s_xnT, s_hist = ts("ln"), ts("x_turned"), ts("xnT"), ts("hist")
                s_qkv, s_qk, s_kh, s_v, s_spread = ts("qkv"), ts("qk_copied"), ts("k_hist"), ts("v_copied"), ts("spread")
                s_score, s_mask, s_top, s_sub, s_exp = ts("score"), ts("masked"), ts("top"), ts("sub"), ts("exp")
                s_total, s_inv, s_probs = ts("total"), ts("inv"), ts("probs")
                s_turn, s_turned, s_pv = ts("turn"), ts("turned"), ts("pv")
                s_own, s_ysum, s_yT, s_wo, s_x = ts("own"), ts("ysum"), ts("yT"), ts("wo"), ts("x")

                small = [(ident[:], "ident"), (wqkvT[:], "wqkvT"), (woT[:], "woT"), (bqkv[:], "bqkv"), (bo[:], "bo"),
                         (own_head[:].rearrange("p h q -> p (h q)"), "own_head"),
                         (mask[:].rearrange("p f k -> p (f k)"), "mask"), (ones[:], "ones_row")]
                SMALL = 16 * len(small)

                def at(n, r):
                    return n * B + r

                def tile(n, r):
                    n, r = n + r // B, r % B
                    return r * TPB + n, r

                def run(eng_fori, body):
                    for r in range(-3, B):
                        body(0, r, False)
                    with eng_fori(1, TPB - 1) as n:
                        for r in range(B):
                            body(n, r, False)
                    for r in range(B + 1):
                        body(TPB - 1, r, True)

                def alive(n, r, last):
                    if isinstance(n, int):
                        return 0 <= n * B + r < NT
                    return True

                with nc.Block() as block:
                    @block.sync
                    def _(sp):
                        load_x(sp)
                        for dst, name in small:
                            sp.dma_start(dst, a[name]).then_inc(small_in, 16)
                        load_experts(sp)
                        prefill(sp)

                    @block.gpsimd
                    def _(pool):
                        pool.wait_ge(small_in, SMALL)
                        def body(n, r, last):
                            if alive(n, r + 1, last):
                                t = at(n, r + 1)
                                pool.wait_ge(s_top, t + 1)
                                pool.tensor_tensor(sc[:].rearrange("p g w k -> p (g w) k"), sc[:].rearrange("p g w k -> p (g w) k"),
                                                   top[:, :].unsqueeze(2).to_broadcast([P, 16, KW]), ALU.subtract).then_inc(s_sub, 1)
                            if alive(n, r + 2, last):
                                t = at(n, r + 2)
                                s = r % 2
                                pool.wait_ge(s_qk, t + 1)
                                wait(pool, s_score, t - 1)
                                pool.tensor_tensor(q_spread[:, s], qT[:, s, :].rearrange("p (w q) -> p w q", w=NW).unsqueeze(2).to_broadcast([P, NW, HG, 32]),
                                                   own_head[:].unsqueeze(1).to_broadcast([P, NW, HG, 32]), ALU.mult).then_inc(s_spread, 1)
                            if alive(n, r + 1, last):
                                t = at(n, r + 1)
                                s = (r + 1) % 2
                                pool.wait_ge(s_inv, t + 1)
                                pr = probs[:, s].rearrange("p g w k -> p (g w) k")
                                pool.tensor_tensor(pr, pr, inv[:, :].unsqueeze(2).to_broadcast([P, 16, KW]), ALU.mult).then_inc(s_probs, 1)
                        run(pool.Fori, body)

                    @block.scalar
                    def _(act):
                        act.wait_ge(small_in, SMALL)
                        act.mul(bq[:], bqkv[:, 0:1], HD ** -0.5).then_inc(s_bq, 1)
                        stats_act(act, s_var, s_std)
                        act.wait_ge(s_bq, 1)
                        act.wait_ge(s_zero, 1)
                        def body(n, r, last):
                            if alive(n, r + 2, last):
                                t = at(n, r + 2)
                                b = (r + 2) % B
                                act.wait_ge(s_x_turned, t + 1)
                                if not (isinstance(t, int) and t < B):
                                    act.activation(xnT[:, b, 0:32], xnT[:, b, P:P + 32], ACT.Copy).then_inc(s_hist, 1)
                                    act.wait_ge(s_hist, t + 1 - B)
                                act.activation(xnT[:, b, 32:32 + P], qkv_ps[:, 0:P], ACT.Copy).then_inc(s_xnT, 1)
                            if alive(n, r, last):
                                t = at(n, r)
                                act.wait_ge(s_turn, 2 * t + 1)
                                wait(act, s_pv, t)
                                act.activation(probsT[:, 0, :], turn_ps[:].rearrange("p g q -> p (g q)"), ACT.Copy).then_inc(s_turned, 1)
                            if alive(n, r + 2, last):
                                t = at(n, r + 2)
                                b = (r + 2) % B
                                s = r % 2
                                act.wait_ge(s_qkv, t + 1)
                                wait(act, s_spread, t - 1)
                                act.activation(qT[:, s, :], qkv_ps[:, 0:P], ACT.Identity, bias=bq[:], scale=HD ** -0.5)
                                wait(act, s_score, t - B + 1)
                                if not (isinstance(t, int) and t < B):
                                    act.activation(kT[:, b, 0:32], kT[:, b, P:P + 32], ACT.Copy).then_inc(s_kh, 1)
                                    act.wait_ge(s_kh, t + 1 - B)
                                act.activation(kT[:, b, 32:32 + P], qkv_ps[:, P:2 * P], ACT.Identity, bias=bqkv[:, 1:2])
                                wait(act, s_pv, t - B + 1)
                                act.activation(v[:, b].rearrange("p a d -> p (a d)"), qkv_ps[:, 2 * P:4 * P], ACT.Copy).then_inc(s_qk, 1)
                            if alive(n, r, last):
                                t = at(n, r)
                                act.wait_ge(s_turn, 2 * t + 2)
                                act.activation(probsT[:, 1, :], turn_ps[:].rearrange("p g q -> p (g q)"), ACT.Copy).then_inc(s_turned, 1)
                            if alive(n, r + 1, last):
                                t = at(n, r + 1)
                                s = (r + 1) % 2
                                act.wait_ge(s_sub, t + 1)
                                wait(act, s_turn, 2 * (t - 1))
                                act.activation(probs[:, s].rearrange("p g w k -> p (g w k)"), sc[:].rearrange("p g w k -> p (g w k)"), ACT.Exp).then_inc(s_exp, 1)
                        run(act.Fori, body)

                    @block.vector
                    def _(dve):
                        dve.memset(xnT[:], 0.0)
                        dve.memset(kT[:], 0.0).then_inc(s_zero, 1)
                        dve.wait_ge(x_in, 64)
                        stats_dve(dve, s_stats, s_var, s_std, s_rstd)
                        dve.wait_ge(small_in, SMALL)
                        def body(n, r, last):
                            if alive(n, r - 1, last):
                                t = at(n, r - 1)
                                dve.wait_ge(s_pv, t + 1)
                                dve.tensor_tensor(own[:].rearrange("p a b h q -> p a b (h q)"),
                                                  pv_ps[:, :, 0:2 * P].rearrange("p a (b c) -> p a b c", b=2),
                                                  own_head[:].rearrange("p h q -> p (h q)").unsqueeze(1).unsqueeze(1).to_broadcast([P, 2, 2, P]),
                                                  ALU.mult).then_inc(s_own, 1)
                            if alive(n, r + 1, last):
                                t = at(n, r + 1)
                                first = isinstance(t, int) and t < B
                                dve.wait_ge(s_score, t + 1)
                                wait(dve, s_exp, t)
                                dve.tensor_tensor(sc[:].rearrange("p g w k -> p g (w k)"), score_ps[:, :, 0:NW * KW],
                                                  mask[:, int(first), :].unsqueeze(1).to_broadcast([P, NG, NW * KW]), ALU.add).then_inc(s_mask, 1)
                            if alive(n, r - 1, last):
                                t = at(n, r - 1)
                                dve.wait_ge(s_own, t + 1)
                                dve.tensor_reduce(ysum[:].rearrange("p (b a q) -> p a b q", b=2, a=2), own[:].rearrange("p a b h q -> p a b q h"),
                                                  AX.X, ALU.add).then_inc(s_ysum, 1)
                            if alive(n, r + 1, last):
                                t = at(n, r + 1)
                                dve.wait_ge(s_mask, t + 1)
                                wait(dve, s_sub, t)
                                dve.tensor_reduce(top[:], sc[:].rearrange("p g w k -> p (g w) k"), AX.X, ALU.max).then_inc(s_top, 1)
                            if alive(n, r - 1, last):
                                t = at(n, r - 1)
                                dve.wait_ge(s_ysum, t + 1)
                                wait(dve, s_wo, t)
                                dve.tensor_scalar(yT[:], ysum[:], bqkv[:, 2:3], None, ALU.add).then_inc(s_yT, 1)
                            if alive(n, r + 3, last):
                                t = at(n, r + 3)
                                wait(dve, s_x_turned, t - 1)
                                layernorm(dve, xn[:, (r + 3) % 2, :], tile(n, r + 3)[0]).then_inc(s_ln, 1)
                            if alive(n, r - 1, last):
                                t = at(n, r - 1)
                                j = tile(n, r - 1)[0]
                                dve.wait_ge(s_wo, t + 1)
                                dve.tensor_tensor(X[:, ds(j * D, D)], X[:, ds(j * D, D)], qkv_ps[:, 0:D], ALU.add).then_inc(s_x, 1)
                            if alive(n, r + 1, last):
                                t = at(n, r + 1)
                                s = (r + 1) % 2
                                dve.wait_ge(s_exp, t + 1)
                                dve.tensor_reduce(total[:], probs[:, s].rearrange("p g w k -> p (g w) k"), AX.X, ALU.add).then_inc(s_total, 1)
                                dve.wait_ge(s_total, t + 1)
                                wait(dve, s_probs, t)
                                dve.reciprocal(inv[:], total[:]).then_inc(s_inv, 1)
                        run(dve.Fori, body)

                    @block.tensor
                    def _(pe):
                        pe.wait_ge(small_in, SMALL)

                        def products(t, s, r, p):
                            for g in range(NG):
                                for w in range(2):
                                    mm = pe.matmul(pv_ps[32 * g:32 * g + 32, w, p * P:(p + 1) * P], v[64 * w:64 * w + 64, r % B, p, 32 * g:32 * g + 32],
                                                   probsT[64 * w:64 * w + 64, p, g * P:(g + 1) * P], start=True, stop=True)
                            return mm

                        def body(n, r, last):
                            if alive(n, r + 1, last):
                                t = at(n, r + 1)
                                s, b = (r + 1) % 2, (r + 1) % B
                                pe.wait_ge(s_spread, t + 1)
                                wait(pe, s_mask, t)
                                for w in range(NW):
                                    for g in range(NG):
                                        mm = pe.matmul(score_ps[:, g, w * KW:(w + 1) * KW], q_spread[32 * g:32 * g + 32, s, w].rearrange("p h q -> p (h q)"),
                                                       kT[32 * g:32 * g + 32, b, 32 * w:32 * w + KW], start=True, stop=True)
                                mm.then_inc(s_score, 1)
                            if alive(n, r + 2, last):
                                t = at(n, r + 2)
                                pe.wait_ge(s_ln, t + 1)
                                wait(pe, s_x, t - 3)
                                wait(pe, s_qk, t)
                                pe.transpose(qkv_ps[:, 0:P], xn[:, r % 2, :], ident[:]).then_inc(s_x_turned, 1)
                            if alive(n, r, last):
                                t = at(n, r)
                                s = r % 2
                                pe.wait_ge(s_probs, t + 1)
                                wait(pe, s_turned, 2 * t)
                                for g in range(NG):
                                    mm = pe.transpose(turn_ps[:, g, :], probs[:, s, g, 0:2, :].rearrange("p w k -> p (w k)"), ident[:])
                                mm.then_inc(s_turn, 1)
                            if alive(n, r + 2, last):
                                t = at(n, r + 2)
                                b = (r + 2) % B
                                pe.wait_ge(s_xnT, t + 1)
                                pe.matmul(qkv_ps[:, 0:P], wqkvT[:, 0:D], xnT[:, b, 32:32 + P], start=True, stop=True)
                                pe.matmul(qkv_ps[:, P:2 * P], wqkvT[:, D:2 * D], xnT[:, b, 32:32 + P], start=True, stop=True)
                                for p in range(2):
                                    for w in range(2):
                                        c = 32 * (2 * p + w)
                                        mm = pe.matmul(qkv_ps[64 * w:64 * w + 64, (2 + p) * P:(3 + p) * P], xnT[:, b, c:c + KW], wqkvT[:, 2 * D:3 * D], start=True, stop=True)
                                mm.then_inc(s_qkv, 1)
                            if alive(n, r, last):
                                t = at(n, r)
                                s = r % 2
                                wait(pe, s_own, t)
                                pe.wait_ge(s_turned, 2 * t + 1)
                                for g in range(NG):
                                    mm = pe.transpose(turn_ps[:, g, :], probs[:, s, g, 2:4, :].rearrange("p w k -> p (w k)"), ident[:])
                                mm.then_inc(s_turn, 1)
                                products(t, s, r, 0)
                            if alive(n, r - 1, last):
                                t = at(n, r - 1)
                                pe.wait_ge(s_yT, t + 1)
                                wait(pe, s_x, t)
                                if alive(n, r + 2, last):
                                    pe.wait_ge(s_qk, at(n, r + 2) + 1)
                                if alive(n, r, last):
                                    pe.wait_ge(s_turned, 2 * at(n, r) + 2)
                                pe.matmul(qkv_ps[:, 0:D], yT[:], woT[:], start=True, stop=False)
                                pe.matmul(qkv_ps[:, 0:D], ones[:], bo[:], start=False, stop=True).then_inc(s_wo, 1)
                            if alive(n, r, last):
                                t = at(n, r)
                                if isinstance(t, int) and t == 0:
                                    pe.wait_ge(s_turned, 2)
                                products(t, r % 2, r, 1).then_inc(s_pv, 1)
                        run(pe.Fori, body)

        def ffn(n):
            scope = ExitStack()
            with scope:
                def tb(name, shape, dt=F32):
                    return sb(f"f{n}_" + name, shape, dt, scope)

                def ts(name):
                    return sem(f"f{n}_" + name, scope)

                def pb(name, shape):
                    return inner.enter_context(nc.psum_tensor(f"f{n}_" + name, shape, F32))

                rows = tb("rows", [P, NT * D])
                cols = tb("cols", [P, NT * P])
                logits = tb("logits", [P, NT, E])
                G0, G1 = rows, cols

                inner = ExitStack()
                with inner:
                    xn = sb(f"f{n}_xn", [P, 2, D], F32, inner)
                    xT = sb(f"f{n}_xTr", [P, 2, P], F32, inner)
                    turn_ps = pb("rturn_ps", [P, 2, SEG])
                    s_stats, s_var, s_std, s_rstd = ts("stats"), ts("var"), ts("std"), ts("rstd")
                    s_ln, s_turn, s_xT, s_rows, s_cols, s_logit, s_logit_out = (ts(x) for x in ("ln", "rturn", "rxT", "rows", "cols", "logit", "logit_out"))

                    def by_two(fori, body):
                        body(0, 0), body(1, 1)
                        with fori(1, NT // 2) as m:
                            body(m * 2, 0), body(m * 2 + 1, 1)
                        body(NT, 0)

                    with nc.Block() as block:
                        @block.vector
                        def _(dve):
                            stats_dve(dve, s_stats, s_var, s_std, s_rstd)
                            def body(t, s):
                                if isinstance(t, int) and t == NT:
                                    return
                                wait(dve, s_turn, t - 1)
                                wait(dve, s_rows, t - 1)
                                layernorm(dve, xn[:, s, :], t).then_inc(s_ln, 1)
                            by_two(dve.Fori, body)

                        @block.tensor
                        def _(pe):
                            pe.wait_ge(experts_in, EXPERTS_IN)
                            def body(t, s):
                                if not (isinstance(t, int) and t == NT):
                                    wait(pe, s_logit_out, t - 1)
                                    pe.wait_ge(s_ln, t + 1)
                                    pe.transpose(turn_ps[:, s, 0:P], xn[:, s, :], ident[:]).then_inc(s_turn, 1)
                                if not (isinstance(t, int) and t == 0):
                                    pe.wait_ge(s_xT, t)
                                    pe.matmul(turn_ps[:, 1 - s, P:P + E], xT[:, 1 - s, :], gateT[:], start=True, stop=True).then_inc(s_logit, 1)
                            by_two(pe.Fori, body)

                        @block.scalar
                        def _(act):
                            stats_act(act, s_var, s_std)
                            def body(t, s):
                                if not (isinstance(t, int) and t == NT):
                                    wait(act, s_logit, t - 1)
                                    wait(act, s_cols, t - 1)
                                    act.wait_ge(s_turn, t + 1)
                                    act.activation(xT[:, s, :], turn_ps[:, s, 0:P], ACT.Copy).then_inc(s_xT, 1)
                                if not (isinstance(t, int) and t == 0):
                                    act.wait_ge(s_logit, t)
                                    act.activation(logits[:, ds(t - 1, 1), :], turn_ps[:, 1 - s, P:P + E], ACT.Copy).then_inc(s_logit_out, 1)
                            by_two(act.Fori, body)

                        @block.sync
                        def _(sp):
                            if n and "mamba" in phases:
                                for e in range(E - LODGERS, E):
                                    load_expert(sp, e, lodgers_in)

                        @block.gpsimd
                        def _(pool):
                            def body(t, s):
                                if isinstance(t, int) and t == NT:
                                    return
                                pool.wait_ge(s_ln, t + 1)
                                pool.tensor_copy(rows[:, ds(t * D, D)], xn[:, s, :]).then_inc(s_rows, 1)
                                pool.wait_ge(s_xT, t + 1)
                                pool.tensor_copy(cols[:, ds(t * P, P)], xT[:, s, :]).then_inc(s_cols, 1)
                            by_two(pool.Fori, body)

                inner = ExitStack()
                with inner:
                    def tb(name, shape, dt=F32):
                        return sb(f"f{n}_" + name, shape, dt, inner)

                    probs = tb("probs", [P, NT, E])
                    red = tb("red", [P, NT])
                    above = tb("above", [P, NT, E * E])
                    equal = tb("equal", [P, NT, E * E])
                    rank = tb("rank", [P, NT, E])
                    first = tb("first", [P, NT, E])
                    second = tb("second", [P, NT, E])
                    taken = tb("taken", [P, NT, E])
                    share = tb("share", [P, NT, E])
                    w0 = tb("w0", [P, NT])
                    w1 = tb("w1", [P, NT])
                    sums = tb("sums", [P, NT, E])
                    upto = tb("upto", [P, NT, E])
                    place = tb("place", [P, NT, E])
                    picked = tb("picked", [P, NT, E])
                    tiles = tb("tiles", [P, E])
                    ends = tb("ends", [P, E])
                    base = tb("base", [P, E])
                    place_f = tb("place_f", [P, 2, NT])
                    place_i = tb("place_i", [P, 2, NT], I32)
                    expert_f = tb("expert_f", [P, SLOTS])
                    gu_at = tb("gu_at", [P, SLOTS], I32)
                    down_at = tb("down_at", [P, SLOTS], I32)
                    send = tb("send", [P, 2, ROW])
                    send_to = tb("send_to", [P, 2], I32)
                    xin = tb("xin", [P, 2, ROW])
                    back = tb("back", [P, 2], I32)
                    back_to = tb("back_to", [P, 2], I32)
                    xT = tb("xT", [P, 2, P])
                    gated = tb("gated", [P, I])
                    inner_h = tb("inner_h", [P, I])
                    hTA = tb("hTA", [P, 2, CA * P])
                    hTB = tb("hTB", [P, CB * P])
                    yout = tb("yout", [P, 2, D])
                    up_ps = pb("up_ps", [P, 4, SEG])
                    ta_ps, tb_ps, xt_ps, y_ps = (pb(x, [P, SEG]) for x in ("ta_ps", "tb_ps", "xt_ps", "y_ps"))

                    s_r, s_shift, s_rexp, s_taken, s_count, s_route = (ts(x) for x in ("r", "shift", "rexp", "taken", "count", "route"))
                    s_send, s_sent = ts("send"), [ts("sent0"), ts("sent1")]
                    s_xin, s_tx, s_xT2 = [ts("xin0"), ts("xin1")], ts("tx"), ts("xT")
                    s_upA, s_upB, s_gA, s_gB, s_hA, s_hB = (ts(x) for x in ("upA", "upB", "gA", "gB", "hA", "hB"))
                    s_tA, s_tB, s_cA, s_cB, s_down, s_y = (ts(x) for x in ("tA", "tB", "cA", "cB", "down", "y"))
                    s_back, s_home, s_g = ts("back"), [ts("home0"), ts("home1")], [ts(f"g{c}") for c in range(4)]

                    STEPS = NT + SLOTS

                    def run(fori, body):
                        def pair(m, kind):
                            for s in range(2):
                                body(m * 2 + s, s, kind)
                        pair(0, None)
                        with fori(1, NT // 2 - 1) as m:
                            pair(m, "shared")
                        pair(NT // 2 - 1, None)
                        pair(NT // 2, None)
                        pair(NT // 2 + 1, None)
                        with fori(NT // 2 + 2, STEPS // 2 - 1) as m:
                            pair(m, "routed")
                        pair(STEPS // 2 - 1, None)
                        body(STEPS, 0, None)

                    def is_routed(t, kind):
                        return t >= NT if isinstance(t, int) else kind == "routed"

                    def exists(t):
                        return not isinstance(t, int) or 0 <= t < STEPS

                    with nc.Block() as block:
                        @block.vector
                        def _(dve):
                            count = [0]

                            def own(ins):
                                count[0] += 1
                                ins.then_inc(s_r, 1)
                                dve.wait_ge(s_r, count[0])

                            def per_token(x):
                                return x.unsqueeze(2).to_broadcast([P, NT, E])

                            own(dve.tensor_reduce(red[:], logits[:], AX.X, ALU.max))
                            dve.tensor_tensor(probs[:], logits[:], per_token(red[:]), ALU.subtract).then_inc(s_shift, 1)
                            dve.wait_ge(s_rexp, 1)
                            own(dve.tensor_reduce(red[:], probs[:], AX.X, ALU.add))
                            own(dve.reciprocal(red[:], red[:]))
                            own(dve.tensor_tensor(probs[:], probs[:], per_token(red[:]), ALU.mult))
                            them = probs[:].unsqueeze(2).to_broadcast([P, NT, E, E])
                            it = probs[:].unsqueeze(3).to_broadcast([P, NT, E, E])
                            four = lambda x: x[:].rearrange("p t (e f) -> p t e f", e=E)
                            dve.tensor_tensor(four(above), them, it, ALU.is_gt)
                            own(dve.tensor_tensor(four(equal), them, it, ALU.is_equal))
                            own(dve.tensor_tensor(equal[:], equal[:], earlier[:].unsqueeze(1).to_broadcast([P, NT, E * E]), ALU.mult))
                            own(dve.tensor_tensor(above[:], above[:], equal[:], ALU.add))
                            own(dve.tensor_reduce(rank[:], four(above), AX.X, ALU.add))
                            dve.tensor_scalar(taken[:], rank[:], 1.5, None, ALU.is_lt).then_inc(s_taken, 1)
                            dve.tensor_scalar(first[:], rank[:], 0.0, None, ALU.is_equal)
                            own(dve.tensor_scalar(second[:], rank[:], 1.0, None, ALU.is_equal))
                            own(dve.tensor_tensor(share[:], taken[:], probs[:], ALU.mult))
                            own(dve.tensor_reduce(red[:], share[:], AX.X, ALU.add))
                            own(dve.tensor_scalar(red[:], red[:], 1e-8, None, ALU.add))
                            own(dve.reciprocal(red[:], red[:]))
                            own(dve.tensor_tensor(share[:], share[:], per_token(red[:]), ALU.mult))
                            own(dve.tensor_tensor(picked[:], first[:], share[:], ALU.mult))
                            own(dve.tensor_reduce(w0[:], picked[:], AX.X, ALU.add))
                            own(dve.tensor_tensor(picked[:], second[:], share[:], ALU.mult))
                            own(dve.tensor_reduce(w1[:], picked[:], AX.X, ALU.add))
                            dve.wait_ge(s_count, 1)
                            count_ps = y_ps[:].rearrange("p (k t e) -> p k t e", k=2, e=E)
                            own(dve.tensor_copy(sums[:], count_ps[:, 1]))
                            for e in range(E):
                                ins = dve.tensor_tensor_scan(upto[:, :, e], ones_tile[:], sums[:, :, e], 0.0, ALU.mult, ALU.add)
                            own(ins)
                            counted = above[:].rearrange("p t f -> p (t f)")[:, 0:E * NT].rearrange("p (e t) -> p e t", e=E)
                            own(dve.tensor_tensor(counted, upto[:, NT - 1, :].unsqueeze(2).to_broadcast([P, E, NT]),
                                                  tile_start[:, 0:NT].unsqueeze(1).to_broadcast([P, E, NT]), ALU.is_gt))
                            own(dve.tensor_reduce(tiles[:], counted, AX.X, ALU.add))
                            own(dve.tensor_tensor_scan(ends[:], ones_tile[:, 0:E], tiles[:], 0.0, ALU.mult, ALU.add))
                            own(dve.tensor_tensor(base[:], ends[:], tiles[:], ALU.subtract))
                            own(dve.tensor_scalar(base[:], base[:], float(P), None, ALU.mult))
                            own(dve.tensor_tensor(place[:], upto[:], sums[:], ALU.subtract))
                            own(dve.tensor_tensor(place[:], place[:], count_ps[:, 0], ALU.add))
                            own(dve.tensor_tensor(place[:], place[:], base[:].unsqueeze(1).to_broadcast([P, NT, E]), ALU.add))
                            own(dve.tensor_tensor(picked[:], first[:], place[:], ALU.mult))
                            own(dve.tensor_reduce(place_f[:, 0, :], picked[:], AX.X, ALU.add))
                            own(dve.tensor_tensor(picked[:], second[:], place[:], ALU.mult))
                            own(dve.tensor_reduce(place_f[:, 1, :], picked[:], AX.X, ALU.add))
                            dve.tensor_copy(place_i[:], place_f[:])
                            ended = equal[:].rearrange("p t f -> p (t f)")[:, 0:SLOTS * E].rearrange("p (t e) -> p t e", e=E)
                            own(dve.tensor_tensor(ended, ends[:].unsqueeze(1).to_broadcast([P, SLOTS, E]),
                                                  tile_number[:].unsqueeze(2).to_broadcast([P, SLOTS, E]), ALU.is_le))
                            own(dve.tensor_reduce(expert_f[:], ended, AX.X, ALU.add))
                            own(dve.tensor_scalar(expert_f[:], expert_f[:], float(E - 1), None, ALU.min))
                            dve.tensor_scalar(gu_at[:], expert_f[:], float(GU), None, ALU.mult)
                            dve.tensor_scalar(down_at[:], expert_f[:], float(NC * D), None, ALU.mult).then_inc(s_route, 1)

                            def body(t, s, kind):
                                if exists(t):
                                    wait(dve, s_tA, t)
                                    dve.wait_ge(s_gA, t + 1)
                                    dve.tensor_tensor(inner_h[:, 0:IA], gated[:, 0:IA], up_ps[:, 1, 0:IA], ALU.mult).then_inc(s_hA, 1)
                                    if is_routed(t, kind):
                                        k = t - NT
                                        dve.wait_ge(s_xin[s], (k - s) * 8 + 16)
                                        wait(dve, s_y, t - 1)
                                        dve.tensor_copy(back[:, s:s + 1], xin[:, s, D:ROW].bitcast(I32)).then_inc(s_back, 1)
                                    wait(dve, s_tB, t)
                                    dve.wait_ge(s_gB, t + 1)
                                    dve.tensor_tensor(inner_h[:, IA:I], gated[:, IA:I], up_ps[:, 3, 0:IB], ALU.mult).then_inc(s_hB, 1)
                                if exists(t - 1):
                                    if not is_routed(t - 1, kind):
                                        dve.wait_ge(s_down, t)
                                        dve.tensor_tensor(X[:, ds((t - 1) * D, D)], X[:, ds((t - 1) * D, D)], y_ps[:, 0:D], ALU.add).then_inc(s_y, 1)
                                    else:
                                        k = t - 1 - NT
                                        wait(dve, s_home[1 - s], (k - (1 - s)) * 8)
                                        dve.wait_ge(s_back, k + 1)
                                        dve.tensor_copy(back_to[:, 1 - s:2 - s], back[:, 1 - s:2 - s])
                                        dve.wait_ge(s_down, t)
                                        dve.tensor_copy(yout[:, 1 - s, :], y_ps[:, 0:D]).then_inc(s_y, 1)
                            run(dve.Fori, body)

                            for c in range(4):
                                dve.wait_ge(s_g[c], 32)
                                with dve.Fori(c * NT // 4, (c + 1) * NT // 4) as j:
                                    for g, w in ((G0, w0), (G1, w1)):
                                        dve.scalar_tensor_tensor(X[:, ds(j * D, D)], g[:, ds(j * D, D)], w[:, ds(j, 1)], X[:, ds(j * D, D)],
                                                                 ALU.mult, ALU.add).then_inc(s_r, 1)
                                        dve.wait_ge(s_r, count[0] + j * 2 + (1 if g is G0 else 2))

                        @block.scalar
                        def _(act):
                            act.wait_ge(s_shift, 1)
                            act.activation(probs[:], probs[:], ACT.Exp).then_inc(s_rexp, 1)
                            act.activation(xT[:, 0, :], cols[:, 0:P], ACT.Copy).then_inc(s_xT2, 1)

                            def body(t, s, kind):
                                if exists(t):
                                    wait(act, s_hA, t)
                                    act.wait_ge(s_upA, t + 1)
                                    act.activation(gated[:, 0:IA], up_ps[:, 0, 0:IA], ACT.Silu).then_inc(s_gA, 1)
                                if exists(t - 1):
                                    act.wait_ge(s_tB, t)
                                    act.activation(hTB[:, 0:(CB - 1) * P], tb_ps[:, 0:(CB - 1) * P], ACT.Copy)
                                    act.activation(hTB[0:ITAIL, (CB - 1) * P:CB * P], tb_ps[0:ITAIL, (CB - 1) * P:CB * P], ACT.Copy).then_inc(s_cB, 1)
                                if exists(t):
                                    wait(act, s_hB, t)
                                    act.wait_ge(s_upB, t + 1)
                                    act.activation(gated[:, IA:I], up_ps[:, 2, 0:IB], ACT.Silu).then_inc(s_gB, 1)
                                if exists(t + 1):
                                    if is_routed(t + 1, kind):
                                        act.wait_ge(s_tx, t + 2 - NT)
                                        src = xt_ps[:, 0:P]
                                    else:
                                        src = cols[:, ds((t + 1) * P, P)]
                                    if exists(t):
                                        act.activation(xT[:, 1 - s, :], src, ACT.Copy).then_inc(s_xT2, 1)
                                if exists(t):
                                    act.wait_ge(s_tA, t + 1)
                                    act.activation(hTA[:, s, :], ta_ps[:], ACT.Copy).then_inc(s_cA, 1)
                            run(act.Fori, body)

                        @block.tensor
                        def _(pe):
                            pe.wait_ge(s_taken, 1)
                            pe.matmul(y_ps[:, 0:NT * E], before[:], taken[:].rearrange("p t e -> p (t e)"), start=True, stop=True)
                            pe.matmul(y_ps[:, NT * E:2 * NT * E], all_ones[:], taken[:].rearrange("p t e -> p (t e)"), start=True, stop=True).then_inc(s_count, 1)
                            pe.wait_ge(s_route, 1)
                            if n and "mamba" in phases:
                                pe.wait_ge(lodgers_in, 16 * 3 * LODGERS)

                            def up(t, s, half, at, width, where):
                                for bank, off in ((2 * half, 0), (2 * half + 1, I)):
                                    mm = pe.matmul(up_ps[:, bank, 0:width], xT[:, s, :], gate_up[:, ds(where + (off + at), width)] if not isinstance(where, int)
                                                   else gate_up[:, where + off + at:where + off + at + width], start=True, stop=True)
                                return mm

                            def expert(table, t, kind, each):
                                if is_routed(t, kind):
                                    return pe.value_load(table[0:1, ds(t - NT, 1)], min_val=0, max_val=(E - 1) * each)
                                return E * each

                            def body(t, s, kind):
                                if exists(t):
                                    where = expert(gu_at, t, kind, GU)
                                    pe.wait_ge(s_xT2, t + 1)
                                    wait(pe, s_hA, t)
                                    up(t, s, 0, 0, IA, where).then_inc(s_upA, 1)
                                if exists(t - 1):
                                    pe.wait_ge(s_hB, t)
                                    wait(pe, s_cB, t - 1)
                                    for c in range(CB):
                                        w = P if c < CB - 1 else ITAIL
                                        mm = pe.transpose(tb_ps[0:w, c * P:(c + 1) * P], inner_h[:, IA + c * P:IA + c * P + w], ident[:])
                                    mm.then_inc(s_tB, 1)
                                if exists(t):
                                    up(t, s, 1, IA, IB, where).then_inc(s_upB, 1)
                                if exists(t + 1) and exists(t) and is_routed(t + 1, kind):
                                    k = t + 1 - NT
                                    pe.wait_ge(s_xin[1 - s], (k - (1 - s)) * 8 + 16)
                                    pe.transpose(xt_ps[:, 0:P], xin[:, 1 - s, 0:D], ident[:]).then_inc(s_tx, 1)
                                if exists(t):
                                    wait(pe, s_cA, t)
                                    pe.wait_ge(s_hA, t + 1)
                                    for c in range(CA):
                                        mm = pe.transpose(ta_ps[:, c * P:(c + 1) * P], inner_h[:, c * P:(c + 1) * P], ident[:])
                                    mm.then_inc(s_tA, 1)
                                if exists(t - 1):
                                    where = expert(down_at, t - 1, kind, NC * D)
                                    wait(pe, s_y, t - 1)
                                    pe.wait_ge(s_cB, t)
                                    pe.wait_ge(s_cA, t)
                                    for c in range(NC):
                                        w = P if c < NC - 1 else ITAIL
                                        lhs = hTA[0:w, 1 - s, c * P:(c + 1) * P] if c < CA else hTB[0:w, (c - CA) * P:(c - CA + 1) * P]
                                        rhs = down[0:w, where + c * D:where + (c + 1) * D] if isinstance(where, int) else down[0:w, ds(where + c * D, D)]
                                        mm = pe.matmul(y_ps[:, 0:D], lhs, rhs, start=(c == 0), stop=(c == NC - 1))
                                    mm.then_inc(s_down, 1)
                            run(pe.Fori, body)

                        @block.sync
                        def _(sp):
                            for q in range(2):
                                sp.wait_ge(s_sent[q], 16 * NT)
                            def load(k, s):
                                wait(sp, s_back, k - 1)
                                wait(sp, s_tx, k - 1)
                                sp.dma_start(xin[:, s, :], routed[n][ds(k * P, P), :]).then_inc(s_xin[s], 16)
                            load(0, 0), load(1, 1)
                            with sp.Fori(1, SLOTS // 2) as m:
                                load(m * 2, 0), load(m * 2 + 1, 1)
                            for q in range(2):
                                sp.wait_ge(s_home[q], 16 * SLOTS // 2)
                            for c in range(4):
                                for q, g in enumerate((G0, G1)):
                                    j = slice(c * NT // 4, (c + 1) * NT // 4)
                                    sp.dma_start(g[:].rearrange("p (t d) -> p t d", d=D)[:, j, :],
                                                 expert_out[n][q * B * T:(q + 1) * B * T, :].rearrange("(t p) d -> p t d", p=P)[:, j, :]).then_inc(s_g[c], 16)

                        @block.gpsimd
                        def _(pool):
                            copied, result, stored = (pool.alloc_register(f"f{n}_{x}") for x in ("copied", "result", "stored"))
                            pool.reg_mov(copied, 0)
                            pool.reg_mov(result, NT)
                            pool.wait_ge(s_route, 1)

                            def send_row(j, q):
                                t = j * 2 + q
                                pool.reg_add(copied, copied, 1)
                                pool.wait_ge(prefilled, 32)
                                wait(pool, s_sent[q], j * 16)
                                pool.tensor_copy(send[:, q, 0:D], rows[:, ds(j * D, D)])
                                pool.tensor_copy(send[:, q, D:ROW].bitcast(I32), token_row[:, ds(j + q * NT, 1)])
                                pool.tensor_copy(send_to[:, q:q + 1], place_i[:, q, ds(j, 1)]).then_inc(s_send, 1)
                                pool.wait_ge(s_route, 1)
                                pool.wait_ge(s_send, copied)
                                pool.indirect_dma_start(routed[n], bass.IndirectOffsetOnAxis(ap=send_to[:, q:q + 1].bitcast(U32), axis=0),
                                                        send[:, q, :], None).then_inc(s_sent[q], 16)
                            send_row(0, 0), send_row(0, 1)
                            with pool.Fori(1, NT) as j:
                                send_row(j, 0), send_row(j, 1)

                            def home(k, s):
                                pool.reg_add(result, result, 1)
                                if not isinstance(k, int):
                                    pool.reg_mov(stored, (k + s) * 8)
                                pool.wait_ge(s_route, 1)
                                pool.wait_ge(s_y, result)
                                wait(pool, s_home[1 - s], k * 16 if isinstance(k, int) else stored)
                                pool.indirect_dma_start(expert_out[n], bass.IndirectOffsetOnAxis(ap=back_to[:, s:s + 1].bitcast(U32), axis=0),
                                                        yout[:, s, :], None).then_inc(s_home[s], 16)
                            home(0, 0), home(1, 1)
                            with pool.Fori(1, SLOTS // 2) as m:
                                home(m * 2, 0), home(m * 2 + 1, 1)


        def mamba():
            scope = ExitStack()
            with scope:
                def tb(name, shape, dt=F32):
                    return sb("m_" + name, shape, dt, scope)

                def ts(name):
                    return sem("m_" + name, scope)

                taps = tb("taps", [P, NL * HALF * TAPS])
                in_tapT = tb("in_tapT", [P, NL * HALF, TAPS, P])
                gateT_w = tb("gateT_w", [P, NL * DI])
                conv_b = tb("conv_b", [P, NL * HALF])
                x_w = tb("x_w", [P, NL * HALF, XR])
                dt_w = tb("dt_w", [XR, NL * DI])
                dt_b = tb("dt_b", [P, NL * HALF])
                decay = tb("decay", [P, NL * HALF * NS])
                skip = tb("skip", [P, NL * HALF])
                skip_diag = tb("skip_diag", [P, NL * HALF, P])
                out_w = tb("out_w", [P, NL * HALF, D])
                spread = tb("spread", [3 * 32, 2 * NS * P], BF16)
                xn = tb("xn", [P, TPB, D])
                xT = tb("xT", [P, TAPS - 1 + T])
                u = tb("u", [P, HALF, T])
                z = tb("z", [P, HALF, T])
                parts = tb("parts", [3 * 32, T], BF16)
                delta = tb("delta", [P, HALF, T])
                delta_u = tb("delta_u", [P, HALF, T])
                state = tb("state", [P, 2, T])
                c_sb = tb("c_sb", [P, 2, T])
                spare = gate_up[:, (E - LODGERS) * GU:E * GU]
                seen = spare[:, 0:2 * T].rearrange("p (s t) -> p s t", s=2)
                bc = spare[0:XR, 2 * T:3 * T]
                drive = down[:, (E - LODGERS) * NC * D:E * NC * D].rearrange("p (s t) -> p s t", s=2)
                in_w = c_sb[:, 0, 0:NL * HALF * D]
                in_tap = state[:].rearrange("p s (a k d) -> p (s a) k d", k=TAPS, d=D)
                rest = c_sb[0:32, 0, :]
                mid = c_sb[0:32, 1, 0:T // 2].bitcast(BF16)

                ps = scope.enter_context(nc.psum_tensor("m_ps", [P, 4, T], F32))
                Y, PB, PC, DA = (ps[:, i, :] for i in range(4))
                seg = lambda x, i: x[:, i * SEG:(i + 1) * SEG]
                SEGS = T // SEG
                STEPS = HALF * NS

                s_w, s_set = ts("w"), ts("set")
                s_stats, s_var, s_std, s_rstd = ts("stats"), ts("var"), ts("std"), ts("rstd")
                s_ln, s_turn, s_xT, s_proj, s_silu, s_xd, s_bc = (ts(x) for x in ("ln", "turn", "xT", "proj", "silu", "xd", "bc"))
                s_dt, s_pre, s_soft, s_dtu, s_split, s_parts = (ts(x) for x in ("dt", "pre", "soft", "dtu", "split", "parts"))
                s_b, s_c, s_acc = ts("b"), ts("c"), ts("acc")
                s_drive, s_decay, s_c_sb, s_state, s_seen = ts("drive"), ts("decay"), ts("c_sb"), ts("state"), ts("seen")
                s_y, s_out, s_x = ts("y"), ts("out"), ts("x")

                weights = [(in_w, "m_in"), (taps[:], "m_taps"), (gateT_w[:], "m_gateT"), (conv_b[:], "m_conv_b"),
                           (x_w[:].rearrange("p a r -> p (a r)"), "m_xT"), (dt_w[2 * NS:XR, :], "m_dtT"), (dt_b[:], "m_dt_b"),
                           (decay[:], "m_A_log"), (skip[:], "m_skip"), (out_w[:].rearrange("p a d -> p (a d)"), "m_outT"), (spread[:], "m_spread")]
                WEIGHTS = 16 * len(weights)

                with nc.Block() as block:
                    @block.sync
                    def _(sp):
                        for dst, name in weights:
                            sp.dma_start(dst, a[name]).then_inc(s_w, 16)

                    @block.vector
                    def _(dve):
                        dve.memset(xT[:, 0:TAPS - 1], 0.0)
                        stats_dve(dve, s_stats, s_var, s_std, s_rstd)
                        dve.wait_ge(s_w, WEIGHTS)
                        for lh in range(NL * HALF):
                            for k in range(TAPS):
                                dve.tensor_scalar(in_tap[:, lh, k, :], in_w[:, lh * D:(lh + 1) * D], taps[:, lh * TAPS + k:lh * TAPS + k + 1], None, ALU.mult)
                            dve.tensor_scalar(skip_diag[:, lh, :], ident[:], skip[:, lh:lh + 1], None, ALU.mult).then_inc(s_set, 1)
                        dve.wait_ge(s_var, 2)
                        dve.tensor_scalar(decay[:], decay[:], -1.0, None, ALU.mult)

                    @block.scalar
                    def _(act):
                        stats_act(act, s_var, s_std)
                        act.wait_ge(s_w, WEIGHTS)
                        act.activation(decay[:], decay[:], ACT.Exp).then_inc(s_var, 1)
                        for lh in range(NL * HALF):
                            act.wait_ge(s_turn, lh + 1)
                            act.activation(in_tapT[:, lh].rearrange("p k d -> p (k d)"), ps[:, lh, 0:TAPS * P], ACT.Copy)

                    @block.tensor
                    def _(pe):
                        for lh in range(NL * HALF):
                            pe.wait_ge(s_set, lh + 1)
                            for k in range(TAPS):
                                mm = pe.transpose(ps[:, lh, k * P:(k + 1) * P], in_tap[:, lh, k, :], ident[:])
                            mm.then_inc(s_turn, 1)

                with nc.Block() as block:
                    @block.tensor
                    def _(pe):
                        pe.sem_inc(s_acc, 2)
                        with pe.Fori(0, B) as b:
                            pe.wait_ge(s_ln, b + 1)
                            for i in range(TPB):
                                mm = pe.transpose(PB[:, i * P:(i + 1) * P], xn[:, i, :], ident[:])
                            mm.then_inc(s_turn, 1)
                            for l in range(NL):
                                it = b * NL + l
                                pe.wait_ge(s_xT, it + 1)
                                for h, bank in enumerate((Y, PB)):
                                    for i in range(SEGS):
                                        for k in range(TAPS):
                                            mm = pe.matmul(seg(bank, i), in_tapT[:, l * HALF + h, k, :], xT[:, i * SEG + k:i * SEG + k + SEG], start=(k == 0), stop=(k == TAPS - 1))
                                    mm.then_inc(s_proj, 1)
                                for h, bank in enumerate((PC, DA)):
                                    for i in range(SEGS):
                                        mm = pe.matmul(seg(bank, i), gateT_w[:, l * DI + h * P:l * DI + (h + 1) * P], xT[:, TAPS - 1 + i * SEG:TAPS - 1 + (i + 1) * SEG], start=True, stop=True)
                                    mm.then_inc(s_proj, 1)
                                pe.wait_ge(s_silu, it * 4 + 2)
                                for i in range(SEGS):
                                    for h in range(HALF):
                                        mm = pe.matmul(seg(Y, i)[0:XR], x_w[:, l * HALF + h, :], u[:, h, i * SEG:(i + 1) * SEG], start=(h == 0), stop=(h == HALF - 1))
                                mm.then_inc(s_xd, 1)
                                pe.wait_ge(s_bc, it + 1)
                                for h, bank in enumerate((PB, Y)):
                                    for i in range(SEGS):
                                        mm = pe.matmul(seg(bank, i), dt_w[2 * NS:XR, l * DI + h * P:l * DI + (h + 1) * P], bc[2 * NS:XR, i * SEG:(i + 1) * SEG], start=True, stop=True)
                                    mm.then_inc(s_dt, 1)
                                pe.wait_ge(s_silu, it * 4 + 4)
                                pe.wait_ge(s_parts, it + 1)

                                for h in range(HALF):
                                    g0 = it * STEPS + h * NS

                                    def broadcast(n):
                                        g = g0 + n
                                        pe.wait_ge(s_drive, g + 1)
                                        for i in range(SEGS):
                                            mm = pe.matmul(seg(PB, i), spread[:, ds(n * P, P)], parts[:, i * SEG:(i + 1) * SEG], start=True, stop=True)
                                        mm.then_inc(s_b, 1)
                                        pe.wait_ge(s_c_sb, g + 1)
                                        for i in range(SEGS):
                                            mm = pe.matmul(seg(PC, i), spread[:, ds((n + NS) * P, P)], parts[:, i * SEG:(i + 1) * SEG], start=True, stop=True)
                                        mm.then_inc(s_c, 1)

                                    def accumulate(n, s, last=False):
                                        pe.wait_ge(s_seen, g0 + n + 3)
                                        for i in range(SEGS):
                                            mm = pe.matmul(seg(Y, i), ident[:], seen[:, s, i * SEG:(i + 1) * SEG], start=False, stop=last, skip_group_check=True)
                                        mm.then_inc(s_acc, 1)

                                    if h:
                                        pe.wait_ge(s_y, it * 2 + 1)
                                    for i in range(SEGS):
                                        pe.matmul(seg(Y, i), skip_diag[:, l * HALF + h, :], u[:, h, i * SEG:(i + 1) * SEG], start=True, stop=False, skip_group_check=True)
                                    broadcast(0)
                                    broadcast(1)
                                    with pe.Fori(0, NS // 2 - 1) as m:
                                        for s in range(2):
                                            broadcast(m * 2 + s + 2)
                                            accumulate(m * 2 + s, s)
                                    accumulate(NS - 2, 0)
                                    accumulate(NS - 1, 1, True)
                                pe.wait_ge(s_y, it * 2 + 2)
                                if l < NL - 1:
                                    for i in range(SEGS):
                                        for h in range(HALF):
                                            mm = pe.matmul(seg(PB, i), out_w[:, l * HALF + h, :], z[:, h, i * SEG:(i + 1) * SEG], start=(h == 0), stop=(h == HALF - 1))
                                else:
                                    for i in range(TPB):
                                        for h in range(HALF):
                                            mm = pe.matmul(PB[:, i * P:(i + 1) * P], z[:, h, i * P:(i + 1) * P], out_w[:, l * HALF + h, :], start=(h == 0), stop=(h == HALF - 1))
                                mm.then_inc(s_out, 1)

                    @block.scalar
                    def _(act):
                        act.sem_inc(s_c_sb, 1)
                        with act.Fori(0, B) as b:
                            act.wait_ge(s_turn, b + 1 + NL * HALF)
                            act.activation(xT[:, TAPS - 1:TAPS - 1 + T], PB, ACT.Copy).then_inc(s_xT, 1)
                            for l in range(NL):
                                it = b * NL + l
                                for h, bank in enumerate((Y, PB)):
                                    act.wait_ge(s_proj, it * 4 + h + 1)
                                    act.activation(u[:, h, :], bank, ACT.Silu, bias=conv_b[:, l * HALF + h:l * HALF + h + 1]).then_inc(s_silu, 1)
                                act.wait_ge(s_xd, it + 1)
                                act.activation(bc, Y[0:XR], ACT.Copy).then_inc(s_bc, 1)
                                for h, bank in enumerate((PC, DA)):
                                    act.wait_ge(s_proj, it * 4 + h + 3)
                                    act.activation(z[:, h, :], bank, ACT.Silu).then_inc(s_silu, 1)
                                act.wait_ge(s_pre, it * 2 + 2)
                                act.activation(delta_u[:], delta[:], ACT.Abs).then_inc(s_soft, 1)
                                act.wait_ge(s_soft, it * 3 + 1)
                                act.activation(delta_u[:], delta_u[:], ACT.Exp, scale=-1.0).then_inc(s_soft, 1)
                                act.wait_ge(s_soft, it * 3 + 2)
                                act.activation(delta_u[:], delta_u[:], ACT.Ln, bias=1.0).then_inc(s_soft, 1)
                                act.wait_ge(s_silu, it * 4 + 4)
                                act.wait_ge(s_dtu, it + 1)
                                for h in range(HALF):
                                    with act.Fori(0, NS // 2) as m:
                                        for s in range(2):
                                            g = it * STEPS + (h * NS + s) + m * 2
                                            act.wait_ge(s_state, g + 1)
                                            act.activation(DA, delta[:, h, :], ACT.Exp, scale=decay[:, ds(m * 2 + ((l * HALF + h) * NS + s), 1)]).then_inc(s_decay, 1)
                                            act.wait_ge(s_c, g + 1)
                                            act.wait_ge(s_seen, g + 1)
                                            act.activation(c_sb[:, s, :], PC, ACT.Copy).then_inc(s_c_sb, 1)
                                if l < NL - 1:
                                    act.wait_ge(s_out, it + 1)
                                    act.activation(xT[:, TAPS - 1:TAPS - 1 + T], PB, ACT.Copy).then_inc(s_xT, 1)

                    @block.gpsimd
                    def _(pool):
                        pool.sem_inc(s_seen, 2)
                        with pool.Fori(0, B * NL * STEPS // 2) as m:
                            for s in range(2):
                                g = m * 2 + s
                                pool.wait_ge(s_c_sb, g + 2)
                                pool.wait_ge(s_state, g + 2)
                                pool.wait_ge(s_acc, g + 1)
                                pool.tensor_tensor(seen[:, s, :], state[:, s, :], c_sb[:, s, :], ALU.mult).then_inc(s_seen, 1)

                    @block.vector
                    def _(dve):
                        dve.sem_inc(s_drive, 1)
                        dve.sem_inc(s_state, 1)
                        with dve.Fori(0, B) as b:
                            for i in range(TPB):
                                ins = dve.tensor_scalar(xn[:, i, :], X[:, ds(b * T + i * P, P)], mean[:, ds(b * TPB + i, 1)], rstd[:, ds(b * TPB + i, 1)], ALU.subtract, ALU.mult)
                            ins.then_inc(s_ln, 1)
                            for l in range(NL):
                                it = b * NL + l
                                for h, bank in enumerate((PB, Y)):
                                    dve.wait_ge(s_dt, it * 2 + h + 1)
                                    dve.tensor_scalar(delta[:, h, :], bank, dt_b[:, l * HALF + h:l * HALF + h + 1], None, ALU.add).then_inc(s_pre, 1)
                                dve.wait_ge(s_bc, it + 1)
                                dve.tensor_copy(parts[0:32, :], bc[0:32, :]).then_inc(s_split, 1)
                                dve.wait_ge(s_split, it * 3 + 1)
                                dve.tensor_tensor(rest, bc[0:32, :], parts[0:32, :], ALU.subtract).then_inc(s_split, 1)
                                dve.wait_ge(s_split, it * 3 + 2)
                                dve.tensor_copy(mid, rest).then_inc(s_split, 1)
                                dve.wait_ge(s_split, it * 3 + 3)
                                dve.tensor_copy(parts[32:64, :], mid)
                                dve.wait_ge(s_soft, it * 3 + 3)
                                dve.scalar_tensor_tensor(delta[:], delta[:], 0.0, delta_u[:], ALU.max, ALU.add).then_inc(s_x, 1)
                                dve.wait_ge(s_x, b * 4 + l + 1)
                                dve.tensor_tensor(delta_u[:], delta[:], u[:], ALU.mult).then_inc(s_dtu, 1)
                                dve.wait_ge(s_dtu, it + 1)
                                dve.tensor_tensor(parts[64:96, :], rest, mid, ALU.subtract).then_inc(s_parts, 1)
                                for h in range(HALF):
                                    with dve.Fori(0, NS // 2) as m:
                                        for s in range(2):
                                            g = it * STEPS + (h * NS + s) + m * 2
                                            dve.wait_ge(s_b, g + 1)
                                            dve.tensor_tensor(drive[:, s, :], delta_u[:, h, :], PB, ALU.mult).then_inc(s_drive, 1)
                                            dve.wait_ge(s_drive, g + 2)
                                            dve.wait_ge(s_decay, g + 1)
                                            dve.wait_ge(s_seen, g + 1)
                                            dve.tensor_tensor_scan(state[:, s, :], DA, drive[:, s, :], 0.0, ALU.mult, ALU.add).then_inc(s_state, 1)
                                    dve.wait_ge(s_acc, (it * HALF + h + 1) * NS + 2)
                                    dve.tensor_tensor(z[:, h, :], z[:, h, :], Y, ALU.mult).then_inc(s_y, 1)
                            dve.tensor_tensor(X[:, ds(b * T, T)], X[:, ds(b * T, T)], xn[:].rearrange("p t d -> p (t d)"), ALU.add).then_inc(s_x, 1)
                            dve.wait_ge(s_x, b * 4 + 3)
                            dve.wait_ge(s_out, b * NL + NL)
                            dve.tensor_tensor(X[:, ds(b * T, T)], X[:, ds(b * T, T)], PB, ALU.add).then_inc(s_x, 1)
                            dve.wait_ge(s_x, b * 4 + 4)

        if "attention" in phases:
            attention()
        else:
            with nc.Block() as block:
                @block.sync
                def _(sp):
                    load_x(sp)
                    sp.wait_ge(x_in, 64)
                    sp.dma_start(ident[:], a["ident"]).then_inc(small_in, 16)
                    sp.wait_ge(small_in, 16)
                    load_experts(sp)
                    prefill(sp)
        if "ffn1" in phases:
            ffn(0)
        if "mamba" in phases:
            mamba()
        if "ffn2" in phases:
            ffn(1)

        s_out = sem("s_out")
        with nc.Block() as block:
            @block.sync
            def _(sp):
                sp.dma_start(out.rearrange("(t p) d -> p t d", p=P), X[:].rearrange("p (t d) -> p t d", d=D)).then_inc(s_out, 16)
                sp.wait_ge(s_out, 16)
                sp.wait_ge(experts_in, EXPERTS_IN)
                sp.wait_ge(prefilled, 32)


def lay_out(v):
    f = lambda n: np.asarray(v[n], np.float32)
    c = np.ascontiguousarray
    o = {}
    o["x"] = c(f("L0_attn_a_x").reshape(B * T, D))
    o["wqkvT"] = c(f("L0_attn_a_Wqkv").T)
    o["bqkv"] = c(f("L0_attn_a_bqkv").reshape(3, D).T)
    o["woT"] = c(f("L0_attn_a_Wo").T)
    o["bo"] = c(f("L0_attn_a_bo").reshape(1, D))
    gu = np.concatenate([f("L0_ffn_experts_gate_up"), f("L0_ffn_shared_gate_up")[None]])
    o["gate_up"] = c(gu.transpose(2, 0, 1).reshape(D, (E + 1) * GU))
    dn = np.concatenate([f("L0_ffn_experts_down"), f("L0_ffn_shared_down")[None]]).transpose(0, 2, 1)
    o["down"] = c(dn[:, :(NC - 1) * P].reshape(E + 1, NC - 1, P, D).transpose(2, 0, 1, 3).reshape(P, -1))
    o["down_tail"] = c(dn[:, (NC - 1) * P:].transpose(1, 0, 2).reshape(ITAIL, -1))
    o["gateT"] = c(f("L0_ffn_gate_weight").T)
    chan = lambda x: c(x.reshape(NL, HALF, P, -1).transpose(2, 0, 1, 3).reshape(P, -1))
    w_in = f("L0_attn_b_W_in")
    o["m_in"] = chan(w_in[:, :DI])
    o["m_gateT"] = c(w_in[:, DI:].transpose(2, 0, 1).reshape(D, NL * DI))
    o["m_taps"], o["m_conv_b"] = chan(f("L0_attn_b_conv_w")), chan(f("L0_attn_b_conv_b"))
    w_x = f("L0_attn_b_W_x")
    o["m_xT"] = chan(np.concatenate([w_x[:, RANK:], w_x[:, :RANK]], 1).transpose(0, 2, 1))
    o["m_dtT"] = c(f("L0_attn_b_W_dt").transpose(2, 0, 1).reshape(RANK, NL * DI))
    o["m_dt_b"], o["m_A_log"], o["m_skip"] = chan(f("L0_attn_b_b_dt")), chan(f("L0_attn_b_A_log")), chan(f("L0_attn_b_D"))
    o["m_outT"] = chan(f("L0_attn_b_W_out").transpose(0, 2, 1))
    o["m_spread"] = np.repeat(np.tile(np.eye(2 * NS), (3, 1)), P, 1).astype(mybir.dt.np(BF16))
    p = np.arange(P)
    o["ident"] = np.eye(P, dtype=np.float32)
    o["ones_row"] = np.ones((1, P), np.float32)
    o["ones_tile"] = np.ones((P, NT), np.float32)
    o["all_ones"] = np.ones((P, P), np.float32)
    o["before"] = (p[:, None] < p).astype(np.float32)
    o["earlier"] = np.tile((np.arange(E) < np.arange(E)[:, None]).astype(np.float32).reshape(1, -1), (P, 1))
    o["tile_number"] = np.tile(np.arange(SLOTS, dtype=np.float32), (P, 1))
    o["tile_start"] = o["tile_number"] * P
    o["token_row"] = c(np.arange(2 * B * T, dtype=np.int32).reshape(2 * NT, P).T)
    o["nobody"] = np.zeros((P, ROW), np.int32)
    o["nobody"][:, D] = 2 * B * T + p
    o["own_head"] = c(np.repeat((p[:, None] % 32 // HD == np.arange(HG)).astype(np.float32), 32, 1))
    q, k = (p % 32)[:, None, None], np.arange(KW)
    seen = (k > q) & (k <= q + 32) & np.ones((1, NW, 1), bool)
    first = seen & ((np.arange(NW)[:, None] > 0) | (k >= 32))
    o["mask"] = c(np.where(np.stack([seen, first], 1), 0, MASKED).astype(np.float32).reshape(P, -1))
    return o


PHASES = ("attention", "ffn1", "mamba", "ffn2")


def kernel(**inputs):
    import concourse.bacc as bacc
    from concourse.bass_utils import run_bass_kernel_spmd

    nc = bacc.Bacc("TRN2", target_bir_lowering=False, num_devices=1)
    arrays = lay_out(inputs)
    aps = {n: nc.dram_tensor("in_" + n, v.shape, mybir.dt.from_np(v.dtype), kind="ExternalInput").ap() for n, v in arrays.items()}
    out = nc.dram_tensor("out", (B * T, D), F32, kind="ExternalOutput").ap()
    hybrid_block_kernel(nc, aps, out, PHASES)
    r = run_bass_kernel_spmd(nc, [{"in_" + n: v for n, v in arrays.items()}], core_ids=[0])
    return r.results[0]["out"].reshape(B, T, D)
```

```python
from contextlib import ExitStack

import concourse.bass as bass
from concourse import mybir
import numpy as np

F32 = mybir.dt.float32
BF16 = mybir.dt.bfloat16
I32 = mybir.dt.int32
U32 = mybir.dt.uint32
ALU = mybir.AluOpType
ACT = mybir.ActivationFunctionType
AX = mybir.AxisListType
ds = bass.ds

P = 128
B, T, D = 4, 1024, 128
NT = B * T // P
TPB = T // P
EPS = 1e-5

H, HD, WIN = 16, 8, 32
HG = P // 32
NG = H // HG
NW = P // 32
KW = 64
MASKED = -1e30

E, I = 8, 938
GU = 2 * I
IA = 512
IB = I - IA
CA, CB = IA // P, -(-IB // P)
ITAIL = IB - (CB - 1) * P
NC = CA + CB
LODGERS = 8
SLOTS = 2 * NT + E
ROW = D + 1

NL, DI, NS, TAPS, RANK = 2, 256, 16, 4, 8
HALF = DI // P
STREAMS = 2
XR = 2 * NS + RANK
SEG = 512


def wait(eng, sem, value):
    if isinstance(value, int) and value <= 0:
        return
    eng.wait_ge(sem, value)


def hybrid_block_kernel(nc, a, out, phases):
    ctx = ExitStack()
    with ctx:
        def sb(name, shape, dt=F32, scope=ctx):
            return scope.enter_context(nc.sbuf_tensor(name, shape, dt))

        def sem(name, scope=ctx):
            return scope.enter_context(nc.semaphore(name))

        X = sb("X", [P, NT * D])
        ident = sb("ident", [P, P])
        gate_up = sb("gate_up", [P, (E + 1) * GU])
        down = sb("down", [P, (E + 1) * NC * D])
        gateT = sb("gateT", [P, E])
        mean = sb("mean", [P, NT])
        rstd = sb("rstd", [P, NT])
        row_stats = sb("row_stats", [P, NT, 6])
        apart = sb("apart", [P, NT])

        ones_tile = sb("ones_tile", [P, NT])
        all_ones = sb("all_ones", [P, P])
        before = sb("before", [P, P])
        earlier = sb("earlier", [P, E * E])
        tile_number = sb("tile_number", [P, SLOTS])
        tile_start = sb("tile_start", [P, SLOTS])
        token_row = sb("token_row", [P, 2 * NT], I32)
        nobody = sb("nobody", [P, ROW], I32)

        routed = [nc.dram_tensor(f"routed_{n}", (SLOTS * P, ROW), F32, kind="Internal").ap() for n in range(2)]
        expert_out = [nc.dram_tensor(f"expert_out_{n}", (2 * B * T + P, D), F32, kind="Internal").ap() for n in range(2)]

        x_in = sem("x_in")
        small_in = sem("small_in")
        experts_in = sem("experts_in")
        prefilled = sem("prefilled")

        def load_x(sp):
            x_d = a["x"].rearrange("(t p) d -> p t d", p=P)
            x_s = X[:].rearrange("p (t d) -> p t d", d=D)
            for n in range(4):
                sp.dma_start(x_s[:, n * 8:(n + 1) * 8, :], x_d[:, n * 8:(n + 1) * 8, :]).then_inc(x_in, 16)

        def load_expert(sp, n, done):
            sp.dma_start(gate_up[:, n * GU:(n + 1) * GU], a["gate_up"][:, n * GU:(n + 1) * GU]).then_inc(done, 16)
            body = down[:, n * NC * D:(n + 1) * NC * D]
            sp.dma_start(body[:, 0:(NC - 1) * D], a["down"][:, n * (NC - 1) * D:(n + 1) * (NC - 1) * D]).then_inc(done, 16)
            sp.dma_start(body[0:ITAIL, (NC - 1) * D:NC * D], a["down_tail"][:, n * D:(n + 1) * D]).then_inc(done, 16)

        def load_experts(sp):
            sp.dma_start(gateT[:], a["gateT"]).then_inc(experts_in, 16)
            for dst, name in shapes:
                sp.dma_start(dst[:], a[name]).then_inc(experts_in, 16)
            for n in range(E, -1, -1):
                load_expert(sp, n, experts_in)

        lodgers_in = sem("lodgers_in")
        shapes = [(ones_tile, "ones_tile"), (all_ones, "all_ones"), (before, "before"), (earlier, "earlier"),
                  (tile_number, "tile_number"), (tile_start, "tile_start"), (token_row, "token_row")]
        EXPERTS_IN = 16 * (1 + len(shapes) + 3 * (E + 1))
        s_nobody = sem("s_nobody")

        def prefill(sp):
            sp.dma_start(nobody[:], a["nobody"]).then_inc(s_nobody, 16)
            sp.wait_ge(s_nobody, 16)
            for dst in routed:
                sp.dma_start(dst.rearrange("(t p) r -> p t r", p=P), nobody[:].bitcast(F32).unsqueeze(1).to_broadcast([P, SLOTS, ROW])).then_inc(prefilled, 16)

        def stats_dve(dve, s_stats, s_var, s_std, s_rstd):
            with dve.Fori(0, NT // 8) as m:
                for i in range(8):
                    dve.bn_stats(row_stats[:, ds(m * 8 + i, 1), :], X[:, ds(m * (8 * D) + i * D, D)]).then_inc(s_stats, 1)
            dve.wait_ge(s_stats, NT)
            dve.tensor_tensor(mean[:], row_stats[:, :, 1], row_stats[:, :, 4], ALU.add)
            dve.tensor_tensor(apart[:], row_stats[:, :, 1], row_stats[:, :, 4], ALU.subtract)
            dve.tensor_tensor(rstd[:], row_stats[:, :, 2], row_stats[:, :, 5], ALU.add).then_inc(s_stats, 1)
            dve.wait_ge(s_stats, NT + 1)
            dve.tensor_scalar(mean[:], mean[:], 0.5, None, ALU.mult)
            dve.tensor_scalar(rstd[:], rstd[:], 1.0 / D, EPS, ALU.mult, ALU.add)
            dve.scalar_tensor_tensor(apart[:], apart[:], 0.25, apart[:], ALU.mult, ALU.mult).then_inc(s_stats, 1)
            dve.wait_ge(s_stats, NT + 2)
            dve.tensor_tensor(rstd[:], rstd[:], apart[:], ALU.add).then_inc(s_var, 1)
            dve.wait_ge(s_std, 1)
            dve.reciprocal(rstd[:], rstd[:]).then_inc(s_rstd, 1)
            dve.wait_ge(s_rstd, 1)

        def stats_act(act, s_var, s_std):
            act.wait_ge(s_var, 1)
            act.activation(rstd[:], rstd[:], ACT.Sqrt).then_inc(s_std, 1)

        def layernorm(dve, dst, t):
            return dve.tensor_scalar(dst, X[:, ds(t * D, D)], mean[:, ds(t, 1)], rstd[:, ds(t, 1)], ALU.subtract, ALU.mult)

        def attention():
            scope = ExitStack()
            with scope:
                def tb(name, shape, dt=F32):
                    return sb(name, shape, dt, scope)

                def ts(name):
                    return sem("at_" + name, scope)

                wqkvT = tb("wqkvT", [P, 3 * D])
                woT = tb("woT", [P, D])
                bqkv = tb("bqkv", [P, 3])
                bq = tb("bq", [P, 1])
                bo = tb("bo", [1, D])
                ones = tb("ones", [1, P])
                own_head = tb("own_head", [P, HG, 32])
                mask = tb("mask", [P, 2, NW * KW])
                xn = tb("xn", [P, 2, D])
                xnT = tb("xnT", [P, B, 32 + P])
                qT = tb("qT", [P, 2, P])
                kT = tb("kT", [P, B, 32 + P])
                q_spread = tb("q_spread", [P, 2, NW, HG, 32])
                v = tb("v", [P, B, 2, D])
                sc = tb("sc", [P, NG, NW, KW])
                probs = tb("probs", [P, 2, NG, NW, KW])
                top = tb("top", [P, 16])
                total = tb("total", [P, 16])
                inv = tb("inv", [P, 16])
                probsT = tb("probsT", [P, 2, NG * P])
                own = tb("own", [P, 2, 2, HG, 32])
                ysum = tb("ysum", [P, P])
                yT = tb("yT", [P, P])

                score_ps = scope.enter_context(nc.psum_tensor("score_ps", [P, NG, SEG], F32))
                turn_ps = scope.enter_context(nc.psum_tensor("turn_ps", [P, NG, P], F32))
                pv_ps = scope.enter_context(nc.psum_tensor("pv_ps", [P, 2, SEG], F32))
                qkv_ps = scope.enter_context(nc.psum_tensor("qkv_ps", [P, SEG], F32))

                s_stats, s_var, s_std, s_rstd = ts("stats"), ts("var"), ts("std"), ts("rstd")
                s_zero, s_bq = ts("zeroed"), ts("bq")
                s_ln, s_x_turned, s_xnT, s_hist = ts("ln"), ts("x_turned"), ts("xnT"), ts("hist")
                s_qkv, s_qk, s_kh, s_v, s_spread = ts("qkv"), ts("qk_copied"), ts("k_hist"), ts("v_copied"), ts("spread")
                s_score, s_mask, s_top, s_sub, s_exp = ts("score"), ts("masked"), ts("top"), ts("sub"), ts("exp")
                s_total, s_inv, s_probs = ts("total"), ts("inv"), ts("probs")
                s_turn, s_turned, s_pv = ts("turn"), ts("turned"), ts("pv")
                s_own, s_ysum, s_yT, s_wo, s_x = ts("own"), ts("ysum"), ts("yT"), ts("wo"), ts("x")

                small = [(ident[:], "ident"), (wqkvT[:], "wqkvT"), (woT[:], "woT"), (bqkv[:], "bqkv"), (bo[:], "bo"),
                         (own_head[:].rearrange("p h q -> p (h q)"), "own_head"),
                         (mask[:].rearrange("p f k -> p (f k)"), "mask"), (ones[:], "ones_row")]
                SMALL = 16 * len(small)

                def at(n, r):
                    return n * B + r

                def tile(n, r):
                    n, r = n + r // B, r % B
                    return r * TPB + n, r

                def run(eng_fori, body):
                    for r in range(-3, B):
                        body(0, r, False)
                    with eng_fori(1, TPB - 1) as n:
                        for r in range(B):
                            body(n, r, False)
                    for r in range(B + 1):
                        body(TPB - 1, r, True)

                def alive(n, r, last):
                    if isinstance(n, int):
                        return 0 <= n * B + r < NT
                    return True

                with nc.Block() as block:
                    @block.sync
                    def _(sp):
                        load_x(sp)
                        for dst, name in small:
                            sp.dma_start(dst, a[name]).then_inc(small_in, 16)
                        load_experts(sp)
                        prefill(sp)

                    @block.gpsimd
                    def _(pool):
                        pool.wait_ge(small_in, SMALL)
                        def body(n, r, last):
                            if alive(n, r + 1, last):
                                t = at(n, r + 1)
                                pool.wait_ge(s_top, t + 1)
                                pool.tensor_tensor(sc[:].rearrange("p g w k -> p (g w) k"), sc[:].rearrange("p g w k -> p (g w) k"),
                                                   top[:, :].unsqueeze(2).to_broadcast([P, 16, KW]), ALU.subtract).then_inc(s_sub, 1)
                            if alive(n, r + 2, last):
                                t = at(n, r + 2)
                                s = r % 2
                                pool.wait_ge(s_qk, t + 1)
                                wait(pool, s_score, t - 1)
                                pool.tensor_tensor(q_spread[:, s], qT[:, s, :].rearrange("p (w q) -> p w q", w=NW).unsqueeze(2).to_broadcast([P, NW, HG, 32]),
                                                   own_head[:].unsqueeze(1).to_broadcast([P, NW, HG, 32]), ALU.mult).then_inc(s_spread, 1)
                            if alive(n, r + 1, last):
                                t = at(n, r + 1)
                                s = (r + 1) % 2
                                pool.wait_ge(s_inv, t + 1)
                                pr = probs[:, s].rearrange("p g w k -> p (g w) k")
                                pool.tensor_tensor(pr, pr, inv[:, :].unsqueeze(2).to_broadcast([P, 16, KW]), ALU.mult).then_inc(s_probs, 1)
                        run(pool.Fori, body)

                    @block.scalar
                    def _(act):
                        act.wait_ge(small_in, SMALL)
                        act.mul(bq[:], bqkv[:, 0:1], HD ** -0.5).then_inc(s_bq, 1)
                        stats_act(act, s_var, s_std)
                        act.wait_ge(s_bq, 1)
                        act.wait_ge(s_zero, 1)
                        def body(n, r, last):
                            if alive(n, r + 2, last):
                                t = at(n, r + 2)
                                b = (r + 2) % B
                                act.wait_ge(s_x_turned, t + 1)
                                if not (isinstance(t, int) and t < B):
                                    act.activation(xnT[:, b, 0:32], xnT[:, b, P:P + 32], ACT.Copy).then_inc(s_hist, 1)
                                    act.wait_ge(s_hist, t + 1 - B)
                                act.activation(xnT[:, b, 32:32 + P], qkv_ps[:, 0:P], ACT.Copy).then_inc(s_xnT, 1)
                            if alive(n, r, last):
                                t = at(n, r)
                                act.wait_ge(s_turn, 2 * t + 1)
                                wait(act, s_pv, t)
                                act.activation(probsT[:, 0, :], turn_ps[:].rearrange("p g q -> p (g q)"), ACT.Copy).then_inc(s_turned, 1)
                            if alive(n, r + 2, last):
                                t = at(n, r + 2)
                                b = (r + 2) % B
                                s = r % 2
                                act.wait_ge(s_qkv, t + 1)
                                wait(act, s_spread, t - 1)
                                act.activation(qT[:, s, :], qkv_ps[:, 0:P], ACT.Identity, bias=bq[:], scale=HD ** -0.5)
                                wait(act, s_score, t - B + 1)
                                if not (isinstance(t, int) and t < B):
                                    act.activation(kT[:, b, 0:32], kT[:, b, P:P + 32], ACT.Copy).then_inc(s_kh, 1)
                                    act.wait_ge(s_kh, t + 1 - B)
                                act.activation(kT[:, b, 32:32 + P], qkv_ps[:, P:2 * P], ACT.Identity, bias=bqkv[:, 1:2])
                                wait(act, s_pv, t - B + 1)
                                act.activation(v[:, b].rearrange("p a d -> p (a d)"), qkv_ps[:, 2 * P:4 * P], ACT.Copy).then_inc(s_qk, 1)
                            if alive(n, r, last):
                                t = at(n, r)
                                act.wait_ge(s_turn, 2 * t + 2)
                                act.activation(probsT[:, 1, :], turn_ps[:].rearrange("p g q -> p (g q)"), ACT.Copy).then_inc(s_turned, 1)
                            if alive(n, r + 1, last):
                                t = at(n, r + 1)
                                s = (r + 1) % 2
                                act.wait_ge(s_sub, t + 1)
                                wait(act, s_turn, 2 * (t - 1))
                                act.activation(probs[:, s].rearrange("p g w k -> p (g w k)"), sc[:].rearrange("p g w k -> p (g w k)"), ACT.Exp).then_inc(s_exp, 1)
                        run(act.Fori, body)

                    @block.vector
                    def _(dve):
                        dve.memset(xnT[:], 0.0)
                        dve.memset(kT[:], 0.0).then_inc(s_zero, 1)
                        dve.wait_ge(x_in, 64)
                        stats_dve(dve, s_stats, s_var, s_std, s_rstd)
                        dve.wait_ge(small_in, SMALL)
                        def body(n, r, last):
                            if alive(n, r - 1, last):
                                t = at(n, r - 1)
                                dve.wait_ge(s_pv, t + 1)
                                dve.tensor_tensor(own[:].rearrange("p a b h q -> p a b (h q)"),
                                                  pv_ps[:, :, 0:2 * P].rearrange("p a (b c) -> p a b c", b=2),
                                                  own_head[:].rearrange("p h q -> p (h q)").unsqueeze(1).unsqueeze(1).to_broadcast([P, 2, 2, P]),
                                                  ALU.mult).then_inc(s_own, 1)
                            if alive(n, r + 1, last):
                                t = at(n, r + 1)
                                first = isinstance(t, int) and t < B
                                dve.wait_ge(s_score, t + 1)
                                wait(dve, s_exp, t)
                                dve.tensor_tensor(sc[:].rearrange("p g w k -> p g (w k)"), score_ps[:, :, 0:NW * KW],
                                                  mask[:, int(first), :].unsqueeze(1).to_broadcast([P, NG, NW * KW]), ALU.add).then_inc(s_mask, 1)
                            if alive(n, r - 1, last):
                                t = at(n, r - 1)
                                dve.wait_ge(s_own, t + 1)
                                dve.tensor_reduce(ysum[:].rearrange("p (b a q) -> p a b q", b=2, a=2), own[:].rearrange("p a b h q -> p a b q h"),
                                                  AX.X, ALU.add).then_inc(s_ysum, 1)
                            if alive(n, r + 1, last):
                                t = at(n, r + 1)
                                dve.wait_ge(s_mask, t + 1)
                                wait(dve, s_sub, t)
                                dve.tensor_reduce(top[:], sc[:].rearrange("p g w k -> p (g w) k"), AX.X, ALU.max).then_inc(s_top, 1)
                            if alive(n, r - 1, last):
                                t = at(n, r - 1)
                                dve.wait_ge(s_ysum, t + 1)
                                wait(dve, s_wo, t)
                                dve.tensor_scalar(yT[:], ysum[:], bqkv[:, 2:3], None, ALU.add).then_inc(s_yT, 1)
                            if alive(n, r + 3, last):
                                t = at(n, r + 3)
                                wait(dve, s_x_turned, t - 1)
                                layernorm(dve, xn[:, (r + 3) % 2, :], tile(n, r + 3)[0]).then_inc(s_ln, 1)
                            if alive(n, r - 1, last):
                                t = at(n, r - 1)
                                j = tile(n, r - 1)[0]
                                dve.wait_ge(s_wo, t + 1)
                                dve.tensor_tensor(X[:, ds(j * D, D)], X[:, ds(j * D, D)], qkv_ps[:, 0:D], ALU.add).then_inc(s_x, 1)
                            if alive(n, r + 1, last):
                                t = at(n, r + 1)
                                s = (r + 1) % 2
                                dve.wait_ge(s_exp, t + 1)
                                dve.tensor_reduce(total[:], probs[:, s].rearrange("p g w k -> p (g w) k"), AX.X, ALU.add).then_inc(s_total, 1)
                                dve.wait_ge(s_total, t + 1)
                                wait(dve, s_probs, t)
                                dve.reciprocal(inv[:], total[:]).then_inc(s_inv, 1)
                        run(dve.Fori, body)

                    @block.tensor
                    def _(pe):
                        pe.wait_ge(small_in, SMALL)

                        def products(t, s, r, p):
                            for g in range(NG):
                                for w in range(2):
                                    mm = pe.matmul(pv_ps[32 * g:32 * g + 32, w, p * P:(p + 1) * P], v[64 * w:64 * w + 64, r % B, p, 32 * g:32 * g + 32],
                                                   probsT[64 * w:64 * w + 64, p, g * P:(g + 1) * P], start=True, stop=True)
                            return mm

                        def body(n, r, last):
                            if alive(n, r + 1, last):
                                t = at(n, r + 1)
                                s, b = (r + 1) % 2, (r + 1) % B
                                pe.wait_ge(s_spread, t + 1)
                                wait(pe, s_mask, t)
                                for w in range(NW):
                                    for g in range(NG):
                                        mm = pe.matmul(score_ps[:, g, w * KW:(w + 1) * KW], q_spread[32 * g:32 * g + 32, s, w].rearrange("p h q -> p (h q)"),
                                                       kT[32 * g:32 * g + 32, b, 32 * w:32 * w + KW], start=True, stop=True)
                                mm.then_inc(s_score, 1)
                            if alive(n, r + 2, last):
                                t = at(n, r + 2)
                                pe.wait_ge(s_ln, t + 1)
                                wait(pe, s_x, t - 3)
                                wait(pe, s_qk, t)
                                pe.transpose(qkv_ps[:, 0:P], xn[:, r % 2, :], ident[:]).then_inc(s_x_turned, 1)
                            if alive(n, r, last):
                                t = at(n, r)
                                s = r % 2
                                pe.wait_ge(s_probs, t + 1)
                                wait(pe, s_turned, 2 * t)
                                for g in range(NG):
                                    mm = pe.transpose(turn_ps[:, g, :], probs[:, s, g, 0:2, :].rearrange("p w k -> p (w k)"), ident[:])
                                mm.then_inc(s_turn, 1)
                            if alive(n, r + 2, last):
                                t = at(n, r + 2)
                                b = (r + 2) % B
                                pe.wait_ge(s_xnT, t + 1)
                                pe.matmul(qkv_ps[:, 0:P], wqkvT[:, 0:D], xnT[:, b, 32:32 + P], start=True, stop=True)
                                pe.matmul(qkv_ps[:, P:2 * P], wqkvT[:, D:2 * D], xnT[:, b, 32:32 + P], start=True, stop=True)
                                for p in range(2):
                                    for w in range(2):
                                        c = 32 * (2 * p + w)
                                        mm = pe.matmul(qkv_ps[64 * w:64 * w + 64, (2 + p) * P:(3 + p) * P], xnT[:, b, c:c + KW], wqkvT[:, 2 * D:3 * D], start=True, stop=True)
                                mm.then_inc(s_qkv, 1)
                            if alive(n, r, last):
                                t = at(n, r)
                                s = r % 2
                                wait(pe, s_own, t)
                                pe.wait_ge(s_turned, 2 * t + 1)
                                for g in range(NG):
                                    mm = pe.transpose(turn_ps[:, g, :], probs[:, s, g, 2:4, :].rearrange("p w k -> p (w k)"), ident[:])
                                mm.then_inc(s_turn, 1)
                                products(t, s, r, 0)
                            if alive(n, r - 1, last):
                                t = at(n, r - 1)
                                pe.wait_ge(s_yT, t + 1)
                                wait(pe, s_x, t)
                                if alive(n, r + 2, last):
                                    pe.wait_ge(s_qk, at(n, r + 2) + 1)
                                if alive(n, r, last):
                                    pe.wait_ge(s_turned, 2 * at(n, r) + 2)
                                pe.matmul(qkv_ps[:, 0:D], yT[:], woT[:], start=True, stop=False)
                                pe.matmul(qkv_ps[:, 0:D], ones[:], bo[:], start=False, stop=True).then_inc(s_wo, 1)
                            if alive(n, r, last):
                                t = at(n, r)
                                if isinstance(t, int) and t == 0:
                                    pe.wait_ge(s_turned, 2)
                                products(t, r % 2, r, 1).then_inc(s_pv, 1)
                        run(pe.Fori, body)

        def ffn(n):
            scope = ExitStack()
            with scope:
                def tb(name, shape, dt=F32):
                    return sb(f"f{n}_" + name, shape, dt, scope)

                def ts(name):
                    return sem(f"f{n}_" + name, scope)

                def pb(name, shape):
                    return inner.enter_context(nc.psum_tensor(f"f{n}_" + name, shape, F32))

                rows = tb("rows", [P, NT * D])
                cols = tb("cols", [P, NT * P])
                logits = tb("logits", [P, NT, E])
                G0, G1 = rows, cols

                inner = ExitStack()
                with inner:
                    xn = sb(f"f{n}_xn", [P, 2, D], F32, inner)
                    xT = sb(f"f{n}_xTr", [P, 2, P], F32, inner)
                    turn_ps = pb("rturn_ps", [P, 2, SEG])
                    s_stats, s_var, s_std, s_rstd = ts("stats"), ts("var"), ts("std"), ts("rstd")
                    s_ln, s_turn, s_xT, s_rows, s_cols, s_logit, s_logit_out = (ts(x) for x in ("ln", "rturn", "rxT", "rows", "cols", "logit", "logit_out"))

                    def by_two(fori, body):
                        body(0, 0), body(1, 1)
                        with fori(1, NT // 2) as m:
                            body(m * 2, 0), body(m * 2 + 1, 1)
                        body(NT, 0)

                    with nc.Block() as block:
                        @block.vector
                        def _(dve):
                            stats_dve(dve, s_stats, s_var, s_std, s_rstd)
                            def body(t, s):
                                if isinstance(t, int) and t == NT:
                                    return
                                wait(dve, s_turn, t - 1)
                                wait(dve, s_rows, t - 1)
                                layernorm(dve, xn[:, s, :], t).then_inc(s_ln, 1)
                            by_two(dve.Fori, body)

                        @block.tensor
                        def _(pe):
                            pe.wait_ge(experts_in, EXPERTS_IN)
                            def body(t, s):
                                if not (isinstance(t, int) and t == NT):
                                    wait(pe, s_logit_out, t - 1)
                                    pe.wait_ge(s_ln, t + 1)
                                    pe.transpose(turn_ps[:, s, 0:P], xn[:, s, :], ident[:]).then_inc(s_turn, 1)
                                if not (isinstance(t, int) and t == 0):
                                    pe.wait_ge(s_xT, t)
                                    pe.matmul(turn_ps[:, 1 - s, P:P + E], xT[:, 1 - s, :], gateT[:], start=True, stop=True).then_inc(s_logit, 1)
                            by_two(pe.Fori, body)

                        @block.scalar
                        def _(act):
                            stats_act(act, s_var, s_std)
                            def body(t, s):
                                if not (isinstance(t, int) and t == NT):
                                    wait(act, s_logit, t - 1)
                                    wait(act, s_cols, t - 1)
                                    act.wait_ge(s_turn, t + 1)
                                    act.activation(xT[:, s, :], turn_ps[:, s, 0:P], ACT.Copy).then_inc(s_xT, 1)
                                if not (isinstance(t, int) and t == 0):
                                    act.wait_ge(s_logit, t)
                                    act.activation(logits[:, ds(t - 1, 1), :], turn_ps[:, 1 - s, P:P + E], ACT.Copy).then_inc(s_logit_out, 1)
                            by_two(act.Fori, body)

                        @block.sync
                        def _(sp):
                            if n and "mamba" in phases:
                                for e in range(E - LODGERS, E):
                                    load_expert(sp, e, lodgers_in)

                        @block.gpsimd
                        def _(pool):
                            def body(t, s):
                                if isinstance(t, int) and t == NT:
                                    return
                                pool.wait_ge(s_ln, t + 1)
                                pool.tensor_copy(rows[:, ds(t * D, D)], xn[:, s, :]).then_inc(s_rows, 1)
                                pool.wait_ge(s_xT, t + 1)
                                pool.tensor_copy(cols[:, ds(t * P, P)], xT[:, s, :]).then_inc(s_cols, 1)
                            by_two(pool.Fori, body)

                inner = ExitStack()
                with inner:
                    def tb(name, shape, dt=F32):
                        return sb(f"f{n}_" + name, shape, dt, inner)

                    probs = tb("probs", [P, NT, E])
                    red = tb("red", [P, NT])
                    above = tb("above", [P, NT, E * E])
                    equal = tb("equal", [P, NT, E * E])
                    rank = tb("rank", [P, NT, E])
                    first = tb("first", [P, NT, E])
                    second = tb("second", [P, NT, E])
                    taken = tb("taken", [P, NT, E])
                    share = tb("share", [P, NT, E])
                    w0 = tb("w0", [P, NT])
                    w1 = tb("w1", [P, NT])
                    sums = tb("sums", [P, NT, E])
                    upto = tb("upto", [P, NT, E])
                    place = tb("place", [P, NT, E])
                    picked = tb("picked", [P, NT, E])
                    tiles = tb("tiles", [P, E])
                    ends = tb("ends", [P, E])
                    base = tb("base", [P, E])
                    place_f = tb("place_f", [P, 2, NT])
                    place_i = tb("place_i", [P, 2, NT], I32)
                    expert_f = tb("expert_f", [P, SLOTS])
                    gu_at = tb("gu_at", [P, SLOTS], I32)
                    down_at = tb("down_at", [P, SLOTS], I32)
                    send = tb("send", [P, 2, ROW])
                    send_to = tb("send_to", [P, 2], I32)
                    xin = tb("xin", [P, 2, ROW])
                    back = tb("back", [P, 2], I32)
                    back_to = tb("back_to", [P, 2], I32)
                    xT = tb("xT", [P, 2, P])
                    gated = tb("gated", [P, I])
                    inner_h = tb("inner_h", [P, I])
                    hTA = tb("hTA", [P, 2, CA * P])
                    hTB = tb("hTB", [P, CB * P])
                    yout = tb("yout", [P, 2, D])
                    up_ps = pb("up_ps", [P, 4, SEG])
                    ta_ps, tb_ps, xt_ps, y_ps = (pb(x, [P, SEG]) for x in ("ta_ps", "tb_ps", "xt_ps", "y_ps"))

                    s_r, s_shift, s_rexp, s_taken, s_count, s_route = (ts(x) for x in ("r", "shift", "rexp", "taken", "count", "route"))
                    s_send, s_sent = ts("send"), [ts("sent0"), ts("sent1")]
                    s_xin, s_tx, s_xT2 = [ts("xin0"), ts("xin1")], ts("tx"), ts("xT")
                    s_upA, s_upB, s_gA, s_gB, s_hA, s_hB = (ts(x) for x in ("upA", "upB", "gA", "gB", "hA", "hB"))
                    s_tA, s_tB, s_cA, s_cB, s_down, s_y = (ts(x) for x in ("tA", "tB", "cA", "cB", "down", "y"))
                    s_back, s_home, s_g = ts("back"), [ts("home0"), ts("home1")], [ts(f"g{c}") for c in range(4)]

                    STEPS = NT + SLOTS

                    def run(fori, body):
                        def pair(m, kind):
                            for s in range(2):
                                body(m * 2 + s, s, kind)
                        pair(0, None)
                        with fori(1, NT // 2 - 1) as m:
                            pair(m, "shared")
                        pair(NT // 2 - 1, None)
                        pair(NT // 2, None)
                        pair(NT // 2 + 1, None)
                        with fori(NT // 2 + 2, STEPS // 2 - 1) as m:
                            pair(m, "routed")
                        pair(STEPS // 2 - 1, None)
                        body(STEPS, 0, None)

                    def is_routed(t, kind):
                        return t >= NT if isinstance(t, int) else kind == "routed"

                    def exists(t):
                        return not isinstance(t, int) or 0 <= t < STEPS

                    with nc.Block() as block:
                        @block.vector
                        def _(dve):
                            count = [0]

                            def own(ins):
                                count[0] += 1
                                ins.then_inc(s_r, 1)
                                dve.wait_ge(s_r, count[0])

                            def per_token(x):
                                return x.unsqueeze(2).to_broadcast([P, NT, E])

                            own(dve.tensor_reduce(red[:], logits[:], AX.X, ALU.max))
                            dve.tensor_tensor(probs[:], logits[:], per_token(red[:]), ALU.subtract).then_inc(s_shift, 1)
                            dve.wait_ge(s_rexp, 1)
                            own(dve.tensor_reduce(red[:], probs[:], AX.X, ALU.add))
                            own(dve.reciprocal(red[:], red[:]))
                            own(dve.tensor_tensor(probs[:], probs[:], per_token(red[:]), ALU.mult))
                            them = probs[:].unsqueeze(2).to_broadcast([P, NT, E, E])
                            it = probs[:].unsqueeze(3).to_broadcast([P, NT, E, E])
                            four = lambda x: x[:].rearrange("p t (e f) -> p t e f", e=E)
                            dve.tensor_tensor(four(above), them, it, ALU.is_gt)
                            own(dve.tensor_tensor(four(equal), them, it, ALU.is_equal))
                            own(dve.tensor_tensor(equal[:], equal[:], earlier[:].unsqueeze(1).to_broadcast([P, NT, E * E]), ALU.mult))
                            own(dve.tensor_tensor(above[:], above[:], equal[:], ALU.add))
                            own(dve.tensor_reduce(rank[:], four(above), AX.X, ALU.add))
                            dve.tensor_scalar(taken[:], rank[:], 1.5, None, ALU.is_lt).then_inc(s_taken, 1)
                            dve.tensor_scalar(first[:], rank[:], 0.0, None, ALU.is_equal)
                            own(dve.tensor_scalar(second[:], rank[:], 1.0, None, ALU.is_equal))
                            own(dve.tensor_tensor(share[:], taken[:], probs[:], ALU.mult))
                            own(dve.tensor_reduce(red[:], share[:], AX.X, ALU.add))
                            own(dve.tensor_scalar(red[:], red[:], 1e-8, None, ALU.add))
                            own(dve.reciprocal(red[:], red[:]))
                            own(dve.tensor_tensor(share[:], share[:], per_token(red[:]), ALU.mult))
                            own(dve.tensor_tensor(picked[:], first[:], share[:], ALU.mult))
                            own(dve.tensor_reduce(w0[:], picked[:], AX.X, ALU.add))
                            own(dve.tensor_tensor(picked[:], second[:], share[:], ALU.mult))
                            own(dve.tensor_reduce(w1[:], picked[:], AX.X, ALU.add))
                            dve.wait_ge(s_count, 1)
                            count_ps = y_ps[:].rearrange("p (k t e) -> p k t e", k=2, e=E)
                            own(dve.tensor_copy(sums[:], count_ps[:, 1]))
                            for e in range(E):
                                ins = dve.tensor_tensor_scan(upto[:, :, e], ones_tile[:], sums[:, :, e], 0.0, ALU.mult, ALU.add)
                            own(ins)
                            counted = above[:].rearrange("p t f -> p (t f)")[:, 0:E * NT].rearrange("p (e t) -> p e t", e=E)
                            own(dve.tensor_tensor(counted, upto[:, NT - 1, :].unsqueeze(2).to_broadcast([P, E, NT]),
                                                  tile_start[:, 0:NT].unsqueeze(1).to_broadcast([P, E, NT]), ALU.is_gt))
                            own(dve.tensor_reduce(tiles[:], counted, AX.X, ALU.add))
                            own(dve.tensor_tensor_scan(ends[:], ones_tile[:, 0:E], tiles[:], 0.0, ALU.mult, ALU.add))
                            own(dve.tensor_tensor(base[:], ends[:], tiles[:], ALU.subtract))
                            own(dve.tensor_scalar(base[:], base[:], float(P), None, ALU.mult))
                            own(dve.tensor_tensor(place[:], upto[:], sums[:], ALU.subtract))
                            own(dve.tensor_tensor(place[:], place[:], count_ps[:, 0], ALU.add))
                            own(dve.tensor_tensor(place[:], place[:], base[:].unsqueeze(1).to_broadcast([P, NT, E]), ALU.add))
                            own(dve.tensor_tensor(picked[:], first[:], place[:], ALU.mult))
                            own(dve.tensor_reduce(place_f[:, 0, :], picked[:], AX.X, ALU.add))
                            own(dve.tensor_tensor(picked[:], second[:], place[:], ALU.mult))
                            own(dve.tensor_reduce(place_f[:, 1, :], picked[:], AX.X, ALU.add))
                            dve.tensor_copy(place_i[:], place_f[:])
                            ended = equal[:].rearrange("p t f -> p (t f)")[:, 0:SLOTS * E].rearrange("p (t e) -> p t e", e=E)
                            own(dve.tensor_tensor(ended, ends[:].unsqueeze(1).to_broadcast([P, SLOTS, E]),
                                                  tile_number[:].unsqueeze(2).to_broadcast([P, SLOTS, E]), ALU.is_le))
                            own(dve.tensor_reduce(expert_f[:], ended, AX.X, ALU.add))
                            own(dve.tensor_scalar(expert_f[:], expert_f[:], float(E - 1), None, ALU.min))
                            dve.tensor_scalar(gu_at[:], expert_f[:], float(GU), None, ALU.mult)
                            dve.tensor_scalar(down_at[:], expert_f[:], float(NC * D), None, ALU.mult).then_inc(s_route, 1)

                            def body(t, s, kind):
                                if exists(t):
                                    wait(dve, s_tA, t)
                                    dve.wait_ge(s_gA, t + 1)
                                    dve.tensor_tensor(inner_h[:, 0:IA], gated[:, 0:IA], up_ps[:, 1, 0:IA], ALU.mult).then_inc(s_hA, 1)
                                    if is_routed(t, kind):
                                        k = t - NT
                                        dve.wait_ge(s_xin[s], (k - s) * 8 + 16)
                                        wait(dve, s_y, t - 1)
                                        dve.tensor_copy(back[:, s:s + 1], xin[:, s, D:ROW].bitcast(I32)).then_inc(s_back, 1)
                                    wait(dve, s_tB, t)
                                    dve.wait_ge(s_gB, t + 1)
                                    dve.tensor_tensor(inner_h[:, IA:I], gated[:, IA:I], up_ps[:, 3, 0:IB], ALU.mult).then_inc(s_hB, 1)
                                if exists(t - 1):
                                    if not is_routed(t - 1, kind):
                                        dve.wait_ge(s_down, t)
                                        dve.tensor_tensor(X[:, ds((t - 1) * D, D)], X[:, ds((t - 1) * D, D)], y_ps[:, 0:D], ALU.add).then_inc(s_y, 1)
                                    else:
                                        k = t - 1 - NT
                                        wait(dve, s_home[1 - s], (k - (1 - s)) * 8)
                                        dve.wait_ge(s_back, k + 1)
                                        dve.tensor_copy(back_to[:, 1 - s:2 - s], back[:, 1 - s:2 - s])
                                        dve.wait_ge(s_down, t)
                                        dve.tensor_copy(yout[:, 1 - s, :], y_ps[:, 0:D]).then_inc(s_y, 1)
                            run(dve.Fori, body)

                            for c in range(4):
                                dve.wait_ge(s_g[c], 32)
                                with dve.Fori(c * NT // 4, (c + 1) * NT // 4) as j:
                                    for g, w in ((G0, w0), (G1, w1)):
                                        dve.scalar_tensor_tensor(X[:, ds(j * D, D)], g[:, ds(j * D, D)], w[:, ds(j, 1)], X[:, ds(j * D, D)],
                                                                 ALU.mult, ALU.add).then_inc(s_r, 1)
                                        dve.wait_ge(s_r, count[0] + j * 2 + (1 if g is G0 else 2))

                        @block.scalar
                        def _(act):
                            act.wait_ge(s_shift, 1)
                            act.activation(probs[:], probs[:], ACT.Exp).then_inc(s_rexp, 1)
                            act.activation(xT[:, 0, :], cols[:, 0:P], ACT.Copy).then_inc(s_xT2, 1)

                            def body(t, s, kind):
                                if exists(t):
                                    wait(act, s_hA, t)
                                    act.wait_ge(s_upA, t + 1)
                                    act.activation(gated[:, 0:IA], up_ps[:, 0, 0:IA], ACT.Silu).then_inc(s_gA, 1)
                                if exists(t - 1):
                                    act.wait_ge(s_tB, t)
                                    act.activation(hTB[:, 0:(CB - 1) * P], tb_ps[:, 0:(CB - 1) * P], ACT.Copy)
                                    act.activation(hTB[0:ITAIL, (CB - 1) * P:CB * P], tb_ps[0:ITAIL, (CB - 1) * P:CB * P], ACT.Copy).then_inc(s_cB, 1)
                                if exists(t):
                                    wait(act, s_hB, t)
                                    act.wait_ge(s_upB, t + 1)
                                    act.activation(gated[:, IA:I], up_ps[:, 2, 0:IB], ACT.Silu).then_inc(s_gB, 1)
                                if exists(t + 1):
                                    if is_routed(t + 1, kind):
                                        act.wait_ge(s_tx, t + 2 - NT)
                                        src = xt_ps[:, 0:P]
                                    else:
                                        src = cols[:, ds((t + 1) * P, P)]
                                    if exists(t):
                                        act.activation(xT[:, 1 - s, :], src, ACT.Copy).then_inc(s_xT2, 1)
                                if exists(t):
                                    act.wait_ge(s_tA, t + 1)
                                    act.activation(hTA[:, s, :], ta_ps[:], ACT.Copy).then_inc(s_cA, 1)
                            run(act.Fori, body)

                        @block.tensor
                        def _(pe):
                            pe.wait_ge(s_taken, 1)
                            pe.matmul(y_ps[:, 0:NT * E], before[:], taken[:].rearrange("p t e -> p (t e)"), start=True, stop=True)
                            pe.matmul(y_ps[:, NT * E:2 * NT * E], all_ones[:], taken[:].rearrange("p t e -> p (t e)"), start=True, stop=True).then_inc(s_count, 1)
                            pe.wait_ge(s_route, 1)

                            def up(t, s, half, at, width, where):
                                for bank, off in ((2 * half, 0), (2 * half + 1, I)):
                                    mm = pe.matmul(up_ps[:, bank, 0:width], xT[:, s, :], gate_up[:, ds(where + (off + at), width)] if not isinstance(where, int)
                                                   else gate_up[:, where + off + at:where + off + at + width], start=True, stop=True)
                                return mm

                            def expert(table, t, kind, each):
                                if is_routed(t, kind):
                                    return pe.value_load(table[0:1, ds(t - NT, 1)], min_val=0, max_val=(E - 1) * each)
                                return E * each

                            def body(t, s, kind):
                                if n and "mamba" in phases and isinstance(t, int) and t == NT:
                                    pe.wait_ge(lodgers_in, 16 * 3 * LODGERS)
                                if exists(t):
                                    where = expert(gu_at, t, kind, GU)
                                    pe.wait_ge(s_xT2, t + 1)
                                    wait(pe, s_hA, t)
                                    up(t, s, 0, 0, IA, where).then_inc(s_upA, 1)
                                if exists(t - 1):
                                    pe.wait_ge(s_hB, t)
                                    wait(pe, s_cB, t - 1)
                                    for c in range(CB):
                                        w = P if c < CB - 1 else ITAIL
                                        mm = pe.transpose(tb_ps[0:w, c * P:(c + 1) * P], inner_h[:, IA + c * P:IA + c * P + w], ident[:])
                                    mm.then_inc(s_tB, 1)
                                if exists(t):
                                    up(t, s, 1, IA, IB, where).then_inc(s_upB, 1)
                                if exists(t + 1) and exists(t) and is_routed(t + 1, kind):
                                    k = t + 1 - NT
                                    pe.wait_ge(s_xin[1 - s], (k - (1 - s)) * 8 + 16)
                                    pe.transpose(xt_ps[:, 0:P], xin[:, 1 - s, 0:D], ident[:]).then_inc(s_tx, 1)
                                if exists(t):
                                    wait(pe, s_cA, t)
                                    pe.wait_ge(s_hA, t + 1)
                                    for c in range(CA):
                                        mm = pe.transpose(ta_ps[:, c * P:(c + 1) * P], inner_h[:, c * P:(c + 1) * P], ident[:])
                                    mm.then_inc(s_tA, 1)
                                if exists(t - 1):
                                    where = expert(down_at, t - 1, kind, NC * D)
                                    wait(pe, s_y, t - 1)
                                    pe.wait_ge(s_cB, t)
                                    pe.wait_ge(s_cA, t)
                                    for c in range(NC):
                                        w = P if c < NC - 1 else ITAIL
                                        lhs = hTA[0:w, 1 - s, c * P:(c + 1) * P] if c < CA else hTB[0:w, (c - CA) * P:(c - CA + 1) * P]
                                        rhs = down[0:w, where + c * D:where + (c + 1) * D] if isinstance(where, int) else down[0:w, ds(where + c * D, D)]
                                        mm = pe.matmul(y_ps[:, 0:D], lhs, rhs, start=(c == 0), stop=(c == NC - 1))
                                    mm.then_inc(s_down, 1)
                            run(pe.Fori, body)

                        @block.sync
                        def _(sp):
                            for q in range(2):
                                sp.wait_ge(s_sent[q], 16 * NT)
                            def load(k, s):
                                wait(sp, s_back, k - 1)
                                wait(sp, s_tx, k - 1)
                                sp.dma_start(xin[:, s, :], routed[n][ds(k * P, P), :]).then_inc(s_xin[s], 16)
                            load(0, 0), load(1, 1)
                            with sp.Fori(1, SLOTS // 2) as m:
                                load(m * 2, 0), load(m * 2 + 1, 1)
                            for q in range(2):
                                sp.wait_ge(s_home[q], 16 * SLOTS // 2)
                            for c in range(4):
                                for q, g in enumerate((G0, G1)):
                                    j = slice(c * NT // 4, (c + 1) * NT // 4)
                                    sp.dma_start(g[:].rearrange("p (t d) -> p t d", d=D)[:, j, :],
                                                 expert_out[n][q * B * T:(q + 1) * B * T, :].rearrange("(t p) d -> p t d", p=P)[:, j, :]).then_inc(s_g[c], 16)

                        @block.gpsimd
                        def _(pool):
                            copied, result, stored = (pool.alloc_register(f"f{n}_{x}") for x in ("copied", "result", "stored"))
                            pool.reg_mov(copied, 0)
                            pool.reg_mov(result, NT)
                            pool.wait_ge(s_route, 1)

                            def send_row(j, q):
                                t = j * 2 + q
                                pool.reg_add(copied, copied, 1)
                                pool.wait_ge(prefilled, 32)
                                wait(pool, s_sent[q], j * 16)
                                pool.tensor_copy(send[:, q, 0:D], rows[:, ds(j * D, D)])
                                pool.tensor_copy(send[:, q, D:ROW].bitcast(I32), token_row[:, ds(j + q * NT, 1)])
                                pool.tensor_copy(send_to[:, q:q + 1], place_i[:, q, ds(j, 1)]).then_inc(s_send, 1)
                                pool.wait_ge(s_route, 1)
                                pool.wait_ge(s_send, copied)
                                pool.indirect_dma_start(routed[n], bass.IndirectOffsetOnAxis(ap=send_to[:, q:q + 1].bitcast(U32), axis=0),
                                                        send[:, q, :], None).then_inc(s_sent[q], 16)
                            send_row(0, 0), send_row(0, 1)
                            with pool.Fori(1, NT) as j:
                                send_row(j, 0), send_row(j, 1)

                            def home(k, s):
                                pool.reg_add(result, result, 1)
                                if not isinstance(k, int):
                                    pool.reg_mov(stored, (k + s) * 8)
                                pool.wait_ge(s_route, 1)
                                pool.wait_ge(s_y, result)
                                wait(pool, s_home[1 - s], k * 16 if isinstance(k, int) else stored)
                                pool.indirect_dma_start(expert_out[n], bass.IndirectOffsetOnAxis(ap=back_to[:, s:s + 1].bitcast(U32), axis=0),
                                                        yout[:, s, :], None).then_inc(s_home[s], 16)
                            home(0, 0), home(1, 1)
                            with pool.Fori(1, SLOTS // 2) as m:
                                home(m * 2, 0), home(m * 2 + 1, 1)


        def mamba():
            scope = ExitStack()
            with scope:
                def tb(name, shape, dt=F32):
                    return sb("m_" + name, shape, dt, scope)

                def ts(name):
                    return sem("m_" + name, scope)

                C = T // SEG
                HIST = TAPS - 1
                CHUNK = HIST + SEG
                RING, DECAYS = 4, 4
                taps = tb("taps", [P, NL * HALF * TAPS])
                in_tapT = tb("in_tapT", [P, NL * HALF, TAPS, P])
                gateT_w = tb("gateT_w", [P, NL * DI])
                conv_b = tb("conv_b", [P, NL * HALF])
                x_w = tb("x_w", [P, NL * HALF, XR])
                dt_w = tb("dt_w", [XR, NL * DI])
                dt_b = tb("dt_b", [P, NL * HALF])
                decay = tb("decay", [P, NL * HALF * NS])
                skip = tb("skip", [P, NL * HALF])
                skip_diag = tb("skip_diag", [P, NL * HALF, P])
                out_w = tb("out_w", [P, NL * HALF, D])
                spread = tb("spread", [3 * 32, 2 * NS * P], BF16)
                zu = tb("zu", [P, STREAMS, 2 * HALF, SEG])
                parts = tb("parts", [3 * 32, STREAMS, SEG], BF16)
                delta = tb("delta", [P, STREAMS, HALF, SEG])
                delta_u = tb("delta_u", [P, STREAMS, HALF, SEG])
                first = tb("first", [P, STREAMS, HALF, NS])
                last = tb("last", [P, NL, STREAMS, C, HALF, NS])
                state = tb("state", [P, RING, HALF, SEG])
                z = lambda s: zu[:, 1 - s, 0:HALF, :]
                u = lambda s: zu[:, s, HALF:2 * HALF, :]
                spare = gate_up[:, (E - LODGERS) * GU:E * GU]
                def lodge(at, columns, rows=P):
                    return spare[0:rows, at:at + columns]
                at = 0
                xT = lodge(at, B * C * CHUNK)
                at += B * C * CHUNK
                hT = lodge(at, STREAMS * (HIST + T)).rearrange("p (s t) -> p s t", s=STREAMS)
                at += STREAMS * (HIST + T)
                c_sb = lodge(at, RING * SEG).rearrange("p (r t) -> p r t", r=RING)
                at += RING * SEG
                bc = lodge(at, SEG, XR)
                at += SEG
                rest = lodge(at, SEG, 32)
                at += SEG
                mid = lodge(at, SEG // 2, 32).bitcast(BF16)
                spare_down = down[:, (E - LODGERS) * NC * D:E * NC * D]
                seen = spare_down[:, 0:RING * HALF * SEG].rearrange("p (r h t) -> p r h t", r=RING, h=HALF)
                dA = spare_down[:, RING * HALF * SEG:(RING + DECAYS) * HALF * SEG].rearrange("p (r h t) -> p r h t", r=DECAYS, h=HALF)
                flat = state[:].rearrange("p r h t -> p (r h t)")
                in_w = flat[:, 0:NL * HALF * D]
                in_tap = flat[:, NL * HALF * D:NL * HALF * D * (1 + TAPS)].rearrange("p (a k d) -> p a k d", k=TAPS, d=D)
                xn = delta_u[:, 0]

                ps = scope.enter_context(nc.psum_tensor("m_ps", [P, 8, SEG], F32))
                Y = ps[:, 0:2, :]
                PB = ps[:, 2:4, :]
                PC = ps[:, 4, :]
                DRIVE = ps[:, 5:7, :]
                SIDE = ps[:, 7, :]

                s_w, s_set, s_zero = ts("w"), ts("set"), ts("zeroed")
                s_stats, s_var, s_std, s_rstd = ts("stats"), ts("var"), ts("std"), ts("rstd")
                s_ln, s_turn, s_tapT, s_xT, s_added = ts("ln"), ts("turn"), ts("tapT"), ts("xT"), ts("added")
                s_side, s_side_read, s_silu, s_first = ts("side"), ts("side_read"), ts("silu"), ts("first")
                s_soft, s_dt, s_dtu, s_split, s_parts = ts("soft"), ts("dt"), ts("dtu"), ts("split"), ts("parts")
                s_b, s_c, s_acc = ts("b"), ts("c"), ts("acc")
                s_drive, s_decay, s_c_sb, s_state, s_seen, s_y = ts("drive"), ts("decay"), ts("c_sb"), ts("state"), ts("seen"), ts("y")

                weights = [(in_w, "m_in"), (taps[:], "m_taps"), (gateT_w[:], "m_gateT"), (conv_b[:], "m_conv_b"),
                           (x_w[:].rearrange("p a r -> p (a r)"), "m_xT"), (dt_w[2 * NS:XR, :], "m_dtT"), (dt_b[:], "m_dt_b"),
                           (decay[:], "m_A_log"), (skip[:], "m_skip"), (out_w[:].rearrange("p a d -> p (a d)"), "m_outT"), (spread[:], "m_spread")]
                WEIGHTS = 16 * len(weights)

                def chunks(fori, body):
                    with fori(0, B // STREAMS) as p:
                        for s in range(STREAMS):
                            for c in range(C):
                                body(p * (STREAMS * C) + s * C + c, (s * C + c) % 2, s, c, p * C + c)

                with nc.Block() as block:
                    @block.sync
                    def _(sp):
                        for dst, name in weights:
                            sp.dma_start(dst, a[name]).then_inc(s_w, 16)

                    @block.vector
                    def _(dve):
                        dve.memset(xT.rearrange("p (q t) -> p q t", t=CHUNK)[:, :, 0:HIST], 0.0)
                        dve.memset(hT[:, :, 0:HIST], 0.0)
                        dve.memset(last[:], 0.0).then_inc(s_zero, 1)
                        stats_dve(dve, s_stats, s_var, s_std, s_rstd)
                        def body(j, r, s, c, q):
                            dve.wait_ge(s_turn, j + 1)
                            dve.wait_ge(s_added, j + 1)
                            for i in range(SEG // P):
                                ins = dve.tensor_scalar(xn[:, r, i * P:(i + 1) * P], X[:, ds(j * SEG + i * P, P)], mean[:, ds(j * (SEG // P) + i, 1)],
                                                        rstd[:, ds(j * (SEG // P) + i, 1)], ALU.subtract, ALU.mult)
                            ins.then_inc(s_ln, 1)
                        chunks(dve.Fori, body)
                        dve.wait_ge(s_w, WEIGHTS)
                        for lh in range(NL * HALF):
                            for k in range(TAPS):
                                dve.tensor_scalar(in_tap[:, lh, k, :], in_w[:, lh * D:(lh + 1) * D], taps[:, lh * TAPS + k:lh * TAPS + k + 1], None, ALU.mult)
                            dve.tensor_scalar(skip_diag[:, lh, :], ident[:], skip[:, lh:lh + 1], None, ALU.mult).then_inc(s_set, 1)
                        dve.wait_ge(s_var, 2)
                        dve.tensor_scalar(decay[:], decay[:], -1.0, None, ALU.mult)

                    @block.scalar
                    def _(act):
                        act.sem_inc(s_xT, 2)
                        stats_act(act, s_var, s_std)
                        act.wait_ge(s_zero, 1)
                        def body(j, r, s, c, q):
                            act.wait_ge(s_turn, j + 3)
                            ins = act.activation(xT[:, ds(q * CHUNK + (s * B * CHUNK + HIST), SEG)], ps[:, 4 + r, :], ACT.Copy)
                            if c < C - 1:
                                ins = act.activation(xT[:, ds(q * CHUNK + (s * B + 1) * CHUNK, HIST)], ps[:, 4 + r, SEG - HIST:SEG], ACT.Copy)
                            ins.then_inc(s_xT, 1)
                        chunks(act.Fori, body)
                        act.wait_ge(s_w, WEIGHTS)
                        act.activation(decay[:], decay[:], ACT.Exp).then_inc(s_var, 1)
                        for lh in range(NL * HALF):
                            act.wait_ge(s_tapT, lh + 1)
                            act.activation(in_tapT[:, lh].rearrange("p k d -> p (k d)"), ps[:, lh, :], ACT.Copy)

                    @block.gpsimd
                    def _(pool):
                        pool.sem_inc(s_added, 2)
                        def body(j, r, s, c, q):
                            pool.wait_ge(s_ln, j + 1)
                            pool.tensor_tensor(X[:, ds(j * SEG, SEG)], X[:, ds(j * SEG, SEG)], xn[:, r, :], ALU.add).then_inc(s_added, 1)
                        chunks(pool.Fori, body)

                    @block.tensor
                    def _(pe):
                        pe.sem_inc(s_turn, 2)
                        def body(j, r, s, c, q):
                            pe.wait_ge(s_xT, j + 1)
                            pe.wait_ge(s_ln, j + 1)
                            for i in range(SEG // P):
                                mm = pe.transpose(ps[:, 4 + r, i * P:(i + 1) * P], xn[:, r, i * P:(i + 1) * P], ident[:])
                            mm.then_inc(s_turn, 1)
                        chunks(pe.Fori, body)
                        for lh in range(NL * HALF):
                            pe.wait_ge(s_set, lh + 1)
                            for k in range(TAPS):
                                mm = pe.transpose(ps[:, lh, k * P:(k + 1) * P], in_tap[:, lh, k, :], ident[:])
                            mm.then_inc(s_tapT, 1)

                UNITS = [(l, s) for l in range(NL) for s in range(STREAMS)]
                CONV, ROWS, DT = 0, 2, 3
                HEAD = 4
                CONV_AT, ROWS_AT, DT_AT, SOFT_AT = HEAD, 8, 9, 11
                DECAYED = [[n + 1] for n in range(NS - 1)] + [[]]
                DECAYED[CONV_AT + 3], DECAYED[CONV_AT + 4] = [CONV_AT + 4, CONV_AT + 5], []
                ADDED = [[14], [15], [0], [1], [2], [3], [4], [], [5, 6], [], [7], [8, 9], [10], [11], [], [12, 13]]

                def side(unit, k):
                    return k if isinstance(unit, int) and unit == 0 else unit * 8 + (k - 1)

                def side_gate(unit, h):
                    return 5 + h if isinstance(unit, int) and unit == 0 else unit * 8 + (4 + h)

                def side_out(unit):
                    return unit * 8 + 14

                def ending(i, unit):
                    return unit - 1, *UNITS[i - 1]

                def run(fori, prepare, step):
                    for n in range(NS):
                        prepare(n, *UNITS[0], 0, 0, 0)
                    for n in range(HEAD):
                        step(n, 0, 0, 0, 0, None)
                    with fori(0, B // STREAMS) as p:
                        with fori(0, C) as c:
                            turn = p * C + c
                            where = lambda bs: p * (STREAMS * T) + c * SEG + bs * T
                            for i in range(len(UNITS) + 1):
                                for n in range(HEAD if i == 0 else 0, NS if i < len(UNITS) else HEAD):
                                    unit = turn * len(UNITS) + i
                                    step(n, i % len(UNITS), unit, *((turn, c) if i < len(UNITS) else (turn + 1, c * -1 + 1)), where)
                                    if i < len(UNITS) - 1:
                                        prepare(n, *UNITS[i + 1], unit + 1, turn, c)
                                    elif i == len(UNITS) - 1:
                                        prepare(n, *UNITS[0], unit + 1, turn + 1, c * -1 + 1)

                with nc.Block() as block:
                    @block.tensor
                    def _(pe):
                        pe.sem_inc(s_acc, RING)

                        def layer_in(l, s, turn, c, k):
                            return xT[:, ds(turn * CHUNK + (s * B * CHUNK + k), SEG)] if l == 0 else hT[:, s, ds(c * SEG + k, SEG)]

                        def prepare(n, l, s, unit, turn, c):
                            if n in (CONV_AT, CONV_AT + 1, CONV_AT + 2, CONV_AT + 3):
                                h, part = (n - CONV_AT) // 2, (n - CONV_AT) % 2
                                if part == 0:
                                    wait(pe, s_side_read, side(unit, CONV + h))
                                for k in range(part * TAPS // 2, (part + 1) * TAPS // 2):
                                    mm = pe.matmul(SIDE, in_tapT[:, l * HALF + h, k, :], layer_in(l, s, turn, c, k), start=(k == 0), stop=(k == TAPS - 1), skip_group_check=True)
                                if part == 1:
                                    mm.then_inc(s_side, 1)
                            if n == ROWS_AT:
                                pe.wait_ge(s_silu, unit + 1)
                                for h in range(HALF):
                                    mm = pe.matmul(SIDE[0:XR], x_w[:, l * HALF + h, :], u(s)[:, h, :], start=(h == 0), stop=(h == HALF - 1))
                                mm.then_inc(s_side, 1)
                            if n in (DT_AT, DT_AT + 1):
                                h = n - DT_AT
                                pe.wait_ge(s_side_read, side(unit, DT + h))
                                pe.matmul(SIDE, dt_w[2 * NS:XR, l * DI + h * P:l * DI + (h + 1) * P], bc[2 * NS:XR, :], start=True, stop=True).then_inc(s_side, 1)

                        def accumulate(g, n):
                            pe.wait_ge(s_seen, g + (RING + 1))
                            for h in range(HALF):
                                mm = pe.matmul(Y[:, h, :], ident[:], seen[:, n % RING, h, :], start=False, stop=(n == NS - 1), skip_group_check=True)
                            mm.then_inc(s_acc, 1)

                        def step(n, i, unit, turn, c, where):
                            l, s = UNITS[i]
                            g = unit * NS + n
                            def row_b(n):
                                pe.wait_ge(s_drive, unit * (NS * 2) + (n * 2 + 2))
                                pe.matmul(PB[:, n % 2, :], spread[:, n * P:(n + 1) * P], parts[:, s, :], start=True, stop=True).then_inc(s_b, 1)
                            if n == 0:
                                pe.wait_ge(s_parts, unit + 1)
                                row_b(0)
                            if n < NS - 1:
                                row_b(n + 1)
                            pe.wait_ge(s_c_sb, g + 1)
                            pe.matmul(PC, spread[:, (n + NS) * P:(n + NS + 1) * P], parts[:, s, :], start=True, stop=True).then_inc(s_c, 1)
                            if n == 2:
                                if where:
                                    pe.wait_ge(s_y, unit)
                                for h in range(HALF):
                                    pe.matmul(Y[:, h, :], skip_diag[:, l * HALF + h, :], u(s)[:, h, :], start=True, stop=False, skip_group_check=True)
                            for m in ADDED[n]:
                                if n >= 2:
                                    accumulate(unit * NS + m, m)
                                elif where:
                                    accumulate(unit * NS + (m - NS), m)
                            if n < HALF:
                                pe.wait_ge(s_side_read, side_gate(unit, n))
                                pe.matmul(SIDE, gateT_w[:, l * DI + n * P:l * DI + (n + 1) * P], layer_in(l, s, turn, c, HIST), start=True, stop=True).then_inc(s_side, 1)
                            if n == HEAD - 1 and where:
                                before_, bl, bs = ending(i, unit)
                                pe.wait_ge(s_y, unit)
                                pe.wait_ge(s_side_read, side_out(before_))
                                if bl < NL - 1:
                                    for h in range(HALF):
                                        mm = pe.matmul(SIDE, out_w[:, bl * HALF + h, :], z(bs)[:, h, :], start=(h == 0), stop=(h == HALF - 1))
                                else:
                                    for t in range(SEG // P):
                                        for h in range(HALF):
                                            mm = pe.matmul(SIDE[:, t * P:(t + 1) * P], z(bs)[:, h, t * P:(t + 1) * P], out_w[:, bl * HALF + h, :], start=(h == 0), stop=(h == HALF - 1))
                                mm.then_inc(s_side, 1)
                        run(pe.Fori, prepare, step)

                    @block.scalar
                    def _(act):
                        act.sem_inc(s_c_sb, 1)

                        def prepare(n, l, s, unit, turn, c):
                            if n == 5:
                                act.activation(first[:, s], last[:, l, s, ds(c, 1)].rearrange("p c h n -> p (c h) n"), ACT.Copy).then_inc(s_first, 1)
                            if n in (CONV_AT + 1, CONV_AT + 3):
                                h = (n - CONV_AT) // 2
                                act.wait_ge(s_side, side(unit, CONV + h) + 1)
                                act.activation(u(s)[:, h, :], SIDE, ACT.Identity, bias=conv_b[:, l * HALF + h:l * HALF + h + 1]).then_inc(s_side_read, 1)
                            if n == CONV_AT + 3:
                                act.wait_ge(s_side_read, side(unit, CONV + 1) + 1)
                                both = u(s) if isinstance(unit, int) else zu[:, s]
                                act.activation(both, both, ACT.Silu).then_inc(s_silu, 1)
                                act.preload_act_table_set("natural_log_exp_and_others")
                            if n == ROWS_AT:
                                act.wait_ge(s_side, side(unit, ROWS) + 1)
                                wait(act, s_parts, unit)
                                act.activation(bc, SIDE[0:XR], ACT.Copy).then_inc(s_side_read, 1)
                            if n == SOFT_AT:
                                act.wait_ge(s_side_read, side(unit, DT + 1) + 1)
                                act.activation(delta_u[:, s], delta[:, s], ACT.Abs).then_inc(s_soft, 1)
                            if n == SOFT_AT + 1:
                                act.wait_ge(s_soft, unit * 3 + 1)
                                act.activation(delta_u[:, s], delta_u[:, s], ACT.Exp, scale=-1.0).then_inc(s_soft, 1)
                            if n == SOFT_AT + 2:
                                act.wait_ge(s_soft, unit * 3 + 2)
                                act.activation(delta_u[:, s], delta_u[:, s], ACT.Ln, bias=1.0).then_inc(s_soft, 1)

                        def step(n, i, unit, turn, c, where):
                            l, s = UNITS[i]
                            g = unit * NS + n
                            def decays(n):
                                act.wait_ge(s_state, unit * (NS * 2) + (n * 2 + 2))
                                for h in range(HALF):
                                    lhn = (l * HALF + h) * NS + n
                                    act.activation(dA[:, n % DECAYS, h, :], delta[:, s, h, :], ACT.Exp, scale=decay[:, lhn:lhn + 1]).then_inc(s_decay, 1)
                            if n == 0:
                                act.wait_ge(s_dt, unit + 1)
                                decays(0)
                            if n in (1, 2):
                                act.wait_ge(s_side, side_gate(unit, n - 1) + 1)
                                act.activation(z(s)[:, n - 1, :], SIDE, ACT.Copy).then_inc(s_side_read, 1)
                            for m in DECAYED[n]:
                                decays(m)
                            act.wait_ge(s_c, g + 1)
                            act.wait_ge(s_seen, g + 1)
                            act.activation(c_sb[:, n % RING, :], PC, ACT.Copy).then_inc(s_c_sb, 1)
                            if n == HEAD - 1 and where:
                                before_, bl, bs = ending(i, unit)
                                if bl < NL - 1:
                                    act.wait_ge(s_side, side_out(before_) + 1)
                                    act.activation(hT[:, bs, ds(c * SEG + HIST, SEG)], SIDE, ACT.Copy).then_inc(s_side_read, 1)
                        run(act.Fori, prepare, step)

                    @block.gpsimd
                    def _(pool):
                        pool.sem_inc(s_seen, RING)

                        def step(n, i, unit, turn, c, where):
                            l, s = UNITS[i]
                            g = unit * NS + n
                            pool.wait_ge(s_state, g * 2 + (DECAYS + 1) * HALF)
                            pool.wait_ge(s_c_sb, g + 2)
                            pool.wait_ge(s_acc, g + 1)
                            pool.tensor_tensor(seen[:, n % RING], state[:, n % RING], c_sb[:, n % RING, :].unsqueeze(1).to_broadcast([P, HALF, SEG]), ALU.mult)
                            pool.tensor_copy(last[:, l, s, C - 1, :, n:n + 1], state[:, n % RING, :, SEG - 1:SEG]).then_inc(s_seen, 1)
                        run(pool.Fori, lambda *_: None, step)

                    @block.vector
                    def _(dve):
                        dve.sem_inc(s_drive, 2 * HALF)
                        dve.sem_inc(s_state, DECAYS * HALF)

                        def prepare(n, l, s, unit, turn, c):
                            if n in (DT_AT, DT_AT + 1):
                                h = n - DT_AT
                                dve.wait_ge(s_side, side(unit, DT + h) + 1)
                                dve.tensor_scalar(delta[:, s, h, :], SIDE, dt_b[:, l * HALF + h:l * HALF + h + 1], None, ALU.add).then_inc(s_side_read, 1)
                            if n == DT_AT + 1:
                                dve.tensor_copy(parts[0:32, s, :], bc[0:32, :]).then_inc(s_split, 1)
                            if n == DT_AT + 2:
                                dve.wait_ge(s_split, unit * 3 + 1)
                                dve.tensor_tensor(rest, bc[0:32, :], parts[0:32, s, :], ALU.subtract).then_inc(s_split, 1)
                                dve.wait_ge(s_split, unit * 3 + 2)
                                dve.tensor_copy(mid, rest).then_inc(s_split, 1)
                                dve.wait_ge(s_split, unit * 3 + 3)
                                dve.tensor_copy(parts[32:64, s, :], mid)
                                dve.tensor_tensor(parts[64:96, s, :], rest, mid, ALU.subtract).then_inc(s_parts, 1)
                            if n == SOFT_AT + 3:
                                dve.wait_ge(s_soft, unit * 3 + 3)
                                dve.scalar_tensor_tensor(delta[:, s], delta[:, s], 0.0, delta_u[:, s], ALU.max, ALU.add).then_inc(s_dt, 1)
                                dve.wait_ge(s_dt, unit + 1)
                                dve.tensor_tensor(delta_u[:, s], delta[:, s], u(s), ALU.mult).then_inc(s_dtu, 1)

                        def step(n, i, unit, turn, c, where):
                            l, s = UNITS[i]
                            g = unit * NS + n
                            if n == 2 and where:
                                before_, bl, bs = ending(i, unit)
                                dve.wait_ge(s_acc, unit * NS + RING)
                                dve.wait_ge(s_silu, unit + 1)
                                dve.tensor_tensor(z(bs), z(bs), Y, ALU.mult).then_inc(s_y, 1)
                            if n == 0:
                                dve.wait_ge(s_first, unit + 1)
                                dve.wait_ge(s_dtu, unit + 1)
                            dve.wait_ge(s_b, g + 1)
                            for h in range(HALF):
                                dve.wait_ge(s_state, g * 2 + (h + DECAYS * HALF - 1))
                                dve.tensor_tensor(DRIVE[:, h, :], delta_u[:, s, h, :], PB[:, n % 2, :], ALU.mult).then_inc(s_drive, 1)
                            dve.wait_ge(s_seen, g + 1)
                            for h in range(HALF):
                                dve.wait_ge(s_drive, g * 2 + (h + 5))
                                dve.wait_ge(s_decay, g * 2 + (h + 1))
                                dve.tensor_tensor_scan(state[:, n % RING, h, :], dA[:, n % DECAYS, h, :], DRIVE[:, h, :], first[:, s, h, n:n + 1], ALU.mult, ALU.add).then_inc(s_state, 1)
                            if n == HEAD - 1 and where:
                                before_, bl, bs = ending(i, unit)
                                if bl == NL - 1:
                                    dve.wait_ge(s_side, side_out(before_) + 1)
                                    dve.tensor_tensor(X[:, ds(where(bs), SEG)], X[:, ds(where(bs), SEG)], SIDE, ALU.add).then_inc(s_side_read, 1)
                        run(dve.Fori, prepare, step)

        if "attention" in phases:
            attention()
        else:
            with nc.Block() as block:
                @block.sync
                def _(sp):
                    load_x(sp)
                    sp.wait_ge(x_in, 64)
                    sp.dma_start(ident[:], a["ident"]).then_inc(small_in, 16)
                    sp.wait_ge(small_in, 16)
                    load_experts(sp)
                    prefill(sp)
        if "ffn1" in phases:
            ffn(0)
        if "mamba" in phases:
            mamba()
        if "ffn2" in phases:
            ffn(1)

        s_out = sem("s_out")
        with nc.Block() as block:
            @block.sync
            def _(sp):
                sp.dma_start(out.rearrange("(t p) d -> p t d", p=P), X[:].rearrange("p (t d) -> p t d", d=D)).then_inc(s_out, 16)
                sp.wait_ge(s_out, 16)
                sp.wait_ge(experts_in, EXPERTS_IN)
                sp.wait_ge(prefilled, 32)


def lay_out(v):
    f = lambda n: np.asarray(v[n], np.float32)
    c = np.ascontiguousarray
    o = {}
    o["x"] = c(f("L0_attn_a_x").reshape(B * T, D))
    o["wqkvT"] = c(f("L0_attn_a_Wqkv").T)
    o["bqkv"] = c(f("L0_attn_a_bqkv").reshape(3, D).T)
    o["woT"] = c(f("L0_attn_a_Wo").T)
    o["bo"] = c(f("L0_attn_a_bo").reshape(1, D))
    gu = np.concatenate([f("L0_ffn_experts_gate_up"), f("L0_ffn_shared_gate_up")[None]])
    o["gate_up"] = c(gu.transpose(2, 0, 1).reshape(D, (E + 1) * GU))
    dn = np.concatenate([f("L0_ffn_experts_down"), f("L0_ffn_shared_down")[None]]).transpose(0, 2, 1)
    o["down"] = c(dn[:, :(NC - 1) * P].reshape(E + 1, NC - 1, P, D).transpose(2, 0, 1, 3).reshape(P, -1))
    o["down_tail"] = c(dn[:, (NC - 1) * P:].transpose(1, 0, 2).reshape(ITAIL, -1))
    o["gateT"] = c(f("L0_ffn_gate_weight").T)
    chan = lambda x: c(x.reshape(NL, HALF, P, -1).transpose(2, 0, 1, 3).reshape(P, -1))
    w_in = f("L0_attn_b_W_in")
    o["m_in"] = chan(w_in[:, :DI])
    o["m_gateT"] = c(w_in[:, DI:].transpose(2, 0, 1).reshape(D, NL * DI))
    o["m_taps"], o["m_conv_b"] = chan(f("L0_attn_b_conv_w")), chan(f("L0_attn_b_conv_b"))
    w_x = f("L0_attn_b_W_x")
    o["m_xT"] = chan(np.concatenate([w_x[:, RANK:], w_x[:, :RANK]], 1).transpose(0, 2, 1))
    o["m_dtT"] = c(f("L0_attn_b_W_dt").transpose(2, 0, 1).reshape(RANK, NL * DI))
    o["m_dt_b"], o["m_A_log"], o["m_skip"] = chan(f("L0_attn_b_b_dt")), chan(f("L0_attn_b_A_log")), chan(f("L0_attn_b_D"))
    o["m_outT"] = chan(f("L0_attn_b_W_out").transpose(0, 2, 1))
    o["m_spread"] = np.repeat(np.tile(np.eye(2 * NS), (3, 1)), P, 1).astype(mybir.dt.np(BF16))
    p = np.arange(P)
    o["ident"] = np.eye(P, dtype=np.float32)
    o["ones_row"] = np.ones((1, P), np.float32)
    o["ones_tile"] = np.ones((P, NT), np.float32)
    o["all_ones"] = np.ones((P, P), np.float32)
    o["before"] = (p[:, None] < p).astype(np.float32)
    o["earlier"] = np.tile((np.arange(E) < np.arange(E)[:, None]).astype(np.float32).reshape(1, -1), (P, 1))
    o["tile_number"] = np.tile(np.arange(SLOTS, dtype=np.float32), (P, 1))
    o["tile_start"] = o["tile_number"] * P
    o["token_row"] = c(np.arange(2 * B * T, dtype=np.int32).reshape(2 * NT, P).T)
    o["nobody"] = np.zeros((P, ROW), np.int32)
    o["nobody"][:, D] = 2 * B * T + p
    o["own_head"] = c(np.repeat((p[:, None] % 32 // HD == np.arange(HG)).astype(np.float32), 32, 1))
    q, k = (p % 32)[:, None, None], np.arange(KW)
    seen = (k > q) & (k <= q + 32) & np.ones((1, NW, 1), bool)
    first = seen & ((np.arange(NW)[:, None] > 0) | (k >= 32))
    o["mask"] = c(np.where(np.stack([seen, first], 1), 0, MASKED).astype(np.float32).reshape(P, -1))
    return o


PHASES = ("attention", "ffn1", "mamba", "ffn2")


def kernel(**inputs):
    import concourse.bacc as bacc
    from concourse.bass_utils import run_bass_kernel_spmd

    nc = bacc.Bacc("TRN2", target_bir_lowering=False, num_devices=1)
    arrays = lay_out(inputs)
    aps = {n: nc.dram_tensor("in_" + n, v.shape, mybir.dt.from_np(v.dtype), kind="ExternalInput").ap() for n, v in arrays.items()}
    out = nc.dram_tensor("out", (B * T, D), F32, kind="ExternalOutput").ap()
    hybrid_block_kernel(nc, aps, out, PHASES)
    r = run_bass_kernel_spmd(nc, [{"in_" + n: v for n, v in arrays.items()}], core_ids=[0])
    return r.results[0]["out"].reshape(B, T, D)
```

```python
from contextlib import ExitStack

import concourse.bass as bass
from concourse import mybir
import numpy as np

F32 = mybir.dt.float32
BF16 = mybir.dt.bfloat16
I32 = mybir.dt.int32
U32 = mybir.dt.uint32
ALU = mybir.AluOpType
ACT = mybir.ActivationFunctionType
AX = mybir.AxisListType
ds = bass.ds

P = 128
B, T, D = 4, 1024, 128
NT = B * T // P
TPB = T // P
EPS = 1e-5

H, HD = 16, 8
HG = 32 // HD
NG = H // HG
NW = P // 32
KW = 64
MASKED = -1e30

E, I = 8, 938
GU = 2 * I
IA = 512
IB = I - IA
CA, CB = IA // P, -(-IB // P)
ITAIL = IB - (CB - 1) * P
NC = CA + CB
EXPERT = GU + NC * D
SHARED_TAIL = 64
SHARED_GU = 2 * (NC - 1) * P + SHARED_TAIL + ITAIL
LODGERS = 8
SLOTS = 2 * NT + E - 1
UNROLL = 4
QUARTERS = 4
IN_FLIGHT = 8
LATE = 2
COMBINED = 6
COMBINE_AFTER = 4
ROW = D + 1

NL, DI, NS, TAPS, RANK = 2, 256, 16, 4, 8
HALF = DI // P
STREAMS = 2
XR = 2 * NS + RANK
SEG = 512


def wait(eng, sem, value):
    if isinstance(value, int) and value <= 0:
        return
    eng.wait_ge(sem, value)


def hybrid_block_kernel(nc, a, out):
    ctx = ExitStack()
    with ctx:
        def sb(name, shape, dt=F32, scope=ctx):
            return scope.enter_context(nc.sbuf_tensor(name, shape, dt))

        def sem(name, scope=ctx):
            return scope.enter_context(nc.semaphore(name))

        X = sb("X", [P, NT * D])
        ident = sb("ident", [P, P])
        experts = sb("experts", [P, E * EXPERT + SHARED_GU + NC * D])
        gateT = sb("gateT", [P, E])
        mean = sb("mean", [P, NT])
        rstd = sb("rstd", [P, NT])
        row_stats = sb("row_stats", [P, NT, 6])
        apart = sb("apart", [P, NT])

        ones_tile = sb("ones_tile", [P, NT])
        all_ones = sb("all_ones", [P, P])
        before = sb("before", [P, P])
        ahead = sb("ahead", [P, E])
        tile_number = sb("tile_number", [P, SLOTS])
        tile_start = sb("tile_start", [P, SLOTS])
        token_row = sb("token_row", [P, 2 * NT], I32)
        nobody = sb("nobody", [P, ROW], I32)

        routed = [nc.dram_tensor(f"routed_{n}", (SLOTS * P, ROW), F32, kind="Internal").ap() for n in range(2)]
        expert_out = [nc.dram_tensor(f"expert_out_{n}", (2 * B * T + P, D), F32, kind="Internal").ap() for n in range(2)]

        x_in = sem("x_in")
        small_in = sem("small_in")
        experts_in = sem("experts_in")
        prefilled = sem("prefilled")

        def load_x(sp):
            x_d = a["x"].rearrange("(t p) d -> p t d", p=P)
            x_s = X[:].rearrange("p (t d) -> p t d", d=D)
            for n in range(4):
                sp.dma_start(x_s[:, n * 8:(n + 1) * 8, :], x_d[:, n * 8:(n + 1) * 8, :]).then_inc(x_in, 16)

        def load_expert(sp, n, done):
            at, width, tail = n * EXPERT, SHARED_GU if n == E else GU, SHARED_TAIL if n == E else 0
            sp.dma_start(experts[:, at:at + width], a["gate_up"][:, n * GU:n * GU + width]).then_inc(done, 16)
            body = experts[:, at + width:at + width + NC * D]
            sp.dma_start(body[:, 0:(NC - 1) * D], a["down"][:, n * (NC - 1) * D:(n + 1) * (NC - 1) * D]).then_inc(done, 16)
            sp.dma_start(body[tail:tail + ITAIL, (NC - 1) * D:NC * D], a["down_tail"][:, n * D:(n + 1) * D]).then_inc(done, 16)

        def load_experts(sp):
            sp.dma_start(gateT[:], a["gateT"]).then_inc(experts_in, 16)
            for dst, name in shapes:
                sp.dma_start(dst[:], a[name]).then_inc(experts_in, 16)
            for n in range(E, -1, -1):
                load_expert(sp, n, experts_in)

        lodgers_in = sem("lodgers_in")
        row_summed = sem("row_summed")
        s_out = sem("s_out")
        summed = [0]
        spent = []
        shapes = [(ones_tile, "ones_tile"), (all_ones, "all_ones"), (before, "before"), (ahead, "ahead"),
                  (tile_number, "tile_number"), (tile_start, "tile_start"), (token_row, "token_row")]
        EXPERTS_IN = 16 * (1 + len(shapes) + 3 * (E + 1))
        s_nobody = sem("s_nobody")

        def prefill(sp):
            sp.dma_start(nobody[:], a["nobody"]).then_inc(s_nobody, 16)
            sp.wait_ge(s_nobody, 16)
            for dst in routed:
                sp.dma_start(dst.rearrange("(t p) r -> p t r", p=P), nobody[:].bitcast(F32).unsqueeze(1).to_broadcast([P, SLOTS, ROW])).then_inc(prefilled, 16)

        def row_sums(dve, t):
            dve.bn_stats(row_stats[:, ds(t, 1), :], X[:, ds(t * D, D)]).then_inc(row_summed, 1)

        def whole(x):
            return x

        def variances(dve, s_stats, s_var, of=whole, nth=1):
            halves, mu, var, gap = of(row_stats[:]), of(mean[:]), of(rstd[:]), of(apart[:])
            at = lambda k: halves[..., k]
            dve.wait_ge(row_summed, summed[0])
            dve.tensor_tensor(mu, at(1), at(4), ALU.add)
            dve.tensor_tensor(gap, at(1), at(4), ALU.subtract)
            dve.tensor_tensor(var, at(2), at(5), ALU.add).then_inc(s_stats, 1)
            dve.wait_ge(s_stats, nth * 2 - 1)
            dve.tensor_scalar(mu, mu, 0.5, None, ALU.mult)
            dve.tensor_scalar(var, var, 1.0 / D, EPS, ALU.mult, ALU.add)
            dve.scalar_tensor_tensor(gap, gap, 0.25, gap, ALU.mult, ALU.mult).then_inc(s_stats, 1)
            dve.wait_ge(s_stats, nth * 2)
            dve.tensor_tensor(var, var, gap, ALU.add).then_inc(s_var, 1)

        def inverses(dve, s_std, s_rstd, nth=1, of=whole):
            dve.wait_ge(s_std, nth)
            dve.reciprocal(of(rstd[:]), of(rstd[:])).then_inc(s_rstd, 1)
            dve.wait_ge(s_rstd, nth)

        def deviations(act, s_var, s_std, nth=1, of=whole):
            act.wait_ge(s_var, nth)
            act.activation(of(rstd[:]), of(rstd[:]), ACT.Sqrt).then_inc(s_std, 1)

        def layernorm(dve, dst, t):
            return dve.tensor_scalar(dst, X[:, ds(t * D, D)], mean[:, ds(t, 1)], rstd[:, ds(t, 1)], ALU.subtract, ALU.mult)

        def attention():
            scope = ExitStack()
            with scope:
                def tb(name, shape, dt=F32):
                    return sb(name, shape, dt, scope)

                def ts(name):
                    spent.append(sem("at_" + name, scope))
                    return spent[-1]

                wqkvT = tb("wqkvT", [P, 3 * D])
                woT = tb("woT", [P, D])
                bqkv = tb("bqkv", [P, 3])
                bq = tb("bq", [P, 1])
                bo = tb("bo", [1, D])
                ones = tb("ones", [1, P])
                own_head = tb("own_head", [P, HG])
                mask = tb("mask", [P, 2, KW])
                xn = tb("xn", [P, 2, D])
                xnT = tb("xnT", [P, B, 32 + P])
                qT = tb("qT", [P, 2, P])
                kT = tb("kT", [P, B, 32 + P])
                k_spread = tb("k_spread", [P, 2, HG, 32 + P])
                v = tb("v", [P, B, NW, D])
                sc = tb("sc", [P, H, KW])
                probs = tb("probs", [P, B, H, KW])
                top = tb("top", [P, 16])
                total = tb("total", [P, 16])
                inv = tb("inv", [P, 16])
                probsT = tb("probsT", [P, 2, NG * P])
                own = tb("own", [P, 2, 2, P])
                ysum = tb("ysum", [P, P])
                yT = tb("yT", [P, P])

                score_ps = scope.enter_context(nc.psum_tensor("score_ps", [P, NG, SEG], F32))
                turn_ps = scope.enter_context(nc.psum_tensor("turn_ps", [P, NG, P], F32))
                pv_ps = scope.enter_context(nc.psum_tensor("pv_ps", [P, 2, SEG], F32))
                qkv_ps = scope.enter_context(nc.psum_tensor("qkv_ps", [P, SEG], F32))

                s_stats, s_var, s_std, s_rstd = ts("stats"), ts("var"), ts("std"), ts("rstd")
                s_zero, s_bq = ts("zeroed"), ts("bq")
                s_ln, s_x_turned, s_xnT, s_hist = ts("ln"), ts("x_turned"), ts("xnT"), ts("hist")
                s_qkv, s_qk, s_kh, s_spread = ts("qkv"), ts("qk_copied"), ts("k_hist"), ts("spread")
                s_score, s_mask, s_top, s_sub, s_exp = ts("score"), ts("masked"), ts("top"), ts("sub"), ts("exp")
                s_total, s_inv, s_probs = ts("total"), ts("inv"), ts("probs")
                s_turn, s_turned, s_pv = ts("turn"), ts("turned"), ts("pv")
                s_own, s_ysum, s_yT, s_wo, s_x = ts("own"), ts("ysum"), ts("yT"), ts("wo"), ts("x")

                small = [(ident[:], "ident"), (wqkvT[:], "wqkvT"), (woT[:], "woT"), (bqkv[:], "bqkv"), (bo[:], "bo"),
                         (own_head[:], "own_head"),
                         (mask[:].rearrange("p f k -> p (f k)"), "mask"), (ones[:], "ones_row")]
                SMALL = 16 * len(small)

                def at(n, r):
                    return n * B + r

                def tile(n, r):
                    n, r = n + r // B, r % B
                    return r * TPB + n, r

                def rounds(x, some):
                    return (x.rearrange("p (b k) -> p b k", k=TPB) if len(x.shape) == 2 else x.rearrange("p (b k) s -> p b k s", k=TPB))[:, :, some]

                first_round, later_rounds = (lambda x: rounds(x, slice(0, 1))), (lambda x: rounds(x, slice(1, TPB)))

                def run(eng_fori, body):
                    for r in range(-3, B):
                        body(0, r)
                    with eng_fori(1, TPB - 1) as n:
                        for r in range(B):
                            body(n, r)
                    for r in range(B + 3):
                        body(TPB - 1, r)

                def alive(n, r):
                    if isinstance(n, int):
                        return 0 <= n * B + r < NT
                    return True

                with nc.Block() as block:
                    @block.sync
                    def _(sp):
                        load_x(sp)
                        for dst, name in small:
                            sp.dma_start(dst, a[name]).then_inc(small_in, 16)
                        load_experts(sp)
                        prefill(sp)

                    @block.gpsimd
                    def _(pool):
                        pool.wait_ge(small_in, SMALL)
                        def body(n, r):
                            if alive(n, r + 1):
                                t = at(n, r + 1)
                                pool.wait_ge(s_top, t + 1)
                                pool.tensor_tensor(sc[:], sc[:],
                                                   top[:, :].unsqueeze(2).to_broadcast([P, 16, KW]), ALU.subtract).then_inc(s_sub, 1)
                            if alive(n, r + 2):
                                t = at(n, r + 2)
                                s = r % 2
                                pool.wait_ge(s_qk, 2 * t + 1)
                                wait(pool, s_score, t - 1)
                                pool.tensor_tensor(k_spread[:, s], kT[:, (r + 2) % B, :].unsqueeze(1).to_broadcast([P, HG, 32 + P]),
                                                   own_head[:].unsqueeze(2).to_broadcast([P, HG, 32 + P]), ALU.mult).then_inc(s_spread, 1)
                            if alive(n, r + 1):
                                t = at(n, r + 1)
                                s = (r + 1) % B
                                pool.wait_ge(s_inv, t + 1)
                                pr = probs[:, s]
                                pool.tensor_tensor(pr, pr, inv[:, :].unsqueeze(2).to_broadcast([P, 16, KW]), ALU.mult).then_inc(s_probs, 1)
                        run(pool.Fori, body)

                    @block.scalar
                    def _(act):
                        act.wait_ge(small_in, SMALL)
                        act.mul(bq[:], bqkv[:, 0:1], HD ** -0.5).then_inc(s_bq, 1)
                        deviations(act, s_var, s_std, 1, first_round)
                        act.wait_ge(s_bq, 1)
                        act.wait_ge(s_zero, 1)
                        def body(n, r):
                            if alive(n, r + 2):
                                t = at(n, r + 2)
                                b = (r + 2) % B
                                act.wait_ge(s_x_turned, t + 1)
                                if not (isinstance(t, int) and t < B):
                                    act.activation(xnT[:, b, 0:32], xnT[:, b, P:P + 32], ACT.Copy).then_inc(s_hist, 1)
                                    act.wait_ge(s_hist, t + 1 - B)
                                act.activation(xnT[:, b, 32:32 + P], qkv_ps[:, 0:P], ACT.Copy).then_inc(s_xnT, 1)
                            if alive(n, r - 1):
                                t = at(n, r - 1)
                                act.wait_ge(s_turn, 2 * t + 1)
                                wait(act, s_pv, t)
                                act.activation(probsT[:, 0, :], turn_ps[:].rearrange("p g q -> p (g q)"), ACT.Copy).then_inc(s_turned, 1)
                            if alive(n, r + 2):
                                t = at(n, r + 2)
                                b = (r + 2) % B
                                s = r % 2
                                act.wait_ge(s_qkv, 2 * t + 1)
                                wait(act, s_score, t - 1)
                                act.activation(qT[:, s, :], qkv_ps[:, 0:P], ACT.Identity, bias=bq[:], scale=HD ** -0.5)
                                wait(act, s_spread, t - B + 1)
                                if not (isinstance(t, int) and t < B):
                                    act.activation(kT[:, b, 0:32], kT[:, b, P:P + 32], ACT.Copy).then_inc(s_kh, 1)
                                    act.wait_ge(s_kh, t + 1 - B)
                                act.activation(kT[:, b, 32:32 + P], qkv_ps[:, P:2 * P], ACT.Identity, bias=bqkv[:, 1:2])
                                wait(act, s_pv, t - B + 1)
                                act.activation(v[:, b, 0:2, :].rearrange("p w d -> p (w d)"), qkv_ps[:, 2 * P:4 * P], ACT.Copy).then_inc(s_qk, 1)
                            if alive(n, r - 1):
                                t = at(n, r - 1)
                                act.wait_ge(s_turn, 2 * t + 2)
                                act.activation(probsT[:, 1, :], turn_ps[:].rearrange("p g q -> p (g q)"), ACT.Copy).then_inc(s_turned, 1)
                            if alive(n, r + 2):
                                t = at(n, r + 2)
                                act.wait_ge(s_qkv, 2 * t + 2)
                                act.activation(v[:, (r + 2) % B, 2:4, :].rearrange("p w d -> p (w d)"), qkv_ps[:, 0:2 * P], ACT.Copy).then_inc(s_qk, 1)
                            if alive(n, r + 1):
                                t = at(n, r + 1)
                                s = (r + 1) % B
                                act.wait_ge(s_sub, t + 1)
                                wait(act, s_turn, 2 * (t - B + 1))
                                act.activation(probs[:, s], sc[:], ACT.Exp).then_inc(s_exp, 1)
                                if isinstance(t, int) and t == 1:
                                    deviations(act, s_var, s_std, 2, later_rounds)
                        run(act.Fori, body)

                    @block.vector
                    def _(dve):
                        dve.memset(xnT[:], 0.0)
                        dve.memset(kT[:], 0.0).then_inc(s_zero, 1)
                        dve.wait_ge(x_in, 64)
                        for b in range(B):
                            row_sums(dve, b * TPB)
                        summed[0] = B
                        variances(dve, s_stats, s_var, first_round)
                        inverses(dve, s_std, s_rstd, 1, first_round)
                        dve.wait_ge(small_in, SMALL)
                        def body(n, r):
                            if alive(n, r - 2):
                                t = at(n, r - 2)
                                dve.wait_ge(s_pv, t + 1)
                                dve.tensor_tensor(own[:], pv_ps[:, :, 0:2 * P].rearrange("p o (j c) -> p o j c", j=2),
                                                  own_head[:].rearrange("p (j o) -> p o j", o=2).unsqueeze(3).to_broadcast([P, 2, 2, P]), ALU.mult).then_inc(s_own, 1)
                            if alive(n, r + 1):
                                t = at(n, r + 1)
                                first = isinstance(t, int) and t < B
                                dve.wait_ge(s_score, t + 1)
                                wait(dve, s_exp, t)
                                dve.tensor_tensor(sc[:].rearrange("p (g h) k -> p g h k", g=NG), score_ps[:, :, 0:HG * KW].rearrange("p g (h k) -> p g h k", h=HG),
                                                  mask[:, int(first), :].unsqueeze(1).unsqueeze(1).to_broadcast([P, NG, HG, KW]), ALU.add).then_inc(s_mask, 1)
                            if alive(n, r - 2):
                                t = at(n, r - 2)
                                dve.wait_ge(s_own, t + 1)
                                dve.tensor_reduce(ysum[:], own[:].rearrange("p o j t -> p t o j"), AX.XY, ALU.add).then_inc(s_ysum, 1)
                            if alive(n, r + 1):
                                t = at(n, r + 1)
                                dve.wait_ge(s_mask, t + 1)
                                wait(dve, s_sub, t)
                                dve.tensor_reduce(top[:], sc[:], AX.X, ALU.max).then_inc(s_top, 1)
                            if alive(n, r - 2):
                                t = at(n, r - 2)
                                dve.wait_ge(s_ysum, t + 1)
                                wait(dve, s_wo, t)
                                dve.tensor_scalar(yT[:], ysum[:], bqkv[:, 2:3], None, ALU.add).then_inc(s_yT, 1)
                            if alive(n, r + 3):
                                t = at(n, r + 3)
                                wait(dve, s_x_turned, t - 1)
                                layernorm(dve, xn[:, (r + 3) % 2, :], tile(n, r + 3)[0]).then_inc(s_ln, 1)
                                if isinstance(t, int) and t == 1:
                                    with dve.Fori(1, TPB) as k:
                                        for b in range(B):
                                            row_sums(dve, k + b * TPB)
                                    summed[0] = NT
                                if isinstance(t, int) and t == B - 1:
                                    variances(dve, s_stats, s_var, later_rounds, 2)
                            if alive(n, r - 2):
                                t = at(n, r - 2)
                                j = tile(n, r - 2)[0]
                                dve.wait_ge(s_wo, t + 1)
                                dve.tensor_tensor(X[:, ds(j * D, D)], X[:, ds(j * D, D)], qkv_ps[:, 0:D], ALU.add).then_inc(s_x, 1)
                            if alive(n, r + 1):
                                t = at(n, r + 1)
                                s = (r + 1) % B
                                dve.wait_ge(s_exp, t + 1)
                                dve.tensor_reduce(total[:], probs[:, s], AX.X, ALU.add).then_inc(s_total, 1)
                                dve.wait_ge(s_total, t + 1)
                                wait(dve, s_probs, t)
                                dve.reciprocal(inv[:], total[:]).then_inc(s_inv, 1)
                                if isinstance(t, int) and t == 1:
                                    inverses(dve, s_std, s_rstd, 2, later_rounds)
                            if alive(n, r - 3):
                                t = at(n, r - 3)
                                dve.wait_ge(s_x, t + 1)
                                row_sums(dve, tile(n, r - 3)[0])
                        run(dve.Fori, body)

                    @block.tensor
                    def _(pe):
                        pe.wait_ge(small_in, SMALL)

                        spread_count, mask_count, turned_count = (pe.alloc_register(x) for x in ("spread_count", "mask_count", "turned_count"))

                        def products(r, half):
                            for g in range(half * NG // 2, (half + 1) * NG // 2):
                                for w in range(NW):
                                    for odd in range(2):
                                        mm = pe.matmul(pv_ps[32 * g:32 * g + 32, odd, 0:2 * P].rearrange("p (j c) -> p j c", j=2)[:, :, 32 * w:32 * w + 32],
                                                       v[64 * odd:64 * odd + 64, r % B, w, 32 * g:32 * g + 32],
                                                       probsT[64 * odd:64 * odd + 64, half, g % 2 * 2 * P:(g % 2 + 1) * 2 * P].rearrange("p (j c) -> p j c", j=2)[:, :, 32 * w:32 * w + 32],
                                                       start=True, stop=True)
                            return mm

                        def v_of(r, windows, at):
                            for w in windows:
                                for odd in range(2):
                                    mm = pe.matmul(qkv_ps[64 * odd:64 * odd + 64, (at + w % 2) * P:(at + w % 2 + 1) * P], xnT[:, r % B, 32 * w:32 * w + KW],
                                                   wqkvT[:, 2 * D:3 * D], start=True, stop=True)
                            return mm

                        def body(n, r):
                            if alive(n, r + 1):
                                t = at(n, r + 1)
                                s = (r + 1) % 2
                                if not isinstance(t, int):
                                    pe.reg_mov(spread_count, t + 1)
                                    pe.reg_mov(mask_count, t)
                                pe.wait_ge(small_in, SMALL)
                                pe.wait_ge(s_spread, t + 1 if isinstance(t, int) else spread_count)
                                wait(pe, s_mask, t if isinstance(t, int) else mask_count)
                                for w in range(NW):
                                    for g in range(NG):
                                        mm = pe.matmul(score_ps[32 * w:32 * w + 32, g, 0:HG * KW], qT[32 * g:32 * g + 32, s, 32 * w:32 * w + 32],
                                                       k_spread[32 * g:32 * g + 32, s, :, 32 * w:32 * w + KW], start=True, stop=True)
                                mm.then_inc(s_score, 1)
                            if alive(n, r + 2):
                                t = at(n, r + 2)
                                pe.wait_ge(s_ln, t + 1)
                                wait(pe, s_x, t - 4)
                                wait(pe, s_qk, 2 * t)
                                pe.transpose(qkv_ps[:, 0:P], xn[:, r % 2, :], ident[:]).then_inc(s_x_turned, 1)
                            if alive(n, r - 1):
                                t = at(n, r - 1)
                                s = (r - 1) % B
                                pe.wait_ge(s_probs, t + 1)
                                wait(pe, s_turned, 2 * t)
                                for g in range(NG):
                                    mm = pe.transpose(turn_ps[:, g, :], probs[:, s, 2 * g:2 * g + 2, :].rearrange("p h k -> p (h k)"), ident[:])
                                mm.then_inc(s_turn, 1)
                            if alive(n, r + 2):
                                t = at(n, r + 2)
                                b = (r + 2) % B
                                pe.wait_ge(s_xnT, t + 1)
                                pe.matmul(qkv_ps[:, 0:P], wqkvT[:, 0:D], xnT[:, b, 32:32 + P], start=True, stop=True)
                                pe.matmul(qkv_ps[:, P:2 * P], wqkvT[:, D:2 * D], xnT[:, b, 32:32 + P], start=True, stop=True)
                                mm = v_of(r + 2, (0, 1), 2)
                                mm.then_inc(s_qkv, 1)
                            if alive(n, r - 1):
                                t = at(n, r - 1)
                                s = (r - 1) % B
                                wait(pe, s_own, t)
                                pe.wait_ge(s_turned, 2 * t + 1)
                                for g in range(NG):
                                    mm = pe.transpose(turn_ps[:, g, :], probs[:, s, H // 2 + 2 * g:H // 2 + 2 * g + 2, :].rearrange("p h k -> p (h k)"), ident[:])
                                mm.then_inc(s_turn, 1)
                                products(r - 1, 0)
                            if alive(n, r + 2):
                                pe.wait_ge(s_qk, 2 * at(n, r + 2) + 1)
                                v_of(r + 2, (2, 3), 0).then_inc(s_qkv, 1)
                            if alive(n, r - 1):
                                t = at(n, r - 1)
                                if not isinstance(t, int):
                                    pe.reg_mov(turned_count, 2 * t + 2)
                                pe.wait_ge(small_in, SMALL)
                                pe.wait_ge(s_turned, 2 * t + 2 if isinstance(t, int) else turned_count)
                                products(r - 1, 1).then_inc(s_pv, 1)
                            if alive(n, r - 2):
                                t = at(n, r - 2)
                                pe.wait_ge(s_yT, t + 1)
                                wait(pe, s_x, t)
                                if alive(n, r + 2):
                                    pe.wait_ge(s_qk, 2 * at(n, r + 2) + 2)
                                pe.matmul(qkv_ps[:, 0:D], yT[:], woT[:], start=True, stop=False)
                                pe.matmul(qkv_ps[:, 0:D], ones[:], bo[:], start=False, stop=True).then_inc(s_wo, 1)
                        run(pe.Fori, body)

        def ffn(n):
            scope = ExitStack()
            with scope:
                def tb(name, shape, dt=F32):
                    return sb(f"f{n}_" + name, shape, dt, scope)

                def ts(name):
                    return sem(f"f{n}_" + name, scope)

                def pb(name, shape):
                    return inner.enter_context(nc.psum_tensor(f"f{n}_" + name, shape, F32))

                rows = tb("rows", [P, NT, 2, ROW])
                cols = tb("cols", [P, NT * P])
                G0, G1 = rows[:, :, 0, 0:D], cols[:].rearrange("p (t d) -> p t d", d=D)

                inner = ExitStack()
                with inner:
                    def tb(name, shape, dt=F32):
                        return sb(f"f{n}_" + name, shape, dt, inner)

                    scratch = tb("scratch", [P, LATE * SEG])
                    probs, rest, chosen, taken = (scratch[:, k * NT * E:(k + 1) * NT * E].rearrange("p (t e) -> p t e", e=E) for k in range(4))
                    top = tb("top", [P, NT])
                    next_top = tb("next_top", [P, NT])
                    red = tb("red", [P, NT])
                    many = tb("many", [P, max(E * NT, SLOTS * E)])
                    first = tb("first", [P, NT, E])
                    second = tb("second", [P, NT, E])
                    w0 = tb("w0", [P, NT])
                    w1 = tb("w1", [P, NT])
                    sums = tb("sums", [P, NT, E])
                    upto = tb("upto", [P, NT, E])
                    place = tb("place", [P, NT, E])
                    picked = tb("picked", [P, NT, E])
                    tiles = tb("tiles", [P, E])
                    ends = tb("ends", [P, E])
                    base = tb("base", [P, E])
                    place_f = tb("place_f", [P, 2, NT])
                    place_i = tb("place_i", [P, 2, NT], I32)
                    expert_f = tb("expert_f", [P, SLOTS])
                    weights_at = tb("weights_at", [P, SLOTS // UNROLL + 1, UNROLL], I32)
                    xin = tb("xin", [P, 2, ROW])
                    back = tb("back", [P, 2], I32)
                    back_to = tb("back_to", [P, 2], I32)
                    xT = tb("xT", [P, 2, P])
                    gated = tb("gated", [P, I])
                    inner_h = tb("inner_h", [P, I])
                    hTA = tb("hTA", [P, 2, CA * P])
                    hTB = tb("hTB", [P, CB * P])
                    yout = tb("yout", [P, 2, D])
                    up_ps = pb("up_ps", [P, 4, SEG])
                    ta_ps, tb_ps, xt_ps, y_ps = (pb(x, [P, SEG]) for x in ("ta_ps", "tb_ps", "xt_ps", "y_ps"))

                    s_stats, s_var, s_std, s_rstd = ts("stats"), ts("var"), ts("std"), ts("rstd")
                    s_ln, s_turn, s_cols, s_logit = ts("ln"), ts("turn"), ts("cols"), ts("logit")
                    s_r, s_shift, s_rexp, s_taken, s_count, s_route = (ts(x) for x in ("r", "shift", "rexp", "taken", "count", "route"))
                    s_copied, s_sent = ts("copied"), [ts(f"sent{k}") for k in range(IN_FLIGHT)]
                    s_xin, s_tx, s_xT2 = [ts("xin0"), ts("xin1")], ts("tx"), ts("xT")
                    s_upA, s_upB, s_gA, s_gB, s_hA, s_hB = (ts(x) for x in ("upA", "upB", "gA", "gB", "hA", "hB"))
                    s_tA, s_tB, s_cA, s_cB, s_down, s_y = (ts(x) for x in ("tA", "tB", "cA", "cB", "down", "y"))
                    s_upS, s_gS, s_hS, s_dS = (ts(x) for x in ("upS", "gS", "hS", "dS"))
                    s_yS, s_tS, s_xS, s_late, s_sum = (ts(x) for x in ("yS", "tS", "xS", "late", "sum"))
                    s_back, s_home, s_g = ts("back"), [ts("home0"), ts("home1")], [ts(f"g{c}") for c in range(QUARTERS)]

                    GROUP = SEG // P
                    GROUPS = NT // GROUP
                    COUNT_AFTER = 4

                    gates = hTA
                    acts = [gated[:, 0:SEG], inner_h[:, 0:SEG]]
                    out_cols = hTB
                    late_cols = scratch
                    GU_AT, DOWN_AT = E * EXPERT, E * EXPERT + SHARED_GU

                    def chunk_rows(c):
                        return slice(0, P) if c < NC - 1 else slice(SHARED_TAIL, SHARED_TAIL + ITAIL)

                    def shared(fori, chunk, end, groups, after=lambda g, c: None):
                        def group(g, follows):
                            for c in range(NC):
                                chunk(g, c, follows)
                                if isinstance(g, int):
                                    after(g, c)
                        group(groups[0], False)
                        group(groups[1], True)
                        if len(groups) > 2:
                            with fori(groups[2], groups[-1] + 1) as g:
                                group(g, True)
                        end(groups[-1])

                    EARLY_GROUPS, LATE_GROUPS = range(GROUPS - LATE), range(GROUPS - LATE, GROUPS)

                    def run(fori, body, before=lambda m: None):
                        def turn(m):
                            before(m)
                            for i in range(UNROLL):
                                body(m * UNROLL + i, i % 2, i)
                        turn(0)
                        with fori(1, SLOTS // UNROLL) as m:
                            turn(m)
                        turn(SLOTS // UNROLL)

                    def exists(t):
                        return not isinstance(t, int) or 0 <= t < SLOTS

                    with nc.Block() as block:
                        @block.vector
                        def _(dve):
                            count = [0]

                            def own(ins):
                                count[0] += 1
                                ins.then_inc(s_r, 1)
                                dve.wait_ge(s_r, count[0])

                            def per_token(x):
                                return x.unsqueeze(2).to_broadcast([P, NT, E])

                            variances(dve, s_stats, s_var)
                            inverses(dve, s_std, s_rstd)
                            def normalise_rows(g):
                                for t in range(g * GROUP, (g + 1) * GROUP):
                                    ins = layernorm(dve, rows[:, t, 0, 0:D], t)
                                ins.then_inc(s_ln, 1)
                            normalise_rows(0)
                            normalise_rows(1)

                            logits = xt_ps[:, 0:NT * E].rearrange("p (t e) -> p t e", e=E)

                            def shift():
                                dve.wait_ge(s_logit, 1)
                                own(dve.tensor_reduce(red[:], logits, AX.X, ALU.max))
                                dve.tensor_tensor(probs, logits, per_token(red[:]), ALU.subtract).then_inc(s_shift, 1)

                            def choose(it, best, choice):
                                own(dve.tensor_reduce(best[:], it[:], AX.X, ALU.max))
                                own(dve.tensor_tensor(chosen, it[:], per_token(best[:]), ALU.is_equal))
                                own(dve.tensor_tensor(chosen, chosen, ahead[:].unsqueeze(1).to_broadcast([P, NT, E]), ALU.mult))
                                own(dve.tensor_reduce(red[:], chosen, AX.X, ALU.max))
                                own(dve.tensor_tensor(choice[:], chosen, per_token(red[:]), ALU.is_equal))

                            def normalise():
                                dve.wait_ge(s_rexp, 1)
                                own(dve.tensor_reduce(red[:], probs, AX.X, ALU.add))
                                own(dve.reciprocal(red[:], red[:]))
                                own(dve.tensor_tensor(probs, probs, per_token(red[:]), ALU.mult))

                            def choose_first():
                                choose(probs, top, first)
                                own(dve.scalar_tensor_tensor(rest, first[:], -2.0, probs, ALU.mult, ALU.add))

                            def choose_second():
                                choose(rest, next_top, second)
                                dve.tensor_tensor(taken, first[:], second[:], ALU.add).then_inc(s_taken, 1)

                            def shares():
                                own(dve.scalar_tensor_tensor(red[:], top[:], 1e-8, next_top[:], ALU.add, ALU.add))
                                own(dve.reciprocal(red[:], red[:]))
                                dve.tensor_tensor(w0[:], top[:], red[:], ALU.mult)
                                own(dve.tensor_tensor(w1[:], next_top[:], red[:], ALU.mult))

                            count_ps = xt_ps[:].rearrange("p (k t e) -> p k t e", k=2, e=E)

                            def count_tiles():
                                dve.wait_ge(s_count, 1)
                                own(dve.tensor_copy(sums[:], count_ps[:, 1]))
                                for e in range(E):
                                    ins = dve.tensor_tensor_scan(upto[:, :, e], ones_tile[:], sums[:, :, e], 0.0, ALU.mult, ALU.add)
                                own(ins)
                                counted = many[:, 0:E * NT].rearrange("p (e t) -> p e t", e=E)
                                own(dve.tensor_tensor(counted, upto[:, NT - 1, :].unsqueeze(2).to_broadcast([P, E, NT]),
                                                      tile_start[:, 0:NT].unsqueeze(1).to_broadcast([P, E, NT]), ALU.is_gt))
                                own(dve.tensor_reduce(tiles[:], counted, AX.X, ALU.add))
                                own(dve.tensor_tensor_scan(ends[:], ones_tile[:, 0:E], tiles[:], 0.0, ALU.mult, ALU.add))
                                own(dve.tensor_tensor(base[:], ends[:], tiles[:], ALU.subtract))
                                own(dve.tensor_scalar(base[:], base[:], float(P), None, ALU.mult))

                            def find_places():
                                own(dve.tensor_tensor(place[:], upto[:], sums[:], ALU.subtract))
                                own(dve.tensor_tensor(place[:], place[:], count_ps[:, 0], ALU.add))
                                own(dve.tensor_tensor(place[:], place[:], base[:].unsqueeze(1).to_broadcast([P, NT, E]), ALU.add))
                                own(dve.tensor_tensor(picked[:], first[:], place[:], ALU.mult))
                                own(dve.tensor_reduce(place_f[:, 0, :], picked[:], AX.X, ALU.add))
                                own(dve.tensor_tensor(picked[:], second[:], place[:], ALU.mult))
                                own(dve.tensor_reduce(place_f[:, 1, :], picked[:], AX.X, ALU.add))
                                dve.tensor_copy(place_i[:], place_f[:])

                            def find_experts():
                                ended = many[:, 0:SLOTS * E].rearrange("p (t e) -> p t e", e=E)
                                own(dve.tensor_tensor(ended, ends[:].unsqueeze(1).to_broadcast([P, SLOTS, E]),
                                                      tile_number[:].unsqueeze(2).to_broadcast([P, SLOTS, E]), ALU.is_le))
                                own(dve.tensor_reduce(expert_f[:], ended, AX.X, ALU.add))
                                own(dve.tensor_scalar(expert_f[:], expert_f[:], float(E - 1), None, ALU.min))
                                own(dve.tensor_scalar(expert_f[:], expert_f[:], float(EXPERT), None, ALU.mult))
                                full = SLOTS // UNROLL
                                by_turn = expert_f[:, 0:full * UNROLL].rearrange("p (m i) -> p m i", i=UNROLL)
                                dve.tensor_copy(weights_at[:, 0:full, :], by_turn)
                                dve.tensor_copy(weights_at[:, full, 0:SLOTS % UNROLL], expert_f[:, full * UNROLL:SLOTS]).then_inc(s_route, 1)

                            router = [normalise, choose_first, choose_second, shares, lambda: None, count_tiles, find_places, find_experts]

                            def chunk(g, c, follows):
                                k = g * NC + c
                                w = chunk_rows(c)
                                up_half = up_ps[w, 2 * (c % 2) + (1 if c < NC - 1 else 0), :]
                                dve.wait_ge(s_gS, k + 1)
                                wait(dve, s_dS, k - 1)
                                dve.tensor_tensor(acts[c % 2][w], gates[w, c % 2, :], up_half, ALU.mult).then_inc(s_hS, 1)
                                if follows and c == 2:
                                    end(g - 1)

                            def end(g):
                                dve.wait_ge(s_tS, g + 1)
                                dve.tensor_tensor(X[:, ds(g * SEG, SEG)], X[:, ds(g * SEG, SEG)], ta_ps[:], ALU.add).then_inc(s_xS, 1)

                            def beside(g, c):
                                if g == 0:
                                    if c + 2 < GROUPS:
                                        normalise_rows(c + 2)
                                    elif c == NC - 1:
                                        shift()
                                else:
                                    router[c]()
                            shared(dve.Fori, chunk, end, EARLY_GROUPS, beside)

                            def body(t, s, i):
                                if exists(t):
                                    wait(dve, s_tA, t)
                                    dve.wait_ge(s_gA, t + 1)
                                    dve.tensor_tensor(inner_h[:, 0:IA], gated[:, 0:IA], up_ps[:, 1, 0:IA], ALU.mult).then_inc(s_hA, 1)
                                    dve.wait_ge(s_xin[s], (t - s) * 8 + 16)
                                    wait(dve, s_y, t - 1)
                                    dve.tensor_copy(back[:, s:s + 1], xin[:, s, D:ROW].bitcast(I32)).then_inc(s_back, 1)
                                    wait(dve, s_tB, t)
                                    dve.wait_ge(s_gB, t + 1)
                                    dve.tensor_tensor(inner_h[:, IA:I], gated[:, IA:I], up_ps[:, 3, 0:IB], ALU.mult).then_inc(s_hB, 1)
                                if exists(t - 1):
                                    k = t - 1
                                    wait(dve, s_home[1 - s], (k - (1 - s)) * 8)
                                    dve.wait_ge(s_back, k + 1)
                                    dve.tensor_copy(back_to[:, 1 - s:2 - s], back[:, 1 - s:2 - s])
                                    dve.wait_ge(s_down, t)
                                    dve.tensor_copy(yout[:, 1 - s, :], y_ps[:, 0:D]).then_inc(s_y, 1)
                            run(dve.Fori, body)

                            SHARES = [(j, g, w) for c in range(QUARTERS) for g, w in ((G0, w0), (G1, w1)) for j in range(c * NT // QUARTERS, (c + 1) * NT // QUARTERS)]

                            def combine(first, stop):
                                final = []
                                for j, g, w in SHARES[first:stop]:
                                    if n == 0 and g is G1 and j < NT - GROUP:
                                        final.append(j)
                                    dve.wait_ge(s_g[j * QUARTERS // NT], 32)
                                    ins = dve.scalar_tensor_tensor(X[:, j * D:(j + 1) * D], g[:, j, :], w[:, j:j + 1], X[:, j * D:(j + 1) * D],
                                                                   ALU.mult, ALU.add)
                                ins.then_inc(s_sum, 1)
                                dve.wait_ge(s_sum, first // COMBINED + 1)
                                for j in final:
                                    row_sums(dve, j)

                            def beside_late(g, c):
                                k = (g - LATE_GROUPS[0]) * NC + c - COMBINE_AFTER
                                if 0 <= k * COMBINED < len(SHARES):
                                    combine(k * COMBINED, (k + 1) * COMBINED)
                            shared(dve.Fori, chunk, end, LATE_GROUPS, beside_late)
                            if n == 0:
                                dve.wait_ge(s_xS, GROUPS)
                                for j in range(NT - GROUP, NT):
                                    row_sums(dve, j)

                        @block.scalar
                        def _(act):
                            deviations(act, s_var, s_std)
                            def copy_columns(g):
                                act.wait_ge(s_turn, g + 1)
                                act.activation(cols[:, g * SEG:(g + 1) * SEG], (ta_ps, tb_ps)[g % 2][:], ACT.Copy).then_inc(s_cols, 1)
                            copy_columns(0)

                            def beside(g, c):
                                if g == 0 and c + 1 < GROUPS:
                                    copy_columns(c + 1)
                                if g == 1 and c == 0:
                                    act.wait_ge(s_shift, 1)
                                    act.activation(probs, probs, ACT.Exp).then_inc(s_rexp, 1)

                            def chunk(g, c, follows):
                                k = g * NC + c
                                act.wait_ge(s_upS, k + 1)
                                wait(act, s_hS, k - 1)
                                act.activation(gates[chunk_rows(c), c % 2, :], up_ps[0:P if c < NC - 1 else ITAIL, 2 * (c % 2), :], ACT.Silu).then_inc(s_gS, 1)
                                if follows and c == 0:
                                    copy_out(g - 1)

                            def copy_out(g):
                                act.wait_ge(s_dS, g * NC + NC)
                                wait(act, s_tS, g)
                                act.activation(out_cols[:], y_ps[:], ACT.Copy).then_inc(s_yS, 1)

                            shared(act.Fori, chunk, copy_out, EARLY_GROUPS, beside)
                            act.wait_ge(s_route, 1)
                            act.activation(late_cols[:], cols[:, LATE_GROUPS[0] * SEG:GROUPS * SEG], ACT.Copy).then_inc(s_late, 1)

                            def next_columns(t, s):
                                act.wait_ge(s_tx, t + 1)
                                act.activation(xT[:, s, :], xt_ps[:, 0:P], ACT.Copy).then_inc(s_xT2, 1)

                            def body(t, s, i):
                                if exists(t):
                                    wait(act, s_hA, t)
                                    act.wait_ge(s_upA, t + 1)
                                    act.activation(gated[:, 0:IA], up_ps[:, 0, 0:IA], ACT.Silu).then_inc(s_gA, 1)
                                if exists(t - 1):
                                    act.wait_ge(s_tB, t)
                                    act.activation(hTB[:, 0:(CB - 1) * P], tb_ps[:, 0:(CB - 1) * P], ACT.Copy)
                                    act.activation(hTB[0:ITAIL, (CB - 1) * P:CB * P], tb_ps[0:ITAIL, (CB - 1) * P:CB * P], ACT.Copy).then_inc(s_cB, 1)
                                if exists(t):
                                    wait(act, s_hB, t)
                                    act.wait_ge(s_upB, t + 1)
                                    act.activation(gated[:, IA:I], up_ps[:, 2, 0:IB], ACT.Silu).then_inc(s_gB, 1)
                                    if exists(t + 1):
                                        next_columns(t + 1, 1 - s)
                                    act.wait_ge(s_tA, t + 1)
                                    act.activation(hTA[:, s, :], ta_ps[:], ACT.Copy).then_inc(s_cA, 1)
                            next_columns(0, 0)
                            run(act.Fori, body)
                            shared(act.Fori, chunk, copy_out, LATE_GROUPS)

                        @block.tensor
                        def _(pe):
                            pe.wait_ge(experts_in, EXPERTS_IN)
                            def turn(g):
                                wait(pe, s_cols, g - 1)
                                pe.wait_ge(s_ln, g + 1)
                                for i in range(GROUP):
                                    mm = pe.transpose((ta_ps, tb_ps)[g % 2][:, i * P:(i + 1) * P], rows[:, g * GROUP + i, 0, 0:D], ident[:])
                                mm.then_inc(s_turn, 1)

                            def logits(g):
                                pe.wait_ge(s_cols, g + 1)
                                for t in range(g * GROUP, (g + 1) * GROUP):
                                    mm = pe.matmul(xt_ps[:, t * E:(t + 1) * E], cols[:, t * P:(t + 1) * P], gateT[:], start=True, stop=True)
                                if g == GROUPS - 1:
                                    mm.then_inc(s_logit, 1)

                            def beside(g, c):
                                if g == 0:
                                    if c + 1 < GROUPS:
                                        turn(c + 1)
                                    logits(c)
                                elif c == COUNT_AFTER:
                                    pe.wait_ge(s_taken, 1)
                                    pe.matmul(xt_ps[:, 0:NT * E], before[:], taken.rearrange("p t e -> p (t e)"), start=True, stop=True)
                                    pe.matmul(xt_ps[:, NT * E:2 * NT * E], all_ones[:], taken.rearrange("p t e -> p (t e)"), start=True, stop=True).then_inc(s_count, 1)

                            def chunk(g, c, follows):
                                k = g * NC + c
                                tokens = late_cols[:, (g - LATE_GROUPS[0]) * SEG:(g - LATE_GROUPS[0] + 1) * SEG] if isinstance(g, int) and g in LATE_GROUPS else cols[:, ds(g * SEG, SEG)]
                                wait(pe, s_hS, k - 1)
                                if c < NC - 1:
                                    for bank, at in ((0, c * P), (1, (NC - 1 + c) * P)):
                                        mm = pe.matmul(up_ps[:, 2 * (c % 2) + bank, :], experts[:, GU_AT + at:GU_AT + at + P], tokens, start=True, stop=True)
                                else:
                                    mm = pe.matmul(up_ps[0:SHARED_TAIL + ITAIL, 2 * (c % 2), :], experts[:, DOWN_AT - SHARED_TAIL - ITAIL:DOWN_AT], tokens, start=True, stop=True)
                                mm.then_inc(s_upS, 1)
                                if c:
                                    down(g, c - 1)
                                elif follows:
                                    down(g - 1, NC - 1)
                                if follows and c == 1:
                                    turn_out(g - 1)

                            def down(g, c):
                                w = chunk_rows(c)
                                if c == 0:
                                    wait(pe, s_yS, g)
                                pe.wait_ge(s_hS, g * NC + (c + 1))
                                pe.matmul(y_ps[:], experts[w, DOWN_AT + c * D:DOWN_AT + (c + 1) * D], acts[c % 2][w], start=(c == 0), stop=(c == NC - 1), skip_group_check=True).then_inc(s_dS, 1)

                            def turn_out(g):
                                pe.wait_ge(s_yS, g + 1)
                                wait(pe, s_xS, g)
                                for i in range(GROUP):
                                    mm = pe.transpose(ta_ps[:, i * P:(i + 1) * P], out_cols[:, i * P:(i + 1) * P], ident[:])
                                mm.then_inc(s_tS, 1)

                            def end(g):
                                down(g, NC - 1)
                                turn_out(g)

                            turn(0)
                            pe.wait_ge(s_cols, 1)
                            shared(pe.Fori, chunk, end, EARLY_GROUPS, beside)

                            def columns(where, rows, at, width):
                                return experts[0:rows, where + at:where + at + width] if isinstance(where, int) else experts[0:rows, ds(where + at, width)]

                            def up(t, s, half, at, width, where):
                                for bank, off in ((2 * half, 0), (2 * half + 1, I)):
                                    mm = pe.matmul(up_ps[:, bank, 0:width], xT[:, s, :], columns(where, P, off + at, width), start=True, stop=True)
                                return mm

                            where = {}

                            tile_before = pe.alloc_register(f"f{n}_tile_before")

                            def find(m):
                                if not isinstance(m, int) or m > 0:
                                    where[-1] = nc.tensor.snap(tile_before, min_val=0, max_val=(E - 1) * EXPERT)
                                found_tiles = UNROLL if not isinstance(m, int) or m < SLOTS // UNROLL else SLOTS % UNROLL
                                _, found = nc.values_load_multi_w_load_instructions(weights_at[0:1, ds(m, 1), 0:found_tiles], engines=[mybir.EngineType.PE], min_val=0, max_val=(E - 1) * EXPERT)
                                where.update(enumerate(found))

                            def turn_in(t, s):
                                pe.wait_ge(s_xin[s], (t - s) * 8 + 16)
                                pe.transpose(xt_ps[:, 0:P], xin[:, s, 0:D], ident[:]).then_inc(s_tx, 1)

                            def body(t, s, i):
                                if exists(t):
                                    pe.wait_ge(s_xT2, t + 1)
                                    wait(pe, s_hA, t)
                                    up(t, s, 0, 0, IA, where[i]).then_inc(s_upA, 1)
                                if exists(t - 1):
                                    pe.wait_ge(s_hB, t)
                                    wait(pe, s_cB, t - 1)
                                    for c in range(CB):
                                        w = P if c < CB - 1 else ITAIL
                                        mm = pe.transpose(tb_ps[0:w, c * P:(c + 1) * P], inner_h[:, IA + c * P:IA + c * P + w], ident[:])
                                    mm.then_inc(s_tB, 1)
                                if exists(t):
                                    up(t, s, 1, IA, IB, where[i]).then_inc(s_upB, 1)
                                    if exists(t + 1):
                                        turn_in(t + 1, 1 - s)
                                    wait(pe, s_cA, t)
                                    pe.wait_ge(s_hA, t + 1)
                                    for c in range(CA):
                                        mm = pe.transpose(ta_ps[:, c * P:(c + 1) * P], inner_h[:, c * P:(c + 1) * P], ident[:])
                                    mm.then_inc(s_tA, 1)
                                if exists(t - 1):
                                    wait(pe, s_y, t - 1)
                                    pe.wait_ge(s_cB, t)
                                    pe.wait_ge(s_cA, t)
                                    for c in range(NC):
                                        w = P if c < NC - 1 else ITAIL
                                        lhs = hTA[0:w, 1 - s, c * P:(c + 1) * P] if c < CA else hTB[0:w, (c - CA) * P:(c - CA + 1) * P]
                                        rhs = columns(where[i - 1], w, GU + c * D, D)
                                        mm = pe.matmul(y_ps[:, 0:D], lhs, rhs, start=(c == 0), stop=(c == NC - 1))
                                    mm.then_inc(s_down, 1)
                                if i == UNROLL - 1 and exists(t):
                                    pe.reg_mov(tile_before, where[i])

                            pe.wait_ge(s_route, 1)
                            if n:
                                pe.wait_ge(lodgers_in, 16 * 3 * LODGERS)
                            turn_in(0, 0)
                            pe.wait_ge(s_xS, GROUPS - LATE)
                            run(pe.Fori, body, find)
                            pe.wait_ge(s_late, 1)
                            pe.wait_ge(s_y, SLOTS)
                            shared(pe.Fori, chunk, end, LATE_GROUPS)

                        @block.sync
                        def _(sp):
                            if n == 0:
                                for used in spent:
                                    sp.sem_clear(used)
                            if n:
                                for e in range(E - LODGERS, E):
                                    load_expert(sp, e, lodgers_in)
                            for k in range(IN_FLIGHT):
                                sp.wait_ge(s_sent[k], 2 * NT // IN_FLIGHT * 16)
                            def load(k, s):
                                wait(sp, s_back, k - 1)
                                wait(sp, s_tx, k - 1)
                                sp.dma_start(xin[:, s, :], routed[n][ds(k * P, P), :]).then_inc(s_xin[s], 16)
                            load(0, 0), load(1, 1)
                            with sp.Fori(1, SLOTS // 2) as m:
                                load(m * 2, 0), load(m * 2 + 1, 1)
                            load(SLOTS - 1, 0)
                            for q in range(2):
                                sp.wait_ge(s_home[q], (SLOTS + 1 - q) // 2 * 16)
                            for c in range(QUARTERS):
                                for q, g in enumerate((G0, G1)):
                                    j = slice(c * NT // QUARTERS, (c + 1) * NT // QUARTERS)
                                    sp.dma_start(g[:, j, :],
                                                 expert_out[n][q * B * T:(q + 1) * B * T, :].rearrange("(t p) d -> p t d", p=P)[:, j, :]).then_inc(s_g[c], 16)
                            if n == 1:
                                for c in range(QUARTERS):
                                    j = slice(c * NT // QUARTERS, (c + 1) * NT // QUARTERS)
                                    sp.wait_ge(s_sum, -(-2 * j.stop // COMBINED))
                                    if c == QUARTERS - 1:
                                        sp.wait_ge(s_xS, GROUPS)
                                    sp.dma_start(out.rearrange("(t p) d -> p t d", p=P)[:, j, :], X[:].rearrange("p (t d) -> p t d", d=D)[:, j, :]).then_inc(s_out, 16)
                                sp.wait_ge(s_out, 16 * QUARTERS)

                        @block.gpsimd
                        def _(pool):
                            for q in range(2):
                                pool.tensor_copy(rows[:, :, q, D:ROW].bitcast(I32), token_row[:, q * NT:(q + 1) * NT].unsqueeze(2))
                            for g in range(NT // GROUP):
                                pool.wait_ge(s_ln, g + 1)
                                of = slice(g * GROUP, (g + 1) * GROUP)
                                ins = pool.tensor_copy(rows[:, of, 1, 0:D], rows[:, of, 0, 0:D])
                            ins.then_inc(s_copied, 1)
                            pool.wait_ge(s_copied, 1)
                            pool.wait_ge(prefilled, 32)
                            pool.wait_ge(s_route, 1)
                            for k in range(2 * NT):
                                j, q = divmod(k, 2)
                                wait(pool, s_sent[k % IN_FLIGHT], k // IN_FLIGHT * 16)
                                pool.indirect_dma_start(routed[n], bass.IndirectOffsetOnAxis(ap=place_i[:, q, j:j + 1].bitcast(U32), axis=0),
                                                        rows[:, j, q, :], None).then_inc(s_sent[k % IN_FLIGHT], 16)

                            result, stored = (pool.alloc_register(f"f{n}_{x}") for x in ("result", "stored"))
                            pool.reg_mov(result, 0)

                            def home(k, s):
                                pool.reg_add(result, result, 1)
                                if not isinstance(k, int):
                                    pool.reg_mov(stored, (k + s) * 8)
                                pool.wait_ge(s_route, 1)
                                pool.wait_ge(s_y, result)
                                wait(pool, s_home[1 - s], (k + s) * 8 if isinstance(k, int) else stored)
                                pool.indirect_dma_start(expert_out[n], bass.IndirectOffsetOnAxis(ap=back_to[:, s:s + 1].bitcast(U32), axis=0),
                                                        yout[:, s, :], None).then_inc(s_home[s], 16)
                            home(0, 0), home(1, 1)
                            with pool.Fori(1, SLOTS // 2) as m:
                                home(m * 2, 0), home(m * 2 + 1, 1)
                            home(SLOTS - 1, 0)


        def mamba():
            scope = ExitStack()
            with scope:
                def tb(name, shape, dt=F32):
                    return sb("m_" + name, shape, dt, scope)

                def ts(name):
                    return sem("m_" + name, scope)

                C = T // SEG
                HIST = TAPS - 1
                RING, DECAYS, B_RING, C_RING, SEEN = 4, 8, 4, 2, 4
                taps = tb("taps", [P, NL * HALF * TAPS])
                in_wT = tb("in_wT", [P, NL * DI])
                gateT_w = tb("gateT_w", [P, NL * DI])
                conv_b = tb("conv_b", [P, NL * HALF])
                x_w = tb("x_w", [P, NL * HALF, XR])
                dt_w = tb("dt_w", [XR, NL * DI])
                dt_b = tb("dt_b", [P, NL * HALF])
                decay = tb("decay", [P, NL * HALF * NS])
                skip = tb("skip", [P, NL * HALF])
                skip_diag = tb("skip_diag", [P, NL * HALF, P])
                out_w = tb("out_w", [P, NL * HALF, D])
                spread = tb("spread", [3 * 32, 2 * NS * P], BF16)
                zu = tb("zu", [P, STREAMS, 2 * HALF, SEG])
                parts = tb("parts", [3 * 32, STREAMS, SEG], BF16)
                delta = tb("delta", [P, STREAMS, HALF, SEG])
                delta_u = tb("delta_u", [P, STREAMS, HALF, SEG])
                first = tb("first", [P, STREAMS, HALF, NS])
                last = tb("last", [P, NL, STREAMS, C, HALF, NS])
                state = tb("state", [P, RING, HALF, SEG])
                z = lambda s: zu[:, 1 - s, 0:HALF, :]
                u = lambda s: zu[:, s, HALF:2 * HALF, :]
                spare = experts[:, (E - LODGERS) * EXPERT:E * EXPERT]
                def lodge(at, columns, rows=P):
                    return spare[0:rows, at:at + columns]
                at = 0
                xT = lodge(at, B * T)
                at += B * T
                hT = lodge(at, STREAMS * T).rearrange("p (s t) -> p s t", s=STREAMS)
                at += STREAMS * T
                c_sb = lodge(at, C_RING * SEG).rearrange("p (r t) -> p r t", r=C_RING)
                at += C_RING * SEG
                bc = lodge(at, SEG, XR)
                at += SEG
                rest = lodge(at, SEG, 32)
                at += SEG
                mid = lodge(at, SEG // 2, 32).bitcast(BF16)
                at += SEG // 2
                seen = lodge(at, SEEN * HALF * SEG).rearrange("p (r h t) -> p r h t", r=SEEN, h=HALF)
                at += SEEN * HALF * SEG
                dA = lodge(at, DECAYS * HALF * SEG).rearrange("p (r h t) -> p r h t", r=DECAYS, h=HALF)
                at += DECAYS * HALF * SEG
                drive = lodge(at, 2 * HALF * SEG).rearrange("p (r h t) -> p r h t", r=2, h=HALF)
                raw = tb("raw", [P, HALF, HIST + SEG])
                history = tb("history", [P, NL, STREAMS, C, HALF, HIST])
                shares = tb("shares", [P, HIST, SEG])
                xn = delta_u[:, 1]

                ps = scope.enter_context(nc.psum_tensor("m_ps", [P, 8, SEG], F32))
                Y = ps[:, 0:2, :]
                PB = ps[:, 2:2 + B_RING, :]
                PC = ps[:, 2 + B_RING, :]
                SIDE = ps[:, 7, :]

                s_w_first, s_w, s_set, s_zero = ts("w_first"), ts("w"), ts("set"), ts("zeroed")
                s_stats, s_var, s_std, s_rstd = ts("stats"), ts("var"), ts("std"), ts("rstd")
                s_exp_A, s_neg_A = ts("exp_A"), ts("neg_A")
                s_ln, s_turn, s_xT, s_added = ts("ln"), ts("turn"), ts("xT"), ts("added")
                s_raw, s_share, s_conv = ts("raw"), ts("share"), [ts(f"conv{h}") for h in range(HALF)]
                s_side, s_side_read, s_silu, s_first = ts("side"), ts("side_read"), ts("silu"), ts("first")
                s_soft, s_dt, s_dtu, s_split, s_parts = ts("soft"), ts("dt"), ts("dtu"), ts("split"), ts("parts")
                s_b, s_c, s_acc = ts("b"), ts("c"), ts("acc")
                s_drive, s_decay, s_c_sb, s_state, s_seen, s_y = ts("drive"), ts("decay"), ts("c_sb"), ts("state"), ts("seen"), ts("y")

                first_weights = [(in_wT[:], "m_inT"), (taps[:], "m_taps"), (conv_b[:], "m_conv_b"), (skip[:], "m_skip"), (decay[:], "m_A_log")]
                weights = [(gateT_w[:], "m_gateT"),
                           (x_w[:].rearrange("p a r -> p (a r)"), "m_xT"), (dt_w[2 * NS:XR, :], "m_dtT"), (dt_b[:], "m_dt_b"),
                           (out_w[:].rearrange("p a d -> p (a d)"), "m_outT"), (spread[:], "m_spread")]
                FIRST_WEIGHTS, WEIGHTS = 16 * len(first_weights), 16 * len(weights)

                CHUNKS = B * C

                def chunk_of(j):
                    b, c = divmod(j, C)
                    return b % STREAMS, c, b // STREAMS * C + c

                UNITS = [(l, s) for l in range(NL) for s in range(STREAMS)]
                CONV, ROWS, DT = 0, 2, 3
                HEAD = 4
                B_AHEAD = 3
                PROJECT_AT, CONVOLVE_AT = [4, 5], [6, 5]
                SILU_AT, ROWS_AT, DT_AT, SOFT_AT = 7, 8, 9, 11
                DECAYED = [[1], [2], [3], [4, 5], [6], [7], [], [8, 9], [], [10], [11, 12], [], [13, 14], [], [15], []]
                ADDED = [[14], [15], [], [0], [1], [2], [3], [4], [5], [6], [7], [8, 9], [10], [11], [12], [13]]

                def side(unit, k):
                    return k if isinstance(unit, int) and unit == 0 else unit * 8 + (k - 1)

                def side_gate(unit, h):
                    return 5 + h if isinstance(unit, int) and unit == 0 else unit * 8 + (4 + h)

                def side_out(unit):
                    return unit * 8 + 14

                def ending(i, unit):
                    return unit - 1, *UNITS[i - 1]

                def run(fori, prepare, step, beside=lambda j: None):
                    for n in range(NS):
                        if 1 <= n < CHUNKS:
                            beside(n)
                        prepare(n, *UNITS[0], 0, 0, 0)
                    for n in range(HEAD):
                        step(n, 0, 0, 0, 0, None)
                    with fori(0, B // STREAMS) as p:
                        with fori(0, C) as c:
                            turn = p * C + c
                            where = lambda bs, m: p * (STREAMS * TPB * m) + c * (SEG // P * m) + bs * TPB * m
                            for i in range(len(UNITS) + 1):
                                for n in range(HEAD if i == 0 else 0, NS if i < len(UNITS) else HEAD):
                                    unit = turn * len(UNITS) + i
                                    step(n, i % len(UNITS), unit, *((turn, c) if i < len(UNITS) else (turn + 1, c * -1 + 1)), where)
                                    if i < len(UNITS) - 1:
                                        prepare(n, *UNITS[i + 1], unit + 1, turn, c)
                                    elif i == len(UNITS) - 1:
                                        prepare(n, *UNITS[0], unit + 1, turn + 1, c * -1 + 1)

                with nc.Block() as block:
                    @block.sync
                    def _(sp):
                        for dst, name in first_weights:
                            sp.dma_start(dst, a[name]).then_inc(s_w_first, 16)
                        for dst, name in weights:
                            sp.dma_start(dst, a[name]).then_inc(s_w, 16)

                    @block.tensor
                    def _(pe):
                        pe.sem_inc(s_acc, SEEN)
                        pe.sem_inc(s_turn, 2)

                        def turn(j):
                            pe.wait_ge(s_xT, j + 1)
                            pe.wait_ge(s_ln, j + 1)
                            for i in range(SEG // P):
                                mm = pe.transpose(ps[:, 4 + j % 2, i * P:(i + 1) * P], xn[:, j % 2, i * P:(i + 1) * P], ident[:])
                            mm.then_inc(s_turn, 1)
                        turn(0)
                        def beside(j):
                            turn(j)
                            if j == 1:
                                pe.wait_ge(s_zero, 1)
                                pe.wait_ge(s_w, WEIGHTS)
                                pe.wait_ge(s_w_first, FIRST_WEIGHTS)
                                pe.wait_ge(s_set, NL * HALF)
                            if j == CHUNKS - 1:
                                pe.wait_ge(s_xT, CHUNKS + 2)

                        def layer_in(l, s, turn, c):
                            return xT[:, ds(turn * SEG + s * B * SEG, SEG)] if l == 0 else hT[:, s, ds(c * SEG, SEG)]

                        def prepare(n, l, s, unit, turn, c):
                            for h in range(HALF):
                                if n == PROJECT_AT[h]:
                                    wait(pe, s_side_read, side(unit, CONV + h))
                                    pe.matmul(SIDE, in_wT[:, l * DI + h * P:l * DI + (h + 1) * P], layer_in(l, s, turn, c), start=True, stop=True).then_inc(s_side, 1)
                            if n == ROWS_AT:
                                pe.wait_ge(s_silu, unit + 1)
                                for h in range(HALF):
                                    mm = pe.matmul(SIDE[0:XR], x_w[:, l * HALF + h, :], u(s)[:, h, :], start=(h == 0), stop=(h == HALF - 1))
                                mm.then_inc(s_side, 1)
                            if n in (DT_AT, DT_AT + 1):
                                h = n - DT_AT
                                pe.wait_ge(s_side_read, side(unit, DT + h))
                                pe.matmul(SIDE, dt_w[2 * NS:XR, l * DI + h * P:l * DI + (h + 1) * P], bc[2 * NS:XR, :], start=True, stop=True).then_inc(s_side, 1)

                        def accumulate(g, n):
                            pe.wait_ge(s_seen, g + (RING + 1))
                            for h in range(HALF):
                                mm = pe.matmul(Y[:, h, :], ident[:], seen[:, n % SEEN, h, :], start=False, stop=(n == NS - 1), skip_group_check=True)
                            mm.then_inc(s_acc, 1)

                        def step(n, i, unit, turn, c, where):
                            l, s = UNITS[i]
                            g = unit * NS + n
                            def row_b(n):
                                pe.wait_ge(s_drive, unit * (NS * 2) + (n * 2 + 2))
                                pe.matmul(PB[:, n % B_RING, :], spread[:, n * P:(n + 1) * P], parts[:, s, :], start=True, stop=True).then_inc(s_b, 1)
                            if n == 0:
                                pe.wait_ge(s_parts, unit + 1)
                                for m in range(B_AHEAD):
                                    row_b(m)
                            if n < NS - B_AHEAD:
                                row_b(n + B_AHEAD)
                            pe.wait_ge(s_c_sb, g + 1)
                            pe.matmul(PC, spread[:, (n + NS) * P:(n + NS + 1) * P], parts[:, s, :], start=True, stop=True).then_inc(s_c, 1)
                            if n == 2:
                                if where:
                                    pe.wait_ge(s_y, unit)
                                for h in range(HALF):
                                    pe.matmul(Y[:, h, :], skip_diag[:, l * HALF + h, :], u(s)[:, h, :], start=True, stop=False, skip_group_check=True)
                            for m in ADDED[n]:
                                if n >= 2:
                                    accumulate(unit * NS + m, m)
                                elif where:
                                    accumulate(unit * NS + (m - NS), m)
                            if n < HALF:
                                pe.wait_ge(s_side_read, side_gate(unit, n))
                                pe.matmul(SIDE, gateT_w[:, l * DI + n * P:l * DI + (n + 1) * P], layer_in(l, s, turn, c), start=True, stop=True).then_inc(s_side, 1)
                            if n == HEAD - 1 and where:
                                before_, bl, bs = ending(i, unit)
                                pe.wait_ge(s_y, unit)
                                pe.wait_ge(s_side_read, side_out(before_))
                                if bl < NL - 1:
                                    for h in range(HALF):
                                        mm = pe.matmul(SIDE, out_w[:, bl * HALF + h, :], z(bs)[:, h, :], start=(h == 0), stop=(h == HALF - 1))
                                else:
                                    for t in range(SEG // P):
                                        for h in range(HALF):
                                            mm = pe.matmul(SIDE[:, t * P:(t + 1) * P], z(bs)[:, h, t * P:(t + 1) * P], out_w[:, bl * HALF + h, :], start=(h == 0), stop=(h == HALF - 1))
                                mm.then_inc(s_side, 1)
                        run(pe.Fori, prepare, step, beside)

                    @block.scalar
                    def _(act):
                        act.sem_inc(s_c_sb, 1)
                        act.sem_inc(s_xT, 2)
                        deviations(act, s_var, s_std)
                        act.wait_ge(s_zero, 1)

                        def columns(j):
                            s, c, q = chunk_of(j)
                            at = (s * B + q) * SEG
                            act.wait_ge(s_turn, j + 3)
                            act.activation(xT[:, at:at + SEG], ps[:, 4 + j % 2, :], ACT.Copy).then_inc(s_xT, 1)
                        columns(0)
                        act.wait_ge(s_w_first, FIRST_WEIGHTS)
                        act.activation(decay[:], decay[:], ACT.Exp).then_inc(s_exp_A, 1)
                        act.wait_ge(s_w, WEIGHTS)
                        act.wait_ge(s_neg_A, 1)

                        def prepare(n, l, s, unit, turn, c):
                            if n == 5:
                                act.activation(first[:, s], last[:, l, s, ds(c, 1)].rearrange("p c h n -> p (c h) n"), ACT.Copy).then_inc(s_first, 1)
                            if n == PROJECT_AT[0]:
                                act.activation(raw[:, :, 0:HIST], history[:, l, s, ds(c, 1)].rearrange("p c h k -> p (c h) k"), ACT.Copy)
                            for h in range(HALF):
                                if n == PROJECT_AT[h]:
                                    lh = l * HALF + h
                                    act.wait_ge(s_side, side(unit, CONV + h) + 1)
                                    act.activation(raw[:, h, HIST:], SIDE, ACT.Copy).then_inc(s_raw, 1)
                                    act.activation(u(s)[:, h, :], SIDE, ACT.Identity, scale=taps[:, (lh + 1) * TAPS - 1:(lh + 1) * TAPS], bias=conv_b[:, lh:lh + 1]).then_inc(s_side_read, 1)
                            if n == PROJECT_AT[1]:
                                act.wait_ge(s_raw, unit * HALF + HALF)
                                act.activation(history[:, l, s, C - 1], raw[:, :, SEG:SEG + HIST], ACT.Copy)
                                for k in range(HIST):
                                    tap = (l * HALF + 1) * TAPS + k
                                    act.activation(shares[:, k, :], raw[:, 1, k:k + SEG], ACT.Identity, scale=taps[:, tap:tap + 1]).then_inc(s_share, 1)
                            if n == SILU_AT:
                                for h in range(HALF):
                                    act.wait_ge(s_conv[h], unit * HIST + HIST)
                                both = u(s) if isinstance(unit, int) else zu[:, s]
                                act.activation(both, both, ACT.Silu).then_inc(s_silu, 1)
                                act.preload_act_table_set("natural_log_exp_and_others")
                            if n == ROWS_AT:
                                act.wait_ge(s_side, side(unit, ROWS) + 1)
                                wait(act, s_parts, unit)
                                act.activation(parts[0:32, s, :], SIDE[0:32], ACT.Copy)
                                act.activation(bc, SIDE[0:XR], ACT.Copy).then_inc(s_side_read, 1)
                            if n in (DT_AT, DT_AT + 1):
                                h = n - DT_AT
                                act.wait_ge(s_side, side(unit, DT + h) + 1)
                                act.activation(delta[:, s, h, :], SIDE, ACT.Identity, bias=dt_b[:, l * HALF + h:l * HALF + h + 1]).then_inc(s_side_read, 1)
                            if n == SOFT_AT:
                                act.wait_ge(s_side_read, side(unit, DT + 1) + 1)
                                act.activation(delta_u[:, s], delta[:, s], ACT.Abs).then_inc(s_soft, 1)
                            if n == SOFT_AT + 1:
                                act.wait_ge(s_soft, unit * 3 + 1)
                                act.activation(delta_u[:, s], delta_u[:, s], ACT.Exp, scale=-1.0).then_inc(s_soft, 1)
                            if n == SOFT_AT + 2:
                                act.wait_ge(s_soft, unit * 3 + 2)
                                act.activation(delta_u[:, s], delta_u[:, s], ACT.Ln, bias=1.0).then_inc(s_soft, 1)

                        def step(n, i, unit, turn, c, where):
                            l, s = UNITS[i]
                            g = unit * NS + n
                            def decays(n):
                                act.wait_ge(s_state, unit * (NS * 2) + (n * 2 + 2))
                                for h in range(HALF):
                                    lhn = (l * HALF + h) * NS + n
                                    act.activation(dA[:, n % DECAYS, h, :], delta[:, s, h, :], ACT.Exp, scale=decay[:, lhn:lhn + 1]).then_inc(s_decay, 1)
                            if n == 0:
                                act.wait_ge(s_dt, unit + 1)
                                decays(0)
                            if n in (1, 2):
                                act.wait_ge(s_side, side_gate(unit, n - 1) + 1)
                                act.activation(z(s)[:, n - 1, :], SIDE, ACT.Copy).then_inc(s_side_read, 1)
                            for m in DECAYED[n]:
                                decays(m)
                            act.wait_ge(s_c, g + 1)
                            act.wait_ge(s_seen, g + (RING - C_RING + 1))
                            act.activation(c_sb[:, n % C_RING, :], PC, ACT.Copy).then_inc(s_c_sb, 1)
                            if n == HEAD - 1 and where:
                                before_, bl, bs = ending(i, unit)
                                if bl < NL - 1:
                                    act.wait_ge(s_side, side_out(before_) + 1)
                                    act.activation(hT[:, bs, ds(c * SEG, SEG)], SIDE, ACT.Copy).then_inc(s_side_read, 1)
                        run(act.Fori, prepare, step, columns)

                    @block.gpsimd
                    def _(pool):
                        pool.sem_inc(s_seen, RING)
                        pool.sem_inc(s_added, 2)
                        for j in range(CHUNKS):
                            pool.wait_ge(s_ln, j + 1)
                            pool.tensor_tensor(X[:, j * SEG:(j + 1) * SEG], X[:, j * SEG:(j + 1) * SEG], xn[:, j % 2, :], ALU.add).then_inc(s_added, 1)

                        def step(n, i, unit, turn, c, where):
                            l, s = UNITS[i]
                            g = unit * NS + n
                            pool.wait_ge(s_state, g * 2 + (DECAYS + 1) * HALF)
                            pool.wait_ge(s_c_sb, g + 2)
                            pool.wait_ge(s_acc, g + 1)
                            pool.tensor_tensor(seen[:, n % SEEN], state[:, n % RING], c_sb[:, n % C_RING, :].unsqueeze(1).to_broadcast([P, HALF, SEG]), ALU.mult)
                            pool.tensor_copy(last[:, l, s, C - 1, :, n:n + 1], state[:, n % RING, :, SEG - 1:SEG]).then_inc(s_seen, 1)
                        def prepare(n, l, s, unit, turn, c):
                            if n == CONVOLVE_AT[1]:
                                for k in range(HIST):
                                    pool.wait_ge(s_share, unit * HIST + (k + 1))
                                    if k:
                                        pool.wait_ge(s_conv[1], unit * HIST + k)
                                    pool.tensor_tensor(u(s)[:, 1, :], u(s)[:, 1, :], shares[:, k, :], ALU.add).then_inc(s_conv[1], 1)
                        run(pool.Fori, prepare, step)

                    @block.vector
                    def _(dve):
                        dve.sem_inc(s_drive, B_RING * HALF)
                        dve.sem_inc(s_state, DECAYS * HALF)
                        variances(dve, s_stats, s_var)
                        dve.memset(history[:], 0.0)
                        dve.memset(last[:], 0.0).then_inc(s_zero, 1)
                        inverses(dve, s_std, s_rstd)

                        def beside(j):
                            dve.wait_ge(s_turn, j + 1)
                            dve.wait_ge(s_added, j + 1)
                            for i in range(SEG // P):
                                ins = layernorm(dve, xn[:, j % 2, i * P:(i + 1) * P], j * (SEG // P) + i)
                            ins.then_inc(s_ln, 1)
                            if j == CHUNKS - 1:
                                dve.wait_ge(s_added, CHUNKS + 2)
                                dve.wait_ge(s_xT, CHUNKS + 2)
                                dve.wait_ge(s_w, WEIGHTS)
                        beside(0)
                        dve.wait_ge(s_w_first, FIRST_WEIGHTS)
                        for lh in range(NL * HALF):
                            dve.tensor_scalar(skip_diag[:, lh, :], ident[:], skip[:, lh:lh + 1], None, ALU.mult).then_inc(s_set, 1)
                        dve.wait_ge(s_exp_A, 1)
                        dve.tensor_scalar(decay[:], decay[:], -1.0, None, ALU.mult).then_inc(s_neg_A, 1)

                        def prepare(n, l, s, unit, turn, c):
                            if n == CONVOLVE_AT[0]:
                                dve.wait_ge(s_side_read, side(unit, CONV) + 1)
                                for k in range(HIST):
                                    tap = l * HALF * TAPS + k
                                    if k:
                                        dve.wait_ge(s_conv[0], unit * HIST + k)
                                    dve.scalar_tensor_tensor(u(s)[:, 0, :], raw[:, 0, k:k + SEG], taps[:, tap:tap + 1], u(s)[:, 0, :], ALU.mult, ALU.add).then_inc(s_conv[0], 1)
                            if n == DT_AT + 2:
                                dve.wait_ge(s_side_read, side(unit, ROWS) + 1)
                                dve.tensor_tensor(rest, bc[0:32, :], parts[0:32, s, :], ALU.subtract).then_inc(s_split, 1)
                                dve.wait_ge(s_split, unit * 2 + 1)
                                dve.tensor_copy(mid, rest).then_inc(s_split, 1)
                                dve.wait_ge(s_split, unit * 2 + 2)
                                dve.tensor_copy(parts[32:64, s, :], mid)
                                dve.tensor_tensor(parts[64:96, s, :], rest, mid, ALU.subtract).then_inc(s_parts, 1)
                            if n == SOFT_AT + 3:
                                dve.wait_ge(s_soft, unit * 3 + 3)
                                dve.scalar_tensor_tensor(delta[:, s], delta[:, s], 0.0, delta_u[:, s], ALU.max, ALU.add).then_inc(s_dt, 1)
                                dve.wait_ge(s_dt, unit + 1)
                                dve.tensor_tensor(delta_u[:, s], delta[:, s], u(s), ALU.mult).then_inc(s_dtu, 1)

                        def step(n, i, unit, turn, c, where):
                            l, s = UNITS[i]
                            g = unit * NS + n
                            if n == 2 and where:
                                before_, bl, bs = ending(i, unit)
                                dve.wait_ge(s_acc, unit * NS + SEEN)
                                dve.wait_ge(s_silu, unit + 1)
                                dve.tensor_tensor(z(bs), z(bs), Y, ALU.mult).then_inc(s_y, 1)
                            if n == 0:
                                dve.wait_ge(s_first, unit + 1)
                                dve.wait_ge(s_dtu, unit + 1)
                            dve.wait_ge(s_b, g + 1)
                            for h in range(HALF):
                                dve.wait_ge(s_state, g * 2 + (h + (DECAYS - 2) * HALF + 1))
                                dve.tensor_tensor(drive[:, n % 2, h, :], delta_u[:, s, h, :], PB[:, n % B_RING, :], ALU.mult).then_inc(s_drive, 1)
                            dve.wait_ge(s_seen, g + 1)
                            for h in range(HALF):
                                dve.wait_ge(s_drive, g * 2 + (h + B_RING * HALF + 1))
                                dve.wait_ge(s_decay, g * 2 + (h + 1))
                                dve.tensor_tensor_scan(state[:, n % RING, h, :], dA[:, n % DECAYS, h, :], drive[:, n % 2, h, :], first[:, s, h, n:n + 1], ALU.mult, ALU.add).then_inc(s_state, 1)
                            if n == HEAD - 1 and where:
                                before_, bl, bs = ending(i, unit)
                                if bl == NL - 1:
                                    dve.wait_ge(s_side, side_out(before_) + 1)
                                    dve.tensor_tensor(X[:, ds(where(bs, P), SEG)], X[:, ds(where(bs, P), SEG)], SIDE, ALU.add).then_inc(s_side_read, 1)
                                    dve.wait_ge(s_side_read, side_out(before_) + 1)
                                    for t in range(SEG // P):
                                        row_sums(dve, where(bs, 1) + t)
                        run(dve.Fori, prepare, step, beside)

        attention()
        summed[0] += NT
        ffn(0)
        summed[0] += NT
        mamba()
        summed[0] += NT
        ffn(1)


def lay_out(v):
    f = lambda n: np.asarray(v[n], np.float32)
    c = np.ascontiguousarray
    o = {}
    o["x"] = c(f("L0_attn_a_x").reshape(B * T, D))
    o["wqkvT"] = c(f("L0_attn_a_Wqkv").T)
    o["bqkv"] = c(f("L0_attn_a_bqkv").reshape(3, D).T)
    o["woT"] = c(f("L0_attn_a_Wo").T)
    o["bo"] = c(f("L0_attn_a_bo").reshape(1, D))
    gu = f("L0_ffn_experts_gate_up").transpose(2, 0, 1).reshape(D, E * GU)
    gate, up = np.split(f("L0_ffn_shared_gate_up").T, 2, 1)
    full, space = (NC - 1) * P, np.zeros((D, SHARED_TAIL - ITAIL), np.float32)
    o["gate_up"] = np.concatenate([gu, gate[:, :full], up[:, :full], gate[:, full:], space, up[:, full:]], 1)
    dn = np.concatenate([f("L0_ffn_experts_down"), f("L0_ffn_shared_down")[None]]).transpose(0, 2, 1)
    o["down"] = c(dn[:, :(NC - 1) * P].reshape(E + 1, NC - 1, P, D).transpose(2, 0, 1, 3).reshape(P, -1))
    o["down_tail"] = c(dn[:, (NC - 1) * P:].transpose(1, 0, 2).reshape(ITAIL, -1))
    o["gateT"] = c(f("L0_ffn_gate_weight").T)
    chan = lambda x: c(x.reshape(NL, HALF, P, -1).transpose(2, 0, 1, 3).reshape(P, -1))
    w_in = f("L0_attn_b_W_in")
    o["m_inT"] = c(w_in[:, :DI].transpose(2, 0, 1).reshape(D, NL * DI))
    o["m_gateT"] = c(w_in[:, DI:].transpose(2, 0, 1).reshape(D, NL * DI))
    o["m_taps"], o["m_conv_b"] = chan(f("L0_attn_b_conv_w")), chan(f("L0_attn_b_conv_b"))
    w_x = f("L0_attn_b_W_x")
    o["m_xT"] = chan(np.concatenate([w_x[:, RANK:], w_x[:, :RANK]], 1).transpose(0, 2, 1))
    o["m_dtT"] = c(f("L0_attn_b_W_dt").transpose(2, 0, 1).reshape(RANK, NL * DI))
    o["m_dt_b"], o["m_A_log"], o["m_skip"] = chan(f("L0_attn_b_b_dt")), chan(f("L0_attn_b_A_log")), chan(f("L0_attn_b_D"))
    o["m_outT"] = chan(f("L0_attn_b_W_out").transpose(0, 2, 1))
    o["m_spread"] = np.repeat(np.tile(np.eye(2 * NS), (3, 1)), P, 1).astype(mybir.dt.np(BF16))
    p = np.arange(P)
    o["ident"] = np.eye(P, dtype=np.float32)
    o["ones_row"] = np.ones((1, P), np.float32)
    o["ones_tile"] = np.ones((P, NT), np.float32)
    o["all_ones"] = np.ones((P, P), np.float32)
    o["before"] = (p[:, None] < p).astype(np.float32)
    o["ahead"] = np.tile(np.arange(E, 0, -1, dtype=np.float32), (P, 1))
    o["tile_number"] = np.tile(np.arange(SLOTS, dtype=np.float32), (P, 1))
    o["tile_start"] = o["tile_number"] * P
    o["token_row"] = c(np.arange(2 * B * T, dtype=np.int32).reshape(2 * NT, P).T)
    o["nobody"] = np.zeros((P, ROW), np.int32)
    o["nobody"][:, D] = 2 * B * T + p
    o["own_head"] = c((p[:, None] % 32 // HD == np.arange(HG)).astype(np.float32))
    q, k = (p % 32)[:, None], np.arange(KW)
    seen = (k > q) & (k <= q + 32)
    first = seen & ((p[:, None] >= 32) | (k >= 32))
    o["mask"] = c(np.where(np.stack([seen, first], 1), 0, MASKED).astype(np.float32).reshape(P, -1))
    return o


def kernel(**inputs):
    import concourse.bacc as bacc
    from concourse.bass_utils import run_bass_kernel_spmd

    nc = bacc.Bacc("TRN2", target_bir_lowering=False, num_devices=1)
    arrays = lay_out(inputs)
    aps = {n: nc.dram_tensor("in_" + n, v.shape, mybir.dt.from_np(v.dtype), kind="ExternalInput").ap() for n, v in arrays.items()}
    out = nc.dram_tensor("out", (B * T, D), F32, kind="ExternalOutput").ap()
    hybrid_block_kernel(nc, aps, out)
    r = run_bass_kernel_spmd(nc, [{"in_" + n: v for n, v in arrays.items()}], core_ids=[0])
    return r.results[0]["out"].reshape(B, T, D)
```
